# Optimizing a Trainium2 kernel written in Bass

```python
import numpy as np
import jax
import jax.numpy as jnp

def _softmax(x, axis=-1):
    return jax.nn.softmax(x, axis=axis)

def _gelu(x):
    return jax.nn.gelu(x, approximate=True)

def _silu(x):
    return jax.nn.silu(x)

def _sigmoid(x):
    return jax.nn.sigmoid(x)

def _layernorm(x, axis=-1, eps=1e-05):
    m = jnp.mean(x, axis=axis, keepdims=True)
    v = jnp.var(x, axis=axis, keepdims=True)
    return (x - m) / jnp.sqrt(v + eps)

def _scatter_add(tgt, idx, src, axis=0):
    return tgt.at[idx].add(src)

def _segment_sum(src, seg, n):
    return jax.ops.segment_sum(src, seg, n)
kernel_name = 'mk_macaron_d2_jaxref_r8_c8ab09'

def setup_inputs(seed: int=0):
    np.random.seed(seed)
    _w = jnp.asarray

    def _L0_attn_setup():
        import jax, jax.numpy as jnp
        import numpy as np
        D_MODEL = 128
        N_HEADS = 32
        HEAD_DIM = D_MODEL // N_HEADS
        EPS = 1e-05
        key = jax.random.key(seed)
        ks = jax.random.split(key, 6)
        B, S = (2, 256)
        scale = 1.0 / np.sqrt(D_MODEL)
        return {'x': jax.random.normal(ks[0], (B, S, D_MODEL), dtype=jnp.float32), 'Wqkv_w': jax.random.normal(ks[1], (3 * D_MODEL, D_MODEL), dtype=jnp.float32) * scale, 'Wqkv_b': jax.random.normal(ks[2], (3 * D_MODEL,), dtype=jnp.float32) * 0.01, 'gn_w': jnp.ones((D_MODEL,), dtype=jnp.float32), 'gn_b': jnp.zeros((D_MODEL,), dtype=jnp.float32), 'out_w': jax.random.normal(ks[3], (D_MODEL, D_MODEL), dtype=jnp.float32) * scale, 'out_b': jax.random.normal(ks[4], (D_MODEL,), dtype=jnp.float32) * 0.01}
    _L0_attn_in = _L0_attn_setup()

    def _L0_ffn_setup():
        import jax, jax.numpy as jnp
        import numpy as np
        E = 8
        TOP_K = 2
        ROUTE_SCALE = 1.0
        ALPHA = 1.702
        LIMIT = 7.0
        D = 128
        F = 128
        B, S = (2, 128)

        def swiglu(h):
            g = jnp.minimum(h[..., ::2], LIMIT)
            l = jnp.clip(h[..., 1::2], -LIMIT, LIMIT)
            return g * jax.nn.sigmoid(ALPHA * g) * (l + 1.0)
        if __name__ == '__main__':
            out = reference(**setup_inputs())
            print(out.shape, out.dtype)
        key = jax.random.key(seed)
        ks = jax.random.split(key, 16)
        sd = 1.0 / np.sqrt(D)
        sf = 1.0 / np.sqrt(F)
        return {'x': jax.random.normal(ks[0], (B, S, D), jnp.float32), 'gate_w': jax.random.normal(ks[1], (E, D), jnp.float32) * sd, 'gate_b': jax.random.normal(ks[2], (E,), jnp.float32) * 0.01, 'w1': jax.random.normal(ks[3], (E, 2 * F, D), jnp.float32) * sd, 'b1': jax.random.normal(ks[4], (E, 2 * F), jnp.float32) * 0.01, 'w3': jax.random.normal(ks[5], (E, 2 * F, D), jnp.float32) * sd, 'b3': jax.random.normal(ks[6], (E, 2 * F), jnp.float32) * 0.01, 'w2': jax.random.normal(ks[7], (E, D, F), jnp.float32) * sf, 'b2': jax.random.normal(ks[8], (E, D), jnp.float32) * 0.01, 'sw1': jax.random.normal(ks[9], (2 * F, D), jnp.float32) * sd, 'sb1': jax.random.normal(ks[10], (2 * F,), jnp.float32) * 0.01, 'sw3': jax.random.normal(ks[11], (2 * F, D), jnp.float32) * sd, 'sb3': jax.random.normal(ks[12], (2 * F,), jnp.float32) * 0.01, 'sw2': jax.random.normal(ks[13], (D, F), jnp.float32) * sf, 'sb2': jax.random.normal(ks[14], (D,), jnp.float32) * 0.01}
    _L0_ffn_in = _L0_ffn_setup()

    def _L1_attn_setup():
        import jax, jax.numpy as jnp
        import numpy as np
        import math
        B, L, HID, NH = (4, 512, 128, 8)
        DH = HID // NH
        THETA = 10000.0

        def _rope_tables(seq_len, dh):
            half = dh // 2
            inv_freq = 1.0 / THETA ** (jnp.arange(half, dtype=jnp.float32) / half)
            freqs = jnp.arange(seq_len, dtype=jnp.float32)[:, None] * inv_freq[None, :]
            return (jnp.cos(freqs), jnp.sin(freqs))

        def _apply_rope(x, cos, sin):
            half = x.shape[-1] // 2
            x1, x2 = (x[..., :half], x[..., half:2 * half])
            c = cos[None, None]
            s = sin[None, None]
            return jnp.concatenate([x1 * c - x2 * s, x1 * s + x2 * c], axis=-1)
        key = jax.random.key(seed)
        ks = jax.random.split(key, 9)

        def xav(k, sh):
            lim = math.sqrt(6.0 / (sh[0] + sh[1]))
            return jax.random.uniform(k, sh, jnp.float32, -lim, lim)
        return {'x': jax.random.normal(ks[0], (B, L, HID), jnp.float32), 'norm_w': jnp.ones((HID,), jnp.float32), 'Wq': xav(ks[1], (HID, HID)), 'Wk': xav(ks[2], (HID, HID)), 'Wv': xav(ks[3], (HID, HID)), 'Wbeta': xav(ks[4], (NH, HID)), 'bbeta': jnp.full((NH,), 2.0, jnp.float32), 'Wig': xav(ks[5], (NH, HID)), 'big': jnp.zeros((NH,), jnp.float32), 'Wog': xav(ks[6], (NH, HID)), 'bog': jnp.zeros((NH,), jnp.float32), 'Wout': xav(ks[7], (HID, HID)), 'bout': jnp.zeros((HID,), jnp.float32)}
    _L1_attn_in = _L1_attn_setup()

    def _L1_ffn_setup():
        import jax, jax.numpy as jnp
        import numpy as np
        B, T, D, E, H = (8, 256, 128, 8, 32)
        LN_EPS = 1e-05
        key = jax.random.key(seed)
        ks = jax.random.split(key, 4)
        return {'x': jax.random.normal(ks[0], (B, T, D), dtype=jnp.float32), 'Wg': jax.random.normal(ks[1], (E, D), dtype=jnp.float32) * 0.02, 'ln_scale': jnp.ones((E, D), dtype=jnp.float32), 'ln_bias': jnp.zeros((E, D), dtype=jnp.float32), 'W1': jax.random.normal(ks[2], (E, D, H), dtype=jnp.float32) * 0.02, 'b1': jnp.zeros((E, H), dtype=jnp.float32), 'W2': jax.random.normal(ks[3], (E, H, D), dtype=jnp.float32) * 0.02, 'b2': jnp.zeros((E, D), dtype=jnp.float32)}
    _L1_ffn_in = _L1_ffn_setup()
    _d = {'L0_attn_x': _L0_attn_in['x'], 'L0_attn_Wqkv_w': _L0_attn_in['Wqkv_w'], 'L0_attn_Wqkv_b': _L0_attn_in['Wqkv_b'], 'L0_attn_gn_w': _L0_attn_in['gn_w'], 'L0_attn_gn_b': _L0_attn_in['gn_b'], 'L0_attn_out_w': _L0_attn_in['out_w'], 'L0_attn_out_b': _L0_attn_in['out_b'], 'L0_ffn_gate_w': _L0_ffn_in['gate_w'], 'L0_ffn_gate_b': _L0_ffn_in['gate_b'], 'L0_ffn_w1': _L0_ffn_in['w1'], 'L0_ffn_b1': _L0_ffn_in['b1'], 'L0_ffn_w3': _L0_ffn_in['w3'], 'L0_ffn_b3': _L0_ffn_in['b3'], 'L0_ffn_w2': _L0_ffn_in['w2'], 'L0_ffn_b2': _L0_ffn_in['b2'], 'L0_ffn_sw1': _L0_ffn_in['sw1'], 'L0_ffn_sb1': _L0_ffn_in['sb1'], 'L0_ffn_sw3': _L0_ffn_in['sw3'], 'L0_ffn_sb3': _L0_ffn_in['sb3'], 'L0_ffn_sw2': _L0_ffn_in['sw2'], 'L0_ffn_sb2': _L0_ffn_in['sb2'], 'L1_attn_norm_w': _L1_attn_in['norm_w'], 'L1_attn_Wq': _L1_attn_in['Wq'], 'L1_attn_Wk': _L1_attn_in['Wk'], 'L1_attn_Wv': _L1_attn_in['Wv'], 'L1_attn_Wbeta': _L1_attn_in['Wbeta'], 'L1_attn_bbeta': _L1_attn_in['bbeta'], 'L1_attn_Wig': _L1_attn_in['Wig'], 'L1_attn_big': _L1_attn_in['big'], 'L1_attn_Wog': _L1_attn_in['Wog'], 'L1_attn_bog': _L1_attn_in['bog'], 'L1_attn_Wout': _L1_attn_in['Wout'], 'L1_attn_bout': _L1_attn_in['bout'], 'L1_ffn_Wg': _L1_ffn_in['Wg'], 'L1_ffn_ln_scale': _L1_ffn_in['ln_scale'], 'L1_ffn_ln_bias': _L1_ffn_in['ln_bias'], 'L1_ffn_W1': _L1_ffn_in['W1'], 'L1_ffn_b1': _L1_ffn_in['b1'], 'L1_ffn_W2': _L1_ffn_in['W2'], 'L1_ffn_b2': _L1_ffn_in['b2']}
    _x0 = _d['L0_attn_x']
    _d['L0_attn_x'] = jax.random.normal(jax.random.fold_in(jax.random.key(seed), 1), (32, 256, 128), dtype=_x0.dtype)
    del _x0
    return _d

def reference(L0_attn_x, L0_attn_Wqkv_w, L0_attn_Wqkv_b, L0_attn_gn_w, L0_attn_gn_b, L0_attn_out_w, L0_attn_out_b, L0_ffn_gate_w, L0_ffn_gate_b, L0_ffn_w1, L0_ffn_b1, L0_ffn_w3, L0_ffn_b3, L0_ffn_w2, L0_ffn_b2, L0_ffn_sw1, L0_ffn_sb1, L0_ffn_sw3, L0_ffn_sb3, L0_ffn_sw2, L0_ffn_sb2, L1_attn_norm_w, L1_attn_Wq, L1_attn_Wk, L1_attn_Wv, L1_attn_Wbeta, L1_attn_bbeta, L1_attn_Wig, L1_attn_big, L1_attn_Wog, L1_attn_bog, L1_attn_Wout, L1_attn_bout, L1_ffn_Wg, L1_ffn_ln_scale, L1_ffn_ln_bias, L1_ffn_W1, L1_ffn_b1, L1_ffn_W2, L1_ffn_b2):

    def _L0_attn_ref(x, Wqkv_w, Wqkv_b, gn_w, gn_b, out_w, out_b):
        import jax, jax.numpy as jnp
        import numpy as np
        D_MODEL = 128
        N_HEADS = 32
        HEAD_DIM = D_MODEL // N_HEADS
        EPS = 1e-05
        B, S, Dm = x.shape
        H, Dh = (N_HEADS, HEAD_DIM)
        qkv = x @ Wqkv_w.T + Wqkv_b
        qkv = qkv.reshape(B, S, 3, H, Dh)
        q, k, v = (qkv[:, :, 0], qkv[:, :, 1], qkv[:, :, 2])
        a = jnp.einsum('bthd,bshd->bhts', q, k)
        ctx = jnp.einsum('bhts,bshd->bthd', a, v)
        g = ctx.transpose(0, 2, 3, 1)
        mean = g.mean(axis=(2, 3), keepdims=True)
        var = ((g - mean) ** 2).mean(axis=(2, 3), keepdims=True)
        gh = (g - mean) * jax.lax.rsqrt(var + EPS)
        gh = gh * gn_w.reshape(H, Dh, 1) + gn_b.reshape(H, Dh, 1)
        ctx = gh.transpose(0, 3, 1, 2).reshape(B, S, Dm)
        return ctx @ out_w.T + out_b

    def _L0_ffn_ref(x, gate_w, gate_b, w1, b1, w3, b3, w2, b2, sw1, sb1, sw3, sb3, sw2, sb2):
        import jax, jax.numpy as jnp
        import numpy as np
        E = 8
        TOP_K = 2
        ROUTE_SCALE = 1.0
        ALPHA = 1.702
        LIMIT = 7.0
        D = 128
        F = 128
        B, S = (2, 128)

        def swiglu(h):
            g = jnp.minimum(h[..., ::2], LIMIT)
            l = jnp.clip(h[..., 1::2], -LIMIT, LIMIT)
            return g * jax.nn.sigmoid(ALPHA * g) * (l + 1.0)
        if __name__ == '__main__':
            out = reference(**setup_inputs())
            print(out.shape, out.dtype)
        inp_shape = x.shape
        xt = x.reshape(-1, D)
        logits = xt @ gate_w.T
        scores = jax.nn.softmax(logits.astype(jnp.float32), axis=-1)
        biased = scores + gate_b.astype(jnp.float32)
        idx = jax.lax.top_k(biased, TOP_K)[1]
        weights = (jnp.take_along_axis(scores, idx, axis=-1) * ROUTE_SCALE).astype(x.dtype)
        cw = jnp.sum(jax.nn.one_hot(idx, E, dtype=x.dtype) * weights[..., None], axis=1)
        h1 = jnp.einsum('td,efd->etf', xt, w1) + b1[:, None, :]
        h3 = jnp.einsum('td,efd->etf', xt, w3) + b3[:, None, :]
        a = swiglu(h1 * h3)
        y = jnp.einsum('etf,edf->etd', a, w2) + b2[:, None, :]
        routed = jnp.einsum('te,etd->td', cw, y)
        sh = swiglu((xt @ sw1.T + sb1) * (xt @ sw3.T + sb3))
        shared = sh @ sw2.T + sb2
        return (routed + shared).reshape(inp_shape)

    def _L1_attn_ref(x, norm_w, Wq, Wk, Wv, Wbeta, bbeta, Wig, big, Wog, bog, Wout, bout):
        import jax, jax.numpy as jnp
        import numpy as np
        import math
        B, L, HID, NH = (4, 512, 128, 8)
        DH = HID // NH
        THETA = 10000.0

        def _rope_tables(seq_len, dh):
            half = dh // 2
            inv_freq = 1.0 / THETA ** (jnp.arange(half, dtype=jnp.float32) / half)
            freqs = jnp.arange(seq_len, dtype=jnp.float32)[:, None] * inv_freq[None, :]
            return (jnp.cos(freqs), jnp.sin(freqs))

        def _apply_rope(x, cos, sin):
            half = x.shape[-1] // 2
            x1, x2 = (x[..., :half], x[..., half:2 * half])
            c = cos[None, None]
            s = sin[None, None]
            return jnp.concatenate([x1 * c - x2 * s, x1 * s + x2 * c], axis=-1)
        Bq, Lq, _ = x.shape
        h = x * jax.lax.rsqrt(jnp.mean(x * x, axis=-1, keepdims=True) + 1e-06) * norm_w

        def heads(W):
            return jnp.einsum('bld,ed->ble', h, W).reshape(Bq, Lq, NH, DH).transpose(0, 2, 1, 3)
        q, k, v = (heads(Wq), heads(Wk), heads(Wv))
        cos, sin = _rope_tables(Lq, DH)
        q = _apply_rope(q, cos, sin)
        k = _apply_rope(k, cos, sin)

        def gate(W, b):
            return jax.nn.sigmoid(jnp.einsum('bld,hd->blh', h, W) + b).transpose(0, 2, 1)
        beta, ig, og = (gate(Wbeta, bbeta), gate(Wig, big), gate(Wog, bog))
        scale = 1.0 / math.sqrt(DH)
        qT = q.transpose(2, 0, 1, 3)
        kT = k.transpose(2, 0, 1, 3)
        vT = v.transpose(2, 0, 1, 3)
        fT = beta.transpose(2, 0, 1)
        gT = ig.transpose(2, 0, 1)
        oT = og.transpose(2, 0, 1)
        M0 = jnp.zeros((Bq, NH, DH, DH), x.dtype)

        def step(M, inp):
            q_t, k_t, v_t, f_t, g_t, o_t = inp
            M = M * f_t[..., None, None] + g_t[..., None, None] * scale * (k_t[..., :, None] * v_t[..., None, :])
            y_t = jnp.einsum('bhd,bhde->bhe', q_t, M) * o_t[..., None]
            return (M, y_t)
        _, yT = jax.lax.scan(step, M0, (qT, kT, vT, fT, gT, oT))
        y = yT.transpose(1, 0, 2, 3).reshape(Bq, Lq, HID)
        return jnp.einsum('bld,ed->ble', y, Wout) + bout

    def _L1_ffn_ref(x, Wg, ln_scale, ln_bias, W1, b1, W2, b2):
        import jax, jax.numpy as jnp
        import numpy as np
        B, T, D, E, H = (8, 256, 128, 8, 32)
        LN_EPS = 1e-05
        Bs, Ts, Ds = x.shape
        xt = x.reshape(Bs * Ts, Ds)
        logits = xt @ Wg.T
        top1 = jnp.argmax(logits, axis=-1)
        mu = jnp.mean(xt, axis=-1, keepdims=True)
        var = jnp.mean(jnp.square(xt - mu), axis=-1, keepdims=True)
        xhat = (xt - mu) * jax.lax.rsqrt(var + LN_EPS)
        n_experts = Wg.shape[0]

        def body(y, p):
            s_e, b_e, w1, bb1, w2, bb2, eid = p
            h = jax.nn.gelu((xhat * s_e + b_e) @ w1 + bb1, approximate=False)
            out = h @ w2 + bb2
            mask = (top1 == eid)[:, None].astype(out.dtype)
            return (y + mask * out, None)
        y0 = jnp.zeros_like(xt)
        y, _ = jax.lax.scan(body, y0, (ln_scale, ln_bias, W1, b1, W2, b2, jnp.arange(n_experts)))
        return y.reshape(Bs, Ts, Ds)
    x = L0_attn_x
    x = x + 0.5 * _L0_ffn_ref(_layernorm(x, axis=-1), L0_ffn_gate_w, L0_ffn_gate_b, L0_ffn_w1, L0_ffn_b1, L0_ffn_w3, L0_ffn_b3, L0_ffn_w2, L0_ffn_b2, L0_ffn_sw1, L0_ffn_sb1, L0_ffn_sw3, L0_ffn_sb3, L0_ffn_sw2, L0_ffn_sb2)
    x = x + _L0_attn_ref(_layernorm(x, axis=-1), L0_attn_Wqkv_w, L0_attn_Wqkv_b, L0_attn_gn_w, L0_attn_gn_b, L0_attn_out_w, L0_attn_out_b)
    x = x + 0.5 * _L0_ffn_ref(_layernorm(x, axis=-1), L0_ffn_gate_w, L0_ffn_gate_b, L0_ffn_w1, L0_ffn_b1, L0_ffn_w3, L0_ffn_b3, L0_ffn_w2, L0_ffn_b2, L0_ffn_sw1, L0_ffn_sb1, L0_ffn_sw3, L0_ffn_sb3, L0_ffn_sw2, L0_ffn_sb2)
    x = x + 0.5 * _L1_ffn_ref(_layernorm(x, axis=-1), L1_ffn_Wg, L1_ffn_ln_scale, L1_ffn_ln_bias, L1_ffn_W1, L1_ffn_b1, L1_ffn_W2, L1_ffn_b2)
    x = x + _L1_attn_ref(_layernorm(x, axis=-1), L1_attn_norm_w, L1_attn_Wq, L1_attn_Wk, L1_attn_Wv, L1_attn_Wbeta, L1_attn_bbeta, L1_attn_Wig, L1_attn_big, L1_attn_Wog, L1_attn_bog, L1_attn_Wout, L1_attn_bout)
    x = x + 0.5 * _L1_ffn_ref(_layernorm(x, axis=-1), L1_ffn_Wg, L1_ffn_ln_scale, L1_ffn_ln_bias, L1_ffn_W1, L1_ffn_b1, L1_ffn_W2, L1_ffn_b2)
    return x

_drawn_inputs = setup_inputs


def setup_inputs(seed=0):
    import zlib

    import numpy as np

    out = dict(_drawn_inputs(seed))
    spreads = {'L0_attn_gn_w': (1.0, 0.2),
     'L0_attn_gn_b': (0.0, 0.1),
     'L1_attn_norm_w': (1.0, 0.2),
     'L1_attn_bbeta': (2.0, 0.2),
     'L1_attn_big': (0.0, 0.476),
     'L1_attn_bog': (0.0, 0.8),
     'L1_attn_bout': (0.0, 0.1),
     'L1_ffn_ln_scale': (1.0, 0.6),
     'L1_ffn_ln_bias': (0.0, 0.8),
     'L1_ffn_b1': (0.0, 0.8),
     'L1_ffn_b2': (0.0, 0.1)}
    factors = {'L0_attn_Wqkv_b': 3.386,
     'L0_attn_out_b': 4.796,
     'L0_ffn_b1': 8.0,
     'L0_ffn_b3': 8.0,
     'L0_ffn_b2': 8.0,
     'L0_ffn_sb1': 4.6,
     'L0_ffn_sb3': 5.046,
     'L0_ffn_sb2': 4.32,
     'L1_ffn_W1': 7.043,
     'L1_ffn_W2': 6.497}
    for name, (base, spread) in spreads.items():
        noise = np.random.default_rng([zlib.crc32(name.encode()), seed]).standard_normal(out[name].shape)
        drawn = base * np.exp(spread * noise) if base else spread * noise
        out[name] = jnp.asarray(drawn.astype(out[name].dtype))
    for name, factor in factors.items():
        out[name] = (out[name] * factor).astype(out[name].dtype)
    return out
```

```python
from contextlib import ExitStack

import numpy as np

import concourse.bass as bass
from concourse import mybir

F32 = mybir.dt.float32
BF16 = mybir.dt.bfloat16
ALU = mybir.AluOpType
ACT = mybir.ActivationFunctionType
AX = mybir.AxisListType

P = 128
D = 128
T = 4
N = T * P
BATCH_TILES = 2
NB = T // BATCH_TILES
E = 8
NE = E + 1
F = 128
LIMIT, ALPHA = 7.0, 1.702
NH1, DH1 = 8, 16
EPS = 1e-5
RMS_EPS = 1e-6
Z_LEAST = -43.0


class Op:

    def __init__(self, stream, engine, emit, waits):
        self.stream, self.engine, self.emit, self.waits = stream, engine, emit, waits
        self.needed, self.ordinal = False, None
        self.fenced = False
        self.own_semaphore = False


class LastRound:

    def __init__(self, stream, engine):
        self.stream, self.engine = stream, engine


ENGINES = ("sync", "tensor", "vector", "scalar", "gpsimd")


class Stream:

    def __init__(self, name):
        self.name, self.steps = name, [[]]

    def step(self):
        self.steps.append([])

    def put(self, engine, emit, *waits):
        op = Op(self.name, engine, emit, [w for w in waits if w is not None])
        for w in op.waits:
            if isinstance(w, Op):
                w.needed = True
        self.steps[-1].append(op)
        return op

    def pe(self, emit, *waits):
        return self.put("tensor", emit, *waits)

    def dve(self, emit, *waits):
        return self.put("vector", emit, *waits)

    def act(self, emit, *waits):
        return self.put("scalar", emit, *waits)

    def pool(self, emit, *waits):
        return self.put("gpsimd", emit, *waits)

    def sp(self, emit, *waits):
        return self.put("sync", emit, *waits)

    def last(self, *engines):
        return [LastRound(self.name, e) for e in engines]


class Buf:

    def __init__(self, ap, free):
        self.ap, self.free = ap, list(free)


def build(nc, dram, x_in, out):
    chunks = x_in.shape[0] // N
    rounds = chunks // 2
    x_v = x_in.rearrange("(c t p) d -> c p t d", t=T, p=P)
    out_v = out.rearrange("(c t p) d -> c p t d", t=T, p=P)

    with ExitStack() as ctx:
        def sb(name, shape, dt=F32):
            return ctx.enter_context(nc.sbuf_tensor(name, shape, dt))

        const = {}
        staged = ("sel", "sel1", "later")
        for name, ap in dram.items():
            if name not in staged:
                const[name] = sb("w_" + name, list(ap.shape), ap.dtype)
        for name in ("sel", "nsel", "sel1", "later", "ident_b"):
            shape = dram[{"nsel": "sel", "ident_b": "ident"}.get(name, name)].shape
            const[name] = sb("w_" + name, list(shape), BF16)
        w13, w2, b13, b2s = const["w13"], const["w2"], const["b13"], const["b2s"]
        f1_w1s = sb("f1_w1s", [P, E * 32])
        f1_b1s = sb("f1_b1s", [P, 2])
        f1_b2p = sb("f1_b2p", [E, 3, D], BF16)
        f1_b2r = sb("f1_b2r", [E, 2, D])
        a1_wqkv = sb("a1_wqkv", [P, 3 * D])
        a1_wg = sb("a1_wg", [P, 3 * NH1])
        half_neg = sb("half_neg", [P, T])

        fence = ctx.enter_context(nc.semaphore("fence"))
        load_sem = ctx.enter_context(nc.semaphore("weights_loaded"))
        setup_dve = ctx.enter_context(nc.semaphore("setup_vector"))
        setup_pe = ctx.enter_context(nc.semaphore("setup_tensor"))
        n_loads = len(dram)

        streams = []
        for si, sn in enumerate("ab"):
            s = Stream(sn)
            s.index = si
            s.sems = {e: ctx.enter_context(nc.semaphore(f"{e}_{sn}")) for e in ENGINES}
            s.store_sem = ctx.enter_context(nc.semaphore(f"stored_{sn}"))
            s.banks = [ctx.enter_context(nc.psum_tensor(f"bank{k}_{sn}", [P, N], F32)) for k in range(4)]

            def tile(name, shape, dt=F32, sn=sn):
                return sb(f"{name}_{sn}", shape, dt)
            s.x_load = tile("x_load", [P, T, D])
            s.x = tile("x", [P, T, D])
            s.x_bias = tile("x_bias", [P, T, D])
            s.x_store = tile("x_store", [P, T, D])
            s.xn = tile("xn", [P, T, D])
            s.xt = tile("xt", [P, N])
            s.stats = tile("stats", [P, T, 6])
            s.mv = tile("mv", [P, T, 2])
            s.ve = tile("ve", [P, T])
            s.rstd = tile("rstd", [P, T])
            s.small = {k: tile(k, [P, T, E]) for k in
                       ("lg", "ex", "sc", "bi", "ge", "oh1", "b2_", "oh2", "oh", "cw", "r1_", "r2_")}
            s.red = {k: tile(k, [P, T]) for k in ("mx", "sm", "rc", "m1", "i1", "m2", "i2")}
            s.cw9 = tile("cw9", [P, T, NE])
            s.cw3 = tile("cw3", [P, T, 3, E], BF16)
            s.cwt = tile("cwt", [NE, N])
            s.cwt3 = tile("cwt3", [3 * E, N], BF16)
            arena = s.arena = tile("arena", [P, 12, N])

            def piece(i, n=1, t=None, arena=arena):
                ap = arena[:, i:i + n, :].rearrange("p a n -> p (a n)")
                return ap.rearrange("p (t d) -> p t d", t=t) if t else ap
            s.ffn = {k: [piece(i), piece(i + 1)] for k, i in
                     (("tg", 0), ("tl", 2), ("hg", 4), ("hl", 6), ("gs", 8), ("am", 10))}
            s.kv = piece(0, 2, T)
            s.qt = piece(2)
            s.kvm = tile("kvm", [P, NB, D])
            s.ctxn = piece(3)
            s.gn = {k: tile("gn_" + k, [P, NB]) for k in ("mean", "dev", "vv", "ve", "r", "sc", "t", "bi")}
            s.gst = tile("gst", [P, NB, 6])
            s.gmv = tile("gmv", [P, NB, 2])
            s.mask = tile("mask", [P, T, E], BF16)
            s.maskt = tile("maskt", [E, N], BF16)
            s.z = tile("z", [P, T, 3 * NH1])
            s.zc = tile("zc", [P, T, 3 * NH1])
            s.ez = tile("ez", [P, T, 3 * NH1])
            s.e1 = tile("e1", [P, T, 3 * NH1])
            s.lnf = tile("lnf", [P, T, NH1])
            s.gio = tile("gio", [P, T, 2 * NH1])
            s.lc = tile("lc", [P, T, NH1])
            s.lrest = tile("lrest", [P, T, NH1])
            s.ec = tile("ec", [P, T, NH1])
            s.es = tile("es", [P, T, NH1])
            s.lc3 = tile("lc3", [P, T, 3, NH1], BF16)
            s.lct3 = tile("lct3", [3 * NH1, N], BF16)
            s.qk = piece(0, 2, T)
            s.v = piece(6, 1, T)
            s.rc = piece(2, 2, T)
            s.rs = piece(4, 2, T)
            s.qpar = [tile(f"qpar{i}", [P, T, D]) for i in range(2)]
            s.kg = piece(7, 1, T)
            s.kgs = tile("kgs", [P, NB, D])
            s.qd = tile("qd", [P, NB, D])
            s.kt = piece(0)
            s.qpt = [piece(1), piece(4)]
            s.qdt = tile("qdt", [P, NB, P])
            s.st = tile("st", [P, NB, D])
            s.dec = [piece(8), piece(9)]
            s.att = [piece(10), piece(11)]
            s.yo = piece(2, 1, T)
            s.yot = piece(5)
            record(nc, s, const, dict(f1_w1s=f1_w1s, f1_b1s=f1_b1s, f1_b2p=f1_b2p, a1_wqkv=a1_wqkv,
                                      a1_wg=a1_wg, half_neg=half_neg), x_v, out_v)
            streams.append(s)

        lag = 4
        order = []
        a, b = streams[0].steps, streams[1].steps
        for i in range(len(a) + lag):
            order += a[i] if i < len(a) else []
            order += b[i - lag] if 0 <= i - lag < len(b) else []
        queues = {e: [op for op in order if op.engine == e] for e in ENGINES}
        totals = {}
        for s in streams:
            for e in ENGINES:
                mine = [op for op in queues[e] if op.stream == s.name]
                counted = [op for op in mine if not op.own_semaphore]
                if counted:
                    counted[-1].needed = True
                n = 0
                for op in mine:
                    if op.needed:
                        n += 1
                        op.ordinal = n
                totals[s.name, e] = n
        sems = {(s.name, e): s.sems[e] for s in streams for e in ENGINES}

        def run(engine_name, eng):
            step = 16 if engine_name == "sync" else 1
            for s in streams:
                eng.sem_inc(s.sems[engine_name], 1)
                if engine_name == "scalar":
                    eng.sem_inc(s.store_sem, 1)
            with eng.Fori(0, rounds) as r:
                seen = {}
                for op in queues[engine_name]:
                    for w in op.waits:
                        key = (w.stream, w.engine)
                        k = w.ordinal if isinstance(w, Op) else 0
                        if seen.get(key, -1) >= k:
                            continue
                        seen[key] = k
                        unit = 16 if w.engine == "sync" else 1
                        eng.wait_ge(sems[key], r * (totals[key] * unit) + (k * unit + 1))
                        if op.fenced:
                            eng.sem_inc(fence, 1)
                    ins = op.emit(eng, r)
                    if op.needed:
                        ins.then_inc(sems[op.stream, op.engine], step)

        arena = streams[0].arena
        stage = {
            "sel": arena[0:3 * E, 0:2, :].rearrange("p a (e n) -> p (a e) n", n=P),
            "sel1": arena[0:E, 2, 0:2 * P].rearrange("p (j n) -> p j n", j=2),
            "later": arena[:, 3, 0:P],
        }

        block = ctx.enter_context(nc.Block())

        @block.sync
        def _(eng):
            for name, ap in dram.items():
                eng.dma_start(stage[name] if name in stage else const[name][:], ap).then_inc(load_sem, 16)
            run("sync", eng)

        @block.tensor
        def _(eng):
            eng.wait_ge(load_sem, 16 * n_loads)
            for j in range(2):
                for e in range(4):
                    col = (4 * j + e) * 32
                    ins = eng.matmul(streams[0].banks[0][32 * e:32 * e + 32, j:j + 1],
                                     const["f1_w1"][:, col:col + 32],
                                     const["f1_lnb"][:, 4 * j + e:4 * j + e + 1], start=True, stop=True)
            ins.then_inc(setup_pe, 1)
            eng.wait_ge(setup_dve, 10)
            run("tensor", eng)

        @block.vector
        def _(eng):
            eng.memset(half_neg[:], -0.5).then_inc(setup_dve, 1)
            n = 1
            for s in streams:
                eng.memset(s.cw9[:, :, E:NE], 1.0)
                eng.memset(s.qpar[0][:], 0.0)
                eng.memset(s.qpar[1][:], 0.0)
            eng.wait_ge(load_sem, 16 * n_loads)
            eng.tensor_tensor(f1_w1s[:].rearrange("p (e h) -> p e h", e=E),
                              const["f1_w1"][:].rearrange("p (e h) -> p e h", e=E),
                              const["f1_lns"][:].unsqueeze(2).broadcast_to([P, E, 32]),
                              ALU.mult).then_inc(setup_dve, 1)
            eng.tensor_scalar(a1_wqkv[:], const["a1_wqkv"][:], const["a1_nw"][:], None,
                              ALU.mult).then_inc(setup_dve, 1)
            eng.tensor_scalar(a1_wg[:], const["a1_wg"][:], const["a1_nw"][:], None,
                              ALU.mult).then_inc(setup_dve, 1)
            for name in ("sel", "sel1", "later"):
                eng.tensor_copy(const[name][:], stage[name])
            eng.tensor_copy(const["ident_b"][:], const["ident"][:])
            eng.tensor_scalar(const["nsel"][:], stage["sel"], -1.0, None, ALU.mult)
            n = 4
            eng.tensor_copy(f1_b2p[:, 0, :], const["f1_b2"][:]).then_inc(setup_dve, 1)
            for k in range(2):
                n += 1
                eng.wait_ge(setup_dve, n)
                src = const["f1_b2"][:] if k == 0 else f1_b2r[:, 0, :]
                eng.tensor_tensor(f1_b2r[:, k, :], src, f1_b2p[:, k, :], ALU.subtract).then_inc(setup_dve, 1)
                n += 1
                eng.wait_ge(setup_dve, n)
                eng.tensor_copy(f1_b2p[:, k + 1, :], f1_b2r[:, k, :]).then_inc(setup_dve, 1)
            n += 1
            assert n == 9
            eng.wait_ge(setup_pe, 1)
            eng.tensor_tensor(f1_b1s[:], streams[0].banks[0][:, 0:2], const["f1_b1"][:],
                              ALU.add).then_inc(setup_dve, 1)
            eng.wait_ge(setup_dve, 10)
            run("vector", eng)

        @block.scalar
        def _(eng):
            eng.wait_ge(load_sem, 16 * n_loads)
            eng.wait_ge(setup_dve, 10)
            run("scalar", eng)
            for s in streams:
                eng.wait_ge(s.store_sem, 16 * rounds + 1)

        @block.gpsimd
        def _(eng):
            eng.wait_ge(load_sem, 16 * n_loads)
            eng.wait_ge(setup_dve, 10)
            run("gpsimd", eng)


def record(nc, s, c, w, x_v, out_v):
    ident, ident_b = c["ident"], c["ident_b"]
    prev = s.last("tensor", "vector", "scalar")
    bank = [Buf(b, prev) for b in s.banks]
    H0, H1, Y, M = bank

    def bc(ap, shape):
        return ap.broadcast_to(shape)

    loaded = s.sp(lambda e, r: e.dma_start(s.x_load[:], x_v[r * 2 + s.index]), *s.last("vector", "gpsimd"))
    loaded.fenced = True
    s.step()

    def flat(t):
        return t[:].rearrange("p t d -> p (t d)")

    def norm(x, x_ready, a, b, xt_free):
        for t in range(T):
            op = s.dve(lambda e, r, t=t: e.bn_stats(s.stats[:, t, :], x[:, t, :]), x_ready, *s.last("vector"))
        st = op
        for t in range(T):
            op = s.dve(lambda e, r, t=t: e.bn_aggr(s.mv[:, t, :], s.stats[:, t, :]), st)
            op.fenced = True
        ve = s.dve(lambda e, r: e.tensor_scalar(s.ve[:], s.mv[:, :, 1], a, b, ALU.mult, ALU.add), op)
        rs = s.pool(lambda e, r: e.tensor_tensor(s.rstd[:], s.ve[:], w["half_neg"][:], ALU.pow), ve)
        s.step()
        done = []
        for t in range(T):
            xn = s.dve(lambda e, r, t=t: e.tensor_scalar(s.xn[:, t, :], x[:, t, :], s.mv[:, t, 0:1],
                                                         s.rstd[:, t:t + 1], ALU.subtract, ALU.mult),
                       rs, *s.xn_free)
            done.append(xn)
        for t in range(T):
            tr = s.pe(lambda e, r, t=t: e.transpose(M.ap[:, t * P:(t + 1) * P], s.xn[:, t, :], ident[:]),
                      done[t], *M.free)
        s.xn_free = [tr]
        cp = s.act(lambda e, r: e.copy(s.xt[:], M.ap[:]), tr, *xt_free)
        M.free = [cp]
        s.step()
        return cp, tr

    s.xn_free = s.last("tensor")
    s.xt_free = s.last("tensor")

    def logits(weight, xt_ready):
        for t in range(T):
            op = s.pe(lambda e, r, t=t: e.matmul(M.ap[:, t * E:(t + 1) * E], s.xt[:, t * P:(t + 1) * P],
                                                 weight[:], start=True, stop=True), xt_ready, *M.free)
        return op

    def first_best(src, src_ready, mx, rank, best, onehot):
        w8 = c["w8"][:].unsqueeze(1).broadcast_to([P, T, E])
        k = s.small
        o = s.dve(lambda e, r: e.tensor_reduce(s.red[mx][:], src, AX.X, ALU.max), src_ready)
        o = s.dve(lambda e, r: e.tensor_tensor(k["ge"][:], src, bc(s.red[mx][:].unsqueeze(2), [P, T, E]),
                                               ALU.is_ge), o)
        o = s.dve(lambda e, r: e.tensor_tensor(k["ge"][:], k["ge"][:], w8, ALU.mult), o)
        o = s.dve(lambda e, r: e.tensor_reduce(s.red[rank][:], k["ge"][:], AX.X, ALU.max), o)
        o = s.dve(lambda e, r: e.tensor_tensor(onehot, w8, bc(s.red[rank][:].unsqueeze(2), [P, T, E]),
                                               ALU.is_equal), o)
        return o

    def bf16_parts(src, src_ready, parts, free):
        k = s.small
        o = s.dve(lambda e, r: e.tensor_copy(parts[:, :, 0, :], src), src_ready, *free)
        o = s.dve(lambda e, r: e.tensor_tensor(k["r1_"][:], src, parts[:, :, 0, :], ALU.subtract), o)
        o = s.dve(lambda e, r: e.tensor_copy(parts[:, :, 1, :], k["r1_"][:]), o)
        o = s.dve(lambda e, r: e.tensor_tensor(k["r2_"][:], k["r1_"][:], parts[:, :, 1, :], ALU.subtract), o)
        return s.dve(lambda e, r: e.tensor_copy(parts[:, :, 2, :], k["r2_"][:]), o)

    def ffn0(x, x_ready, x_out, x_out_free):
        xt_ready, _ = norm(x, x_ready, 1.0, EPS, s.xt_free)
        k, red = s.small, s.red
        lg = logits(c["gate"], xt_ready)
        mv = M.ap[:, 0:T * E].rearrange("p (t e) -> p t e", e=E)
        o = s.dve(lambda e, r: e.tensor_reduce(red["mx"][:], mv, AX.X, ALU.max), lg)
        o = s.dve(lambda e, r: e.tensor_tensor(k["lg"][:], mv, bc(red["mx"][:].unsqueeze(2), [P, T, E]),
                                               ALU.subtract), o)
        M.free = [o]
        o = s.act(lambda e, r: e.activation(k["ex"][:], k["lg"][:], ACT.Exp), o)
        s.step()
        o = s.dve(lambda e, r: e.tensor_reduce(red["sm"][:], k["ex"][:], AX.X, ALU.add), o)
        o = s.dve(lambda e, r: e.reciprocal(red["rc"][:], red["sm"][:]), o)
        sc = s.dve(lambda e, r: e.tensor_tensor(k["sc"][:], k["ex"][:],
                                                bc(red["rc"][:].unsqueeze(2), [P, T, E]), ALU.mult), o)
        o = s.dve(lambda e, r: e.tensor_tensor(k["bi"][:], k["sc"][:],
                                               c["gate_b"][:].unsqueeze(1).broadcast_to([P, T, E]),
                                               ALU.add), sc)
        o = first_best(k["bi"][:], o, "m1", "i1", None, k["oh1"][:])
        o = s.dve(lambda e, r: e.scalar_tensor_tensor(k["b2_"][:], k["oh1"][:], -3.0e38, k["bi"][:],
                                                      ALU.mult, ALU.add), o)
        o = first_best(k["b2_"][:], o, "m2", "i2", None, k["oh2"][:])
        o = s.dve(lambda e, r: e.tensor_tensor(k["oh"][:], k["oh1"][:], k["oh2"][:], ALU.add), o)
        cw = s.dve(lambda e, r: e.tensor_tensor(s.cw9[:, :, 0:E], k["sc"][:], k["oh"][:], ALU.mult), o,
                   *s.cw_free)
        parts = bf16_parts(s.cw9[:, :, 0:E], cw, s.cw3, s.cw_free)
        s.step()
        for t in range(T):
            o = s.pe(lambda e, r, t=t: e.transpose(M.ap[0:NE, t * P:(t + 1) * P], s.cw9[:, t, :], ident[:]),
                     cw, *M.free)
        cwt = s.act(lambda e, r: e.copy(s.cwt[:], M.ap[0:NE, :]), o, *s.cwt_free)
        M.free = [cwt]
        mb = M.ap[:].bitcast(BF16)
        for t in range(T):
            o = s.pe(lambda e, r, t=t: e.transpose(mb[0:3 * E, t * P:(t + 1) * P],
                                                   s.cw3[:, t, :, :].rearrange("p k e -> p (k e)"),
                                                   ident_b[:]), parts, *M.free)
        s.cw_free = [o]
        cwt3 = s.act(lambda e, r: e.copy(s.cwt3[:], mb[0:3 * E, 0:N]), o, *s.cwt_free)
        M.free = [cwt3]
        s.step()
        yfirst = [True]

        def half(e_, part, t_buf, h_buf, tfree, hfree):
            m3 = s.pe(lambda e, r: e.matmul(H0.ap[:], w13_(e_, 2 * part), s.xt[:], start=True, stop=True),
                      xt_ready, *H0.free)
            m1 = s.pe(lambda e, r: e.matmul(H1.ap[:], w13_(e_, 2 * part + 1), s.xt[:], start=True, stop=True),
                      *H1.free)
            t = s.act(lambda e, r: e.activation(t_buf[:], H0.ap[:], ACT.Identity,
                                                bias=c["b13"][:, e_, 2 * part:2 * part + 1]), m3, *tfree)
            H0.free = [t]
            h = s.dve(lambda e, r: e.scalar_tensor_tensor(h_buf[:], H1.ap[:],
                                                          c["b13"][:, e_, 2 * part + 1:2 * part + 2],
                                                          t_buf[:], ALU.add, ALU.mult), m1, t, *hfree)
            H1.free = [h]
            return m1, h

        def w13_(e_, part):
            return c["w13"][:, e_, part, :]

        def down(e_, a_buf, ready):
            for t in range(T):
                first = yfirst[0]
                yfirst[0] = False
                o = s.pe(lambda e, r, t=t, first=first: e.matmul(
                    Y.ap[:, t * D:(t + 1) * D], a_buf[:, t * P:(t + 1) * P], c["w2"][:, e_, :],
                    start=first, stop=False, skip_group_check=True), ready, *Y.free)
            return o

        pending = None
        for e_ in range(NE):
            i = e_ % 2
            tg, tl, hg, hl, gs, am = (s.ffn[n][i] for n in ("tg", "tl", "hg", "hl", "gs", "am"))
            m, h = half(e_, 0, tg, hg, s.use["tg", i], s.use["hg", i])
            s.use["tg", i] = [h]
            g = s.dve(lambda e, r, hg=hg: e.tensor_scalar(hg[:], hg[:], LIMIT, None, ALU.min), h)
            ga = s.act(lambda e, r, hg=hg, gs=gs: e.activation(gs[:], hg[:], ACT.Gelu_apprx_sigmoid), g,
                       *s.use["gs", i])
            s.use["hg", i] = [ga]
            s.step()
            if pending:
                o = down(*pending)
                s.use["am", 1 - i] = [o]
                s.step()
            m, h = half(e_, 1, tl, hl, s.use["tl", i], s.use["hl", i])
            s.use["tl", i] = [h]
            l = s.dve(lambda e, r, hl=hl: e.tensor_scalar(hl[:], hl[:], LIMIT, -LIMIT, ALU.min, ALU.max), h)
            if e_ < E:
                cb = s.pe(lambda e, r, e_=e_: e.matmul(M.ap[:], c["sel"][:, e_, :], s.cwt3[:], start=True,
                                                       stop=True), cwt3, *M.free)
            a = s.dve(lambda e, r, hl=hl, gs=gs, am=am: e.scalar_tensor_tensor(
                am[:], hl[:], 1.0, gs[:], ALU.add, ALU.mult), l, ga, *s.use["am", i])
            s.use["hl", i] = [a]
            s.use["gs", i] = [a]
            if e_ < E:
                a = s.dve(lambda e, r, am=am: e.tensor_tensor(am[:], am[:], M.ap[:], ALU.mult), a, cb)
                M.free = [a]
            pending = (e_, am, a)
            s.step()
        s.xt_free = [m]
        o = down(*pending)
        s.use["am", (NE - 1) % 2] = [o]
        for t in range(T):
            o = s.pe(lambda e, r, t=t: e.matmul(Y.ap[:, t * D:(t + 1) * D], s.cwt[:, t * P:(t + 1) * P],
                                                c["b2s"][:], start=False, stop=(t == T - 1),
                                                skip_group_check=True), cwt)
        s.cwt_free = [o]
        res = s.dve(lambda e, r: e.scalar_tensor_tensor(flat(x_out), Y.ap[:], 0.5, flat(x),
                                                        ALU.mult, ALU.add), o, *x_out_free)
        Y.free = [res]
        s.step()
        return res

    s.use = {(n, i): s.last("vector", "scalar", "tensor") for n in ("tg", "tl", "hg", "hl", "gs", "am")
             for i in range(2)}
    s.cw_free = s.last("tensor")
    s.cwt_free = s.last("tensor")

    def attn0(x, x_ready):
        xt_ready, tr = norm(x, x_ready, 1.0, EPS, s.xt_free)
        xb = s.pool(lambda e, r: e.tensor_tensor(s.x_bias[:], x[:], c["a0_ob"][:].unsqueeze(1)
                                                 .broadcast_to([P, T, D]), ALU.add), x_ready, tr)
        q = s.pe(lambda e, r: e.matmul(M.ap[:], c["a0_wq"][:], s.xt[:], start=True, stop=True), xt_ready,
                 *M.free)
        qs = s.act(lambda e, r: e.activation(s.qt[:], M.ap[:], ACT.Identity, bias=c["a0_bq"][:]), q,
                   *s.last("tensor"))
        M.free = [qs]
        kvs = []
        for b, B in enumerate((H0, H1)):
            for j in range(BATCH_TILES):
                t = b * BATCH_TILES + j
                o = s.pe(lambda e, r, t=t, j=j, B=B: e.matmul(B.ap[:, j * 2 * D:(j + 1) * 2 * D],
                                                              s.xt[:, t * P:(t + 1) * P], c["a0_wkv"][:],
                                                              start=True, stop=True), *B.free)
            bias = c["a0_bkv"][:].unsqueeze(1).broadcast_to([P, BATCH_TILES, 2 * D])
            kv = s.dve(lambda e, r, b=b, B=B, bias=bias: e.tensor_tensor(
                s.kv[:, b * BATCH_TILES:(b + 1) * BATCH_TILES, :],
                B.ap[:].rearrange("p (j n) -> p j n", j=BATCH_TILES), bias, ALU.add), o, *s.last("tensor"))
            B.free = [kv]
            kvs.append(kv)
        s.xt_free = [o]
        s.step()
        for b in range(NB):
            for j in range(BATCH_TILES):
                t = b * BATCH_TILES + j
                o = s.pe(lambda e, r, t=t, b=b, j=j: e.matmul(
                    Y.ap[:, b * D:(b + 1) * D], s.kv[:, t, 0:D], s.kv[:, t, D:2 * D], start=(j == 0),
                    stop=(j == BATCH_TILES - 1)), kvs[b], *Y.free)
        km = s.dve(lambda e, r: e.tensor_tensor(s.kvm[:], Y.ap[:, 0:NB * D].rearrange("p (b d) -> p b d", b=NB),
                                                c["blk4"][:].unsqueeze(1).broadcast_to([P, NB, D]),
                                                ALU.mult), o)
        Y.free = [km]
        for b in range(NB):
            o = s.pe(lambda e, r, b=b: e.matmul(M.ap[:, b * 256:(b + 1) * 256], s.kvm[:, b, :],
                                                s.qt[:, b * 256:(b + 1) * 256], start=True, stop=True),
                     km, qs, *M.free)
        ctx_ready = o
        s.step()
        g = s.gn
        for b in range(NB):
            o = s.dve(lambda e, r, b=b: e.bn_stats(s.gst[:, b, :], M.ap[:, b * 256:(b + 1) * 256]), ctx_ready)
        st = o
        for b in range(NB):
            o = s.dve(lambda e, r, b=b: e.bn_aggr(s.gmv[:, b, :], s.gst[:, b, :]), st)
            o.fenced = True
        gm = s.pe(lambda e, r: e.matmul(Y.ap[:, 0:NB], c["avg4"][:], s.gmv[:, :, 0], start=True, stop=True),
                  o, *Y.free)
        mean = s.dve(lambda e, r: e.tensor_copy(g["mean"][:], Y.ap[:, 0:NB]), gm)
        Y.free = [mean]
        o = s.dve(lambda e, r: e.tensor_tensor(g["dev"][:], s.gmv[:, :, 0], g["mean"][:], ALU.subtract), mean)
        o = s.dve(lambda e, r: e.tensor_tensor(g["dev"][:], g["dev"][:], g["dev"][:], ALU.mult), o)
        o = s.dve(lambda e, r: e.tensor_tensor(g["vv"][:], g["dev"][:], s.gmv[:, :, 1], ALU.add), o)
        gv = s.pe(lambda e, r: e.matmul(Y.ap[:, 0:NB], c["avg4"][:], g["vv"][:], start=True, stop=True),
                  o, *Y.free)
        o = s.dve(lambda e, r: e.tensor_scalar(g["ve"][:], Y.ap[:, 0:NB], EPS, None, ALU.add), gv)
        Y.free = [o]
        o = s.pool(lambda e, r: e.tensor_tensor(g["r"][:], g["ve"][:], w["half_neg"][:, 0:NB], ALU.pow), o)
        s.step()
        sc = s.dve(lambda e, r: e.tensor_scalar(g["sc"][:], g["r"][:], c["a0_gnw"][:], None, ALU.mult), o)
        o = s.dve(lambda e, r: e.tensor_tensor(g["t"][:], g["mean"][:], g["sc"][:], ALU.mult), sc)
        o = s.dve(lambda e, r: e.tensor_scalar(g["bi"][:], g["t"][:], -1.0, c["a0_gnb"][:], ALU.mult,
                                               ALU.add), o)
        for b in range(NB):
            cn = s.act(lambda e, r, b=b: e.activation(s.ctxn[:, b * 256:(b + 1) * 256],
                                                      M.ap[:, b * 256:(b + 1) * 256], ACT.Identity,
                                                      bias=g["bi"][:, b:b + 1], scale=g["sc"][:, b:b + 1]),
                       o, *s.last("tensor"))
        M.free = [cn]
        for t in range(T):
            o = s.pe(lambda e, r, t=t: e.matmul(H0.ap[:, t * D:(t + 1) * D], s.ctxn[:, t * P:(t + 1) * P],
                                                c["a0_wo"][:], start=True, stop=True), cn, *H0.free)
        res = s.dve(lambda e, r: e.tensor_tensor(flat(x), H0.ap[:], flat(s.x_bias), ALU.add), o, xb)
        H0.free = [res]
        s.step()
        return res

    def ffn1(x, x_ready, x_out, x_out_free):
        xt_ready, _ = norm(x, x_ready, 1.0 + EPS, EPS * EPS, s.xt_free)
        lg = logits(c["f1_gate"], xt_ready)
        k = s.small
        cp = s.dve(lambda e, r: e.tensor_copy(k["lg"][:], M.ap[:, 0:T * E].rearrange("p (t e) -> p t e", e=E)),
                   lg)
        M.free = [cp]
        mk = first_best(k["lg"][:], cp, "m1", "i1", None, s.mask[:])
        mb = M.ap[:].bitcast(BF16)
        hs = []
        for j, B in enumerate((H0, H1)):
            m = s.pe(lambda e, r, j=j, B=B: e.matmul(B.ap[:], w["f1_w1s"][:, j * P:(j + 1) * P], s.xt[:],
                                                     start=True, stop=True), xt_ready, *B.free)
            ga = s.act(lambda e, r, j=j, B=B: e.activation(s.ffn["gs"][j][:], B.ap[:], ACT.Gelu,
                                                           bias=w["f1_b1s"][:, j:j + 1]), m,
                       *s.use["gs", j])
            B.free = [ga]
            hs.append(ga)
        s.xt_free = [m]
        s.step()
        for t in range(T):
            o = s.pe(lambda e, r, t=t: e.transpose(mb[0:E, t * P:(t + 1) * P], s.mask[:, t, :], ident_b[:]),
                     mk, *M.free)
        mt = s.act(lambda e, r: e.copy(s.maskt[:], mb[0:E, 0:N]), o, *s.maskt_free)
        M.free = [mt]
        s.step()
        gm = []
        for j in range(2):
            o = s.pe(lambda e, r, j=j: e.matmul(M.ap[:], c["sel1"][:, j, :], s.maskt[:], start=True,
                                                stop=True), mt, *M.free)
            o = s.dve(lambda e, r, j=j: e.tensor_tensor(s.ffn["am"][j][:], s.ffn["gs"][j][:], M.ap[:], ALU.mult), o, hs[j],
                      *s.use["am", j])
            M.free = [o]
            s.use["gs", j] = [o]
            gm.append(o)
        s.step()
        first = True
        for t in range(T):
            for j in range(2):
                o = s.pe(lambda e, r, t=t, j=j, first=first: e.matmul(
                    Y.ap[:, t * D:(t + 1) * D], s.ffn["am"][j][:, t * P:(t + 1) * P], c["f1_w2"][:, j, :],
                    start=first, stop=False, skip_group_check=True), gm[j], *Y.free)
                first = False
            for j in range(3):
                o = s.pe(lambda e, r, t=t, j=j: e.matmul(
                    Y.ap[:, t * D:(t + 1) * D], s.maskt[:, t * P:(t + 1) * P], w["f1_b2p"][:, j, :],
                    start=False, stop=(t == T - 1 and j == 2), skip_group_check=True), mt)
        s.use["am", 0] = [o]
        s.use["am", 1] = [o]
        s.maskt_free = [o]
        res = s.dve(lambda e, r: e.scalar_tensor_tensor(flat(x_out), Y.ap[:], 0.5, flat(x), ALU.mult,
                                                        ALU.add), o, *x_out_free)
        Y.free = [res]
        s.step()
        return res

    s.maskt_free = s.last("tensor")

    def attn1(x, x_ready):
        xt_ready, tr = norm(x, x_ready, 1.0 + RMS_EPS, EPS * RMS_EPS, s.xt_free)
        G = 3 * NH1
        ring = [H0, H1, M]
        turn = [0]

        def take():
            turn[0] += 1
            return ring[turn[0] % 3]

        xb = s.pool(lambda e, r: e.tensor_tensor(s.x_bias[:], x[:], c["a1_ob"][:].unsqueeze(1)
                                                 .broadcast_to([P, T, D]), ALU.add), x_ready, tr)
        B = take()
        for t in range(T):
            o = s.pe(lambda e, r, t=t, B=B: e.matmul(B.ap[:, t * G:(t + 1) * G], s.xt[:, t * P:(t + 1) * P],
                                                     w["a1_wg"][:], start=True, stop=True), xt_ready, *B.free)
        z = s.dve(lambda e, r, B=B: e.tensor_tensor(
            s.z[:], B.ap[:, 0:T * G].rearrange("p (t g) -> p t g", t=T),
            c["a1_bg"][:].unsqueeze(1).broadcast_to([P, T, G]), ALU.add), o)
        B.free = [z]
        o = s.dve(lambda e, r: e.tensor_scalar(s.zc[:], s.z[:], Z_LEAST, None, ALU.max), z)
        o = s.act(lambda e, r: e.activation(s.ez[:], s.zc[:], ACT.Exp, scale=-1.0), o)
        e1 = s.dve(lambda e, r: e.tensor_scalar(s.e1[:], s.ez[:], 1.0, None, ALU.add), o)
        lnf = s.act(lambda e, r: e.activation(s.lnf[:], s.e1[:, :, 0:NH1], ACT.Ln), e1)
        gio = s.dve(lambda e, r: e.reciprocal(s.gio[:], s.e1[:, :, NH1:G]), e1)
        s.step()
        for t in range(T):
            B = take()
            o = s.pe(lambda e, r, t=t, B=B: e.matmul(B.ap[:, 0:3 * D], s.xt[:, t * P:(t + 1) * P],
                                                     w["a1_wqkv"][:], start=True, stop=True), xt_ready, *B.free)
            qk = s.act(lambda e, r, t=t, B=B: e.copy(s.qk[:, t, :], B.ap[:, 0:2 * D]), o, *s.last("vector"))
            v = s.act(lambda e, r, t=t, B=B: e.copy(s.v[:, t, :], B.ap[:, 2 * D:3 * D]), *s.last("tensor"))
            B.free = [v]
        s.xt_free = [o]
        s.step()
        NHH = 2 * NH1
        hd = DH1 // 2

        def heads(tl):
            return tl[:].rearrange("p t (h d) -> p t h d", h=NHH)

        cosb = c["cos"][:].unsqueeze(2).broadcast_to([P, T, NHH, DH1])
        o1 = s.dve(lambda e, r: e.tensor_tensor(heads(s.rc), heads(s.qk), cosb, ALU.mult), qk)
        for hh in range(2):
            sinb = c["sin"][:, :, hh * hd:(hh + 1) * hd].unsqueeze(2).broadcast_to([P, T, NHH, hd])
            o2 = s.dve(lambda e, r, hh=hh, sinb=sinb: e.tensor_tensor(
                heads(s.rs)[:, :, :, hh * hd:(hh + 1) * hd],
                heads(s.qk)[:, :, :, (1 - hh) * hd:(2 - hh) * hd], sinb, ALU.mult), qk)
        ks = s.dve(lambda e, r: e.tensor_tensor(s.rc[:, :, D:2 * D], s.rc[:, :, D:2 * D],
                                                s.rs[:, :, D:2 * D], ALU.add), o2)
        qps = []
        for par in range(2):
            def view(tl, par=par):
                return tl[:, :, 0:D].rearrange("p t (g h d) -> p t g h d", h=2, d=DH1)[:, :, :, par, :]
            qps.append(s.dve(lambda e, r, par=par, view=view: e.tensor_tensor(
                view(s.qpar[par]), view(s.rc), view(s.rs), ALU.add), o2, *s.last("tensor")))
        s.step()
        B = take()
        NL = T * NH1
        o = s.pe(lambda e, r, B=B: e.matmul(B.ap[:, 0:NL], c["tri"][:], s.lnf[:].rearrange("p t h -> p (t h)"),
                                            start=True, stop=True), lnf, *B.free)
        o = s.pe(lambda e, r, B=B: e.matmul(B.ap[:, NL:2 * NL], c["ones"][:],
                                            s.lnf[:].rearrange("p t h -> p (t h)"), start=True, stop=True))
        lc = s.dve(lambda e, r, B=B: e.tensor_copy(s.lc[:].rearrange("p t h -> p (t h)"), B.ap[:, 0:NL]), o)
        lr = s.dve(lambda e, r, B=B: e.tensor_tensor(s.lrest[:].rearrange("p t h -> p (t h)"),
                                                     B.ap[:, NL:2 * NL],
                                                     s.lc[:].rearrange("p t h -> p (t h)"),
                                                     ALU.subtract), lc)
        B.free = [lr]
        ec = s.act(lambda e, r: e.activation(s.ec[:], s.lc[:], ACT.Exp, scale=-1.0), lc)
        es = s.act(lambda e, r: e.activation(s.es[:], s.lrest[:], ACT.Exp, scale=-1.0), lr)
        parts = bf16_parts(s.lc[:], lc, s.lc3, s.last("tensor"))
        def hv(ap):
            return ap.rearrange("p t (h d) -> p t h d", h=NH1)
        kg = s.dve(lambda e, r: e.tensor_tensor(hv(s.kg[:]), hv(s.rc[:, :, D:2 * D]),
                                                s.gio[:, :, 0:NH1].unsqueeze(3)
                                                .broadcast_to([P, T, NH1, DH1]), ALU.mult),
                   ks, gio, *s.last("tensor"))
        kgs = s.dve(lambda e, r: e.tensor_tensor(
            hv(s.kgs[:]), hv(s.kg[:, 0:T:2, :]), s.es[:, 0:T:2, :].unsqueeze(3)
            .broadcast_to([P, NB, NH1, DH1]), ALU.mult), kg, es, *s.last("tensor"))
        for par in range(2):
            def view(tl, par=par):
                return tl.rearrange("p t (g h d) -> p t g h d", h=2, d=DH1)[:, :, :, par, :]
            ecv = s.ec[:, 1:T:2, :].rearrange("p t (g h) -> p t g h", h=2)[:, :, :, par]
            qd = s.dve(lambda e, r, par=par, view=view, ecv=ecv: e.tensor_tensor(
                view(s.qd[:]), view(s.qpar[par][:, 1:T:2, :]),
                ecv.unsqueeze(3).broadcast_to([P, NB, NH1 // 2, DH1]), ALU.mult), qps[1], ec,
                *s.last("tensor"))
        s.step()
        tgt = [(s.kg, s.kt, kg, T), (s.qpar[0], s.qpt[0], qps[0], T), (s.qpar[1], s.qpt[1], qps[1], T)]
        got = []
        for src, dst, ready, n in tgt:
            B = take()
            for t in range(n):
                o = s.pe(lambda e, r, t=t, src=src, B=B: e.transpose(B.ap[:, t * P:(t + 1) * P], src[:, t, :],
                                                                     ident[:]), ready, *B.free)
            cp = s.act(lambda e, r, dst=dst, B=B: e.copy(dst[:], B.ap[:]), o, *s.last("tensor"))
            B.free = [cp]
            got.append(cp)
        B = take()
        for j in range(NB):
            o = s.pe(lambda e, r, j=j, B=B: e.transpose(B.ap[:, j * P:(j + 1) * P], s.qd[:, j, :], ident[:]),
                     qd, *B.free)
        qdt = s.act(lambda e, r, B=B: e.copy(s.qdt[:].rearrange("p b n -> p (b n)"), B.ap[:, 0:NB * P]), o,
                    *s.last("tensor"))
        B.free = [qdt]
        B = take()
        bb = B.ap[:].bitcast(BF16)
        for t in range(T):
            o = s.pe(lambda e, r, t=t, bb=bb: e.transpose(bb[0:3 * NH1, t * P:(t + 1) * P],
                                                          s.lc3[:, t, :, :].rearrange("p k e -> p (k e)"),
                                                          ident_b[:]), parts, *B.free)
        lct = s.act(lambda e, r, bb=bb: e.copy(s.lct3[:], bb[0:3 * NH1, 0:N]), o, *s.last("tensor"))
        B.free = [lct]
        s.step()
        B = take()
        for b in range(NB):
            o = s.pe(lambda e, r, b=b, B=B: e.matmul(B.ap[:, b * D:(b + 1) * D], s.kgs[:, b, :],
                                                     s.v[:, b * BATCH_TILES, :], start=True, stop=True),
                     kgs, v, *B.free)
        st = s.dve(lambda e, r, B=B: e.tensor_tensor(s.st[:], B.ap[:, 0:NB * D]
                                                     .rearrange("p (b d) -> p b d", b=NB),
                                                     c["blk16"][:].unsqueeze(1).broadcast_to([P, NB, D]),
                                                     ALU.mult), o, *s.last("tensor"))
        B.free = [st]
        for b in range(NB):
            t = b * BATCH_TILES + 1
            o = s.pe(lambda e, r, b=b, t=t: e.matmul(Y.ap[:, t * D:(t + 1) * D], s.qdt[:, b, :], s.st[:, b, :],
                                                     start=(b == 0), stop=False, skip_group_check=True),
                     st, qdt, *Y.free)
        s.step()
        dec_free = [s.last("tensor", "vector"), s.last("tensor", "vector")]
        att_free = [s.last("tensor"), s.last("tensor")]

        def pv(h, ready):
            for t in range(T):
                o = s.pe(lambda e, r, t=t, h=h: e.matmul(
                    Y.ap[:, t * D + h * DH1:t * D + (h + 1) * DH1], s.att[h % 2][:, t * P:(t + 1) * P],
                    s.v[:, t, h * DH1:(h + 1) * DH1], start=False,
                    stop=(h == NH1 - 1 and t == T - 1), skip_group_check=True), ready)
            att_free[h % 2] = [o]
            return o

        pend = None
        for h in range(NH1):
            strip, par = 32 * (h // 2), h % 2
            B = take()
            s.pe(lambda e, r, h=h, B=B: e.matmul(B.ap[:], c["sel"][:, h, :], s.lct3[:], start=True, stop=False,
                                                 skip_group_check=True), lct, *B.free)
            for t in range(T):
                s.pe(lambda e, r, h=h, t=t, B=B: e.matmul(B.ap[:, t * P:(t + 1) * P],
                                                          s.lct3[:, t * P:(t + 1) * P], c["nsel"][:, h, :],
                                                          start=False, stop=False, skip_group_check=True))
            o = s.pe(lambda e, r, B=B: e.matmul(B.ap[:], ident_b[:], c["later"][:].unsqueeze(1)
                                                .broadcast_to([P, T, P]), start=False, stop=True,
                                                skip_group_check=True))
            de = s.act(lambda e, r, h=h, B=B: e.activation(s.dec[h % 2][:], B.ap[:], ACT.Exp, scale=-1.0), o,
                       *dec_free[h % 2])
            B.free = [de]
            B = take()
            for t in range(T):
                sl = slice(t * P, (t + 1) * P)
                o = s.pe(lambda e, r, sl=sl, strip=strip, par=par, B=B: e.matmul(
                    B.ap[:, sl], s.kt[strip:strip + 32, sl], s.qpt[par][strip:strip + 32, sl], start=True,
                    stop=True), *got, *B.free)
            at = s.dve(lambda e, r, h=h, B=B: e.tensor_tensor(s.att[h % 2][:], s.dec[h % 2][:], B.ap[:],
                                                              ALU.mult), o, de, *att_free[h % 2])
            B.free = [at]
            dec_free[h % 2] = [at]
            if pend:
                pv(*pend)
            pend = (h, at)
            s.step()
        o = pv(*pend)
        yo = s.dve(lambda e, r: e.tensor_tensor(hv(s.yo[:]), Y.ap[:].rearrange("p (t h d) -> p t h d", t=T, h=NH1),
                                               s.gio[:, :, NH1:2 * NH1].unsqueeze(3)
                                               .broadcast_to([P, T, NH1, DH1]), ALU.mult), o,
                  *s.last("tensor"))
        Y.free = [yo]
        B = take()
        for t in range(T):
            o = s.pe(lambda e, r, t=t, B=B: e.transpose(B.ap[:, t * P:(t + 1) * P], s.yo[:, t, :], ident[:]),
                     yo, *B.free)
        yt = s.act(lambda e, r, B=B: e.activation(s.yot[:], B.ap[:], ACT.Copy, scale=float(DH1) ** -0.5), o,
                   *s.last("tensor"))
        B.free = [yt]
        s.step()
        B = take()
        for t in range(T):
            o = s.pe(lambda e, r, t=t, B=B: e.matmul(B.ap[:, t * D:(t + 1) * D], s.yot[:, t * P:(t + 1) * P],
                                                     c["a1_wo"][:], start=True, stop=True), yt, *B.free)
        res = s.dve(lambda e, r, B=B: e.tensor_tensor(flat(x), B.ap[:], flat(s.x_bias), ALU.add), o, xb)
        B.free = [res]
        s.step()
        return res

    r_ = ffn0(s.x_load, loaded, s.x, s.last("vector", "gpsimd"))
    r_ = attn0(s.x, r_)
    r_ = ffn0(s.x, r_, s.x, [])
    r_ = ffn1(s.x, r_, s.x, [])
    r_ = attn1(s.x, r_)

    s.dve(lambda e, r: e.wait_ge(s.store_sem, r * 16 + 1)).own_semaphore = True
    r_ = ffn1(s.x, r_, s.x_store, [])
    s.act(lambda e, r: e.dma_start(out_v[r * 2 + s.index], s.x_store[:]).then_inc(s.store_sem, 16),
          r_).own_semaphore = True


def constants():
    k = {}
    k["ident"] = np.eye(P, dtype=np.float32)
    k["w8"] = np.tile(np.arange(E, 0, -1, dtype=np.float32), (P, 1))
    sel = np.zeros((3 * E, E, P), np.float32)
    for e in range(E):
        sel[[e, E + e, 2 * E + e], e, :] = 1
    k["sel"] = sel
    sel1 = np.zeros((E, 2, P), np.float32)
    for e in range(E):
        sel1[e, e // 4, (e % 4) * 32:(e % 4) * 32 + 32] = 1
    k["sel1"] = sel1
    i = np.arange(P)
    k["blk4"] = (i[:, None] // 4 == i[None] // 4).astype(np.float32)
    k["avg4"] = k["blk4"] * np.float32(0.25)
    k["blk16"] = (i[:, None] // 16 == i[None] // 16).astype(np.float32)
    k["tri"] = (i[:, None] <= i[None]).astype(np.float32)
    k["ones"] = np.ones((P, P), np.float32)
    k["later"] = (i[:, None] > i[None]).astype(np.float32) * np.float32(30000.0)
    half = DH1 // 2
    inv = (np.float32(1.0) / np.float32(10000.0) ** (np.arange(half, dtype=np.float32) / np.float32(half)))
    pos = (np.arange(T) % BATCH_TILES)[None] * P + i[:, None]
    ang = pos[:, :, None].astype(np.float32) * inv.astype(np.float32)
    cos, sin = np.cos(ang).astype(np.float32), np.sin(ang).astype(np.float32)
    k["cos"] = np.concatenate([cos, cos], -1)
    k["sin"] = np.concatenate([-sin, sin], -1)
    return k


def kernel(**inputs):
    import concourse.bacc as _bacc
    from concourse.bass_utils import run_bass_kernel_spmd as _run

    a = {k: np.asarray(v) for k, v in inputs.items()}
    f0, f1, a0, a1 = "L0_ffn_", "L1_ffn_", "L0_attn_", "L1_attn_"
    x = a[a0 + "x"]

    def rows(v):
        return np.tile(v[None], (P, 1))

    def w13(w, sw):
        v = np.concatenate([w, sw[None]], 0).reshape(NE, F, 2, D)
        return v.transpose(3, 0, 2, 1)

    def b13(b, sb_):
        return np.concatenate([b, sb_[None]], 0).reshape(NE, F, 2).transpose(1, 0, 2)

    lay = {}
    w1v, w3v = w13(a[f0 + "w1"], a[f0 + "sw1"]), w13(a[f0 + "w3"], a[f0 + "sw3"])
    lay["w13"] = np.stack([w3v[:, :, 0], w1v[:, :, 0], w3v[:, :, 1], w1v[:, :, 1]], 2)
    b1v, b3v = b13(a[f0 + "b1"], a[f0 + "sb1"]), b13(a[f0 + "b3"], a[f0 + "sb3"])
    lay["b13"] = np.stack([b3v[:, :, 0], b1v[:, :, 0], b3v[:, :, 1], b1v[:, :, 1]], 2)
    lay["w2"] = np.concatenate([a[f0 + "w2"], a[f0 + "sw2"][None]], 0).transpose(2, 0, 1)
    lay["b2s"] = np.concatenate([a[f0 + "b2"], a[f0 + "sb2"][None]], 0)
    lay["gate"] = a[f0 + "gate_w"].T
    lay["gate_b"] = rows(a[f0 + "gate_b"])
    wqkv, bqkv = a[a0 + "Wqkv_w"], a[a0 + "Wqkv_b"]
    lay["a0_wq"] = wqkv[0:D].T
    lay["a0_wkv"] = wqkv[D:].T
    lay["a0_bq"] = bqkv[0:D, None]
    lay["a0_bkv"] = rows(bqkv[D:])
    lay["a0_gnw"] = a[a0 + "gn_w"][:, None]
    lay["a0_gnb"] = a[a0 + "gn_b"][:, None]
    lay["a0_wo"] = a[a0 + "out_w"].T
    lay["a0_ob"] = rows(a[a0 + "out_b"])
    lay["f1_gate"] = a[f1 + "Wg"].T
    lay["f1_lns"] = a[f1 + "ln_scale"].T
    lay["f1_lnb"] = a[f1 + "ln_bias"].T
    lay["f1_w1"] = a[f1 + "W1"].transpose(1, 0, 2).reshape(D, E * 32)
    lay["f1_b1"] = a[f1 + "b1"].reshape(2, P).T
    lay["f1_w2"] = a[f1 + "W2"].reshape(2, P, D).transpose(1, 0, 2)
    lay["f1_b2"] = a[f1 + "b2"]
    lay["a1_nw"] = a[a1 + "norm_w"][:, None]
    lay["a1_wqkv"] = np.concatenate([a[a1 + "Wq"], a[a1 + "Wk"], a[a1 + "Wv"]], 0).T
    lay["a1_wg"] = np.concatenate([a[a1 + "Wbeta"], a[a1 + "Wig"], a[a1 + "Wog"]], 0).T
    lay["a1_bg"] = rows(np.concatenate([a[a1 + "bbeta"], a[a1 + "big"], a[a1 + "bog"]], 0))
    lay["a1_wo"] = a[a1 + "Wout"].T
    lay["a1_ob"] = rows(a[a1 + "bout"])
    lay.update(constants())
    lay = {k: np.ascontiguousarray(v) for k, v in lay.items()}

    nc = _bacc.Bacc("TRN2", target_bir_lowering=False, num_devices=1)
    arrays = {"in_" + k: v for k, v in lay.items()}
    dram = {k: nc.dram_tensor("in_" + k, v.shape, mybir.dt.from_np(v.dtype), kind="ExternalInput").ap()
            for k, v in lay.items()}
    arrays["x_dram"] = np.ascontiguousarray(x.reshape(-1, D))
    x_in = nc.dram_tensor("x_dram", arrays["x_dram"].shape, F32, kind="ExternalInput").ap()
    out = nc.dram_tensor("out_dram", arrays["x_dram"].shape, F32, kind="ExternalOutput").ap()
    build(nc, dram, x_in, out)
    r = _run(nc, [arrays], core_ids=[0])
    return r.results[0]["out_dram"].reshape(x.shape)
```

```python
from contextlib import ExitStack

import numpy as np

import concourse.bass as bass
from concourse import mybir

F32 = mybir.dt.float32
BF16 = mybir.dt.bfloat16
F16 = mybir.dt.float16
I32 = mybir.dt.int32
ALU = mybir.AluOpType
ACT = mybir.ActivationFunctionType
AX = mybir.AxisListType

P = 128
D = 128
T = 4
N = T * P
BATCH_TILES = 2
NB = T // BATCH_TILES
DEBUG = True
OFFSET = 0.5
E = 8
NE = E + 1
F = 128
LIMIT, ALPHA = 7.0, 1.702
NH1, DH1 = 8, 16
EPS = 1e-5
RMS_EPS = 1e-6
NM = 4 * NE + 1
X_SCALE = 1024.0
W_TOP = 2.0 ** 14
W_LEAST = 2.0 ** -40
Z_LEAST = -43.0


SETUP_STEPS = 20


class Op:

    def __init__(self, stream, engine, emit, waits):
        self.stream, self.engine, self.emit, self.waits = stream, engine, emit, waits
        self.needed, self.ordinal = False, None
        self.took = None
        self.behind = 0
        self.fenced = False
        self.own_semaphore = False


class LastRound:

    def __init__(self, stream, engine):
        self.stream, self.engine = stream, engine


ENGINES = ("sync", "tensor", "vector", "scalar", "gpsimd")


class Stream:

    def __init__(self, name):
        self.name, self.steps = name, [[]]

    def step(self):
        self.steps.append([])

    def put(self, engine, emit, *waits):
        op = Op(self.name, engine, emit, [w for w in waits if w is not None])
        for w in op.waits:
            if isinstance(w, Op):
                w.needed = True
        self.steps[-1].append(op)
        return op

    def pe(self, emit, *waits):
        return self.put("tensor", emit, *waits)

    def dve(self, emit, *waits):
        return self.put("vector", emit, *waits)

    def act(self, emit, *waits):
        return self.put("scalar", emit, *waits)

    def pool(self, emit, *waits):
        return self.put("gpsimd", emit, *waits)

    def sp(self, emit, *waits):
        return self.put("sync", emit, *waits)

    def last(self, *engines):
        return [LastRound(self.name, e) for e in engines]


class Estimate:

    @staticmethod
    def columns(ap):
        n = 1
        for k in ap.shape[1:]:
            n *= k
        return n

    def matmul(self, out, lhsT, rhs, **_):
        passes = 4 if rhs.dtype == F32 else 1
        return passes * max(self.columns(out), P) / 2400

    def transpose(self, out, in_, identity):
        return P / 2400

    def two_inputs(self, out, *_, **__):
        return 0.09 + self.columns(out) / 960

    tensor_tensor = scalar_tensor_tensor = two_inputs

    def one_input(self, out, *_, **__):
        return 0.07 + self.columns(out) / 1920

    tensor_scalar = tensor_copy = one_input

    def reduction(self, out, in_, *_):
        return 0.07 + self.columns(in_) / 960

    tensor_reduce = bn_stats = bn_aggr = reciprocal = reduction

    def activation(self, out, in_, func, *_, **__):
        self.table = TABLES.get(func)
        return 0.13 + self.columns(out) / 1200

    def copy(self, out, in_):
        return 0.06 + self.columns(out) / 1200

    def dma_start(self, *_):
        return 2.0


TABLES = {ACT.Gelu_apprx_sigmoid: 1, ACT.Exp: 2, ACT.Ln: 2, ACT.Gelu: 3}
TABLE_LOAD = 1.3
HOPS = {"tensor": 0.25, "vector": 0.13, "scalar": 0.2, "gpsimd": 0.2, "sync": 0.0}


def estimate(op):
    e = Estimate()
    e.table = None
    if op.own_semaphore:
        return 0.0, None
    t = op.emit(e, 0)
    return (t + 0.7 if op.engine == "gpsimd" else t), e.table


def play(lanes):
    queues = [{e: [op for op in lane if op.engine == e] for e in ENGINES} for lane in lanes]
    at = [dict.fromkeys(ENGINES, 0) for _ in lanes]
    inside = {op for lane in lanes for op in lane}
    free = dict.fromkeys(ENGINES, 0.0)
    end, order, starts = {}, [], {}
    ready_at = {}
    table = None
    for op in inside:
        if op.took is None:
            op.took = estimate(op)
    while len(order) < len(inside):
        best = None
        for n, q in enumerate(queues):
            for e in ENGINES:
                if at[n][e] == len(q[e]):
                    continue
                op = q[e][at[n][e]]
                if op not in ready_at:
                    needs = [w for w in op.waits if isinstance(w, Op) and w in inside
                             and w.behind == op.behind]
                    if any(w not in end for w in needs):
                        continue
                    ready_at[op] = max([0.0] + [end[w] + HOPS[w.engine] for w in needs])
                start = max(ready_at[op], free[e])
                if op.took[1] and op.took[1] != table:
                    start += TABLE_LOAD
                if best is None or (start, ready_at[op], n) < best[:3]:
                    best = (start, ready_at[op], n, op)
        start, _, n, op = best
        at[n][op.engine] += 1
        starts[op] = start
        end[op] = free[op.engine] = start + op.took[0]
        table = op.took[1] or table
        order.append(op)
    return order, starts, max(end.values())


class Buf:

    def __init__(self, ap, free):
        self.ap, self.free = ap, list(free)


def build(nc, dram, x_in, out):
    chunks = x_in.shape[0] // N
    nc.disable_value_cache = True
    rounds = chunks // 2
    x_v = x_in.rearrange("(c t p) d -> c p t d", t=T, p=P)
    out_v = out.rearrange("(c t p) d -> c p t d", t=T, p=P)

    with ExitStack() as ctx:
        def sb(name, shape, dt=F32):
            return ctx.enter_context(nc.sbuf_tensor(name, shape, dt))

        const = {}
        staged = ("sel", "sel1", "later", "w13", "gate")
        for name, ap in dram.items():
            if name not in staged:
                const[name] = sb("w_" + name, list(ap.shape), ap.dtype)
        for name in ("sel", "nsel", "sel1", "later", "ident_b"):
            shape = dram[{"nsel": "sel", "ident_b": "ident"}.get(name, name)].shape
            const[name] = sb("w_" + name, list(shape), BF16)
        f1_w1s = sb("f1_w1s", [P, E * 32])
        f1_b1s = sb("f1_b1s", [P, 2])
        f1_b2p = sb("f1_b2p", [E, 3, D], BF16)
        f1_b2r = sb("f1_b2r", [E, 2, D])
        w_hi = sb("w_hi", [P, 4 * NE, F], F16)
        w_lo = sb("w_lo", [P, 4 * NE, F], F16)
        g_hi = sb("g_hi", [P, E], F16)
        g_lo = sb("g_lo", [P, E], F16)
        w_max = sb("w_max", [P, NM])
        w_maxt = sb("w_maxt", [NM, 4])
        w_diag = sb("w_diag", [NM, P])
        w_scale = sb("w_scale", [P, NM])
        w_back = sb("w_back", [P, NM])
        sc31 = sb("sc31", [P, NE, 2])
        b3s = sb("b3s", [P, NE, 2])
        b1s = sb("b1s", [P, NE, 2])
        inv_back = sb("inv_back", [P, NM])
        a1_wqkv = sb("a1_wqkv", [P, 3 * D])
        a1_wg = sb("a1_wg", [P, 3 * NH1])
        half_neg = sb("half_neg", [P, T])

        fence = ctx.enter_context(nc.semaphore("fence"))
        load_sem = ctx.enter_context(nc.semaphore("weights_loaded"))
        setup_dve = ctx.enter_context(nc.semaphore("setup_vector"))
        setup_pe = ctx.enter_context(nc.semaphore("setup_tensor"))
        n_loads = len(dram)

        streams = []
        for si, sn in enumerate("ab"):
            s = Stream(sn)
            s.index = si
            s.sems = {e: ctx.enter_context(nc.semaphore(f"{e}_{sn}")) for e in ENGINES}
            s.store_sem = ctx.enter_context(nc.semaphore(f"stored_{sn}"))
            s.banks = [ctx.enter_context(nc.psum_tensor(f"bank{k}_{sn}", [P, N], F32)) for k in range(4)]

            def tile(name, shape, dt=F32, sn=sn):
                return sb(f"{name}_{sn}", shape, dt)
            s.x_load = tile("x_load", [P, T, D])
            s.x = tile("x", [P, T, D])
            s.x_bias = tile("x_bias", [P, T, D])
            s.x_store = tile("x_store", [P, T, D])
            s.xn = tile("xn", [P, T, D])
            s.xt = tile("xt", [P, N])
            s.xh = tile("xh", [P, N], F16)
            s.cwb = [tile(f"cwb{i}", [P, N]) for i in range(2)]
            s.xl = tile("xl", [P, N], F16)
            s.stats = tile("stats", [P, T, 6])
            s.mv = tile("mv", [P, T, 2])
            s.ve = tile("ve", [P, T])
            s.rstd = tile("rstd", [P, T])
            s.small = {k: tile(k, [P, T, E]) for k in
                       ("lg", "ex", "sc", "bi", "ge", "oh1", "b2_", "oh2", "oh", "cw", "r1_", "r2_")}
            s.red = {k: tile(k, [P, T]) for k in ("mx", "sm", "rc", "m1", "i1", "m2", "i2")}
            s.cw9 = tile("cw9", [P, T, NE])
            s.cw3 = tile("cw3", [P, T, 3, E], BF16)
            s.cwt = tile("cwt", [NE, N])
            s.cwt3 = tile("cwt3", [3 * E, N], BF16)
            arena = s.arena = tile("arena", [P, 12, N])

            def piece(i, n=1, t=None, arena=arena):
                ap = arena[:, i:i + n, :].rearrange("p a n -> p (a n)")
                return ap.rearrange("p (t d) -> p t d", t=t) if t else ap
            s.ffn = {k: [piece(i), piece(i + 1)] for k, i in
                     (("tg", 0), ("tl", 2), ("hg", 4), ("hl", 6), ("gs", 8), ("am", 10))}
            s.kv = piece(0, 2, T)
            s.qt = piece(2)
            s.kvm = tile("kvm", [P, NB, D])
            s.ctxn = piece(3)
            s.gn = {k: tile("gn_" + k, [P, NB]) for k in ("mean", "dev", "vv", "ve", "r", "sc", "t", "bi")}
            s.gst = tile("gst", [P, NB, 6])
            s.gmv = tile("gmv", [P, NB, 2])
            s.mask = tile("mask", [P, T, E], BF16)
            s.maskt = tile("maskt", [E, N], BF16)
            s.z = tile("z", [P, T, 3 * NH1])
            s.zc = tile("zc", [P, T, 3 * NH1])
            s.ez = tile("ez", [P, T, 3 * NH1])
            s.e1 = tile("e1", [P, T, 3 * NH1])
            s.lnf = tile("lnf", [P, T, NH1])
            s.gio = tile("gio", [P, T, 2 * NH1])
            s.lc = tile("lc", [P, T, NH1])
            s.lrest = tile("lrest", [P, T, NH1])
            s.ec = tile("ec", [P, T, NH1])
            s.es = tile("es", [P, T, NH1])
            s.lc3 = tile("lc3", [P, T, 3, NH1], BF16)
            s.lct3 = tile("lct3", [3 * NH1, N], BF16)
            s.qk = piece(0, 2, T)
            s.v = piece(6, 1, T)
            s.rc = piece(2, 2, T)
            s.rs = piece(4, 2, T)
            s.qpar = [tile(f"qpar{i}", [P, T, D]) for i in range(2)]
            s.kg = piece(7, 1, T)
            s.kgs = tile("kgs", [P, NB, D])
            s.qd = tile("qd", [P, NB, D])
            s.kt = piece(0)
            s.qpt = [piece(1), piece(4)]
            s.qdt = tile("qdt", [P, NB, P])
            s.st = tile("st", [P, NB, D])
            s.dec = [piece(8), piece(9)]
            s.att = [piece(10), piece(11)]
            s.yo = piece(2, 1, T)
            s.yot = piece(5)
            record(nc, s, const, dict(f1_w1s=f1_w1s, f1_b1s=f1_b1s, f1_b2p=f1_b2p, a1_wqkv=a1_wqkv,
                                      a1_wg=a1_wg, half_neg=half_neg,
                                      w_hi=w_hi, w_lo=w_lo, g_hi=g_hi, g_lo=g_lo, w_back=w_back,
                                      sc31=sc31, b3s=b3s, b1s=b1s), x_v, out_v)
            streams.append(s)

        lanes = []
        for s in streams:
            ops = [op for step in s.steps for op in step]
            _, starts, length = play([ops])
            alone = length
            if DEBUG and s.index == 0:
                print({k: round(starts[v], 1) for k, v in s.marks})
            cut = len(ops)
            if s.index == 1:
                cut = next(i for i, op in enumerate(ops) if op.engine == "tensor" and
                           starts[op] >= (1 - OFFSET) * length)
                for op in ops[cut:]:
                    op.behind = 1
            lanes.append(ops[cut:] + ops[:cut])
        order, _, length = play(lanes)
        if DEBUG:
            print("SBUF left", nc.sbuf_bytes_remaining)
            print("estimated round", length, "alone", alone,
                  {e: sum(op.took[0] for op in order if op.engine == e) for e in ENGINES})
        queues = {e: [op for op in order if op.engine == e] for e in ENGINES}
        totals = {}
        for s in streams:
            for e in ENGINES:
                mine = [op for step in s.steps for op in step if op.engine == e]
                counted = [op for op in mine if not op.own_semaphore]
                if counted:
                    counted[-1].needed = True
                n = 0
                for op in mine:
                    if op.needed:
                        n += 1
                        op.ordinal = n
                totals[s.name, e] = n
        sems = {(s.name, e): s.sems[e] for s in streams for e in ENGINES}

        def run(engine_name, eng):
            step = 16 if engine_name == "sync" else 1
            for s in streams:
                eng.sem_inc(s.sems[engine_name], 1)
                if engine_name == "scalar":
                    eng.sem_inc(s.store_sem, 1)

            def once(r, chosen):
                seen = {}
                base = {}

                def before(key, behind):
                    if (key, behind) not in base:
                        per_round = totals[key] * (16 if key[1] == "sync" else 1)
                        v = (r - behind) * per_round + 1
                        base[key, behind] = v if isinstance(v, int) else eng.snap(v)
                    return base[key, behind]
                for op in queues[engine_name]:
                    if op.behind not in chosen:
                        continue
                    mine = r - op.behind if op.behind else r
                    for w in op.waits:
                        key = (w.stream, w.engine)
                        k = w.ordinal if isinstance(w, Op) else 0
                        if seen.get(key, (-9, 0)) >= (-op.behind, k):
                            continue
                        seen[key] = (-op.behind, k)
                        unit = 16 if w.engine == "sync" else 1
                        eng.wait_ge(sems[key], before(key, op.behind) + k * unit)
                        if op.fenced:
                            eng.sem_inc(fence, 1)
                    ins = op.emit(eng, mine)
                    if op.needed:
                        ins.then_inc(sems[op.stream, op.engine], step)

            once(0, (0,))
            with eng.Fori(1, rounds) as r:
                once(r, (0, 1))
            once(rounds, (1,))

        arena = streams[0].arena
        stage = {
            "sel": arena[0:3 * E, 0:2, :].rearrange("p a (e n) -> p (a e) n", n=P),
            "sel1": arena[0:E, 2, 0:2 * P].rearrange("p (j n) -> p j n", j=2),
            "later": arena[:, 3, 0:P],
            "gate": arena[:, 3, P:P + E],
            "w13": streams[1].arena[:, 0:9, :].rearrange("p a n -> p (a n)").rearrange("p (m n) -> p m n",
                                                                                    n=F),
        }

        block = ctx.enter_context(nc.Block())

        @block.sync
        def _(eng):
            for name, ap in dram.items():
                eng.dma_start(stage[name] if name in stage else const[name][:], ap).then_inc(load_sem, 16)
            run("sync", eng)

        @block.tensor
        def _(eng):
            eng.wait_ge(load_sem, 16 * n_loads)
            for j in range(2):
                for e in range(4):
                    col = (4 * j + e) * 32
                    ins = eng.matmul(streams[0].banks[0][32 * e:32 * e + 32, j:j + 1],
                                     const["f1_w1"][:, col:col + 32],
                                     const["f1_lnb"][:, 4 * j + e:4 * j + e + 1], start=True, stop=True)
            ins.then_inc(setup_pe, 1)
            eng.wait_ge(setup_dve, 11)
            eng.transpose(streams[1].banks[0][0:NM, 0:P], w_max[:], const["ident"][:]).then_inc(setup_pe, 1)
            eng.wait_ge(setup_dve, 14)
            eng.matmul(streams[1].banks[1][:, 0:NM], w_diag[:], const["ident"][0:NM, 0:NM], start=True,
                       stop=True).then_inc(setup_pe, 1)
            eng.wait_ge(setup_dve, SETUP_STEPS)
            run("tensor", eng)

        @block.vector
        def _(eng):
            eng.memset(half_neg[:], -0.5).then_inc(setup_dve, 1)
            n = 1
            for s in streams:
                eng.memset(s.cw9[:, :, E:NE], 1.0)
                eng.memset(s.qpar[0][:], 0.0)
                eng.memset(s.qpar[1][:], 0.0)
            eng.wait_ge(load_sem, 16 * n_loads)
            eng.tensor_tensor(f1_w1s[:].rearrange("p (e h) -> p e h", e=E),
                              const["f1_w1"][:].rearrange("p (e h) -> p e h", e=E),
                              const["f1_lns"][:].unsqueeze(2).broadcast_to([P, E, 32]),
                              ALU.mult).then_inc(setup_dve, 1)
            eng.tensor_scalar(a1_wqkv[:], const["a1_wqkv"][:], const["a1_nw"][:], None,
                              ALU.mult).then_inc(setup_dve, 1)
            eng.tensor_scalar(a1_wg[:], const["a1_wg"][:], const["a1_nw"][:], None,
                              ALU.mult).then_inc(setup_dve, 1)
            for name in ("sel", "sel1", "later"):
                eng.tensor_copy(const[name][:], stage[name])
            eng.tensor_copy(const["ident_b"][:], const["ident"][:])
            eng.tensor_scalar(const["nsel"][:], stage["sel"], -1.0, None, ALU.mult)
            n = 4
            eng.tensor_copy(f1_b2p[:, 0, :], const["f1_b2"][:]).then_inc(setup_dve, 1)
            for k in range(2):
                n += 1
                eng.wait_ge(setup_dve, n)
                src = const["f1_b2"][:] if k == 0 else f1_b2r[:, 0, :]
                eng.tensor_tensor(f1_b2r[:, k, :], src, f1_b2p[:, k, :], ALU.subtract).then_inc(setup_dve, 1)
                n += 1
                eng.wait_ge(setup_dve, n)
                eng.tensor_copy(f1_b2p[:, k + 1, :], f1_b2r[:, k, :]).then_inc(setup_dve, 1)
            n += 1
            assert n == 9
            eng.wait_ge(setup_pe, 1)
            eng.tensor_tensor(f1_b1s[:], streams[0].banks[0][:, 0:2], const["f1_b1"][:],
                              ALU.add).then_inc(setup_dve, 1)
            n = 10

            def then(ins):
                nonlocal n
                ins.then_inc(setup_dve, 1)
                n += 1
                eng.wait_ge(setup_dve, n)

            w13 = stage["w13"]
            eng.tensor_reduce(w_max[:, 0:NM - 1], w13, AX.X, ALU.max, apply_absolute_value=True)
            then(eng.tensor_reduce(w_max[:, NM - 1:NM], stage["gate"], AX.X, ALU.max,
                                   apply_absolute_value=True))
            eng.wait_ge(setup_pe, 2)
            then(eng.tensor_reduce(w_maxt[:, 0:1], streams[1].banks[0][0:NM, 0:P], AX.X, ALU.max))
            then(eng.tensor_scalar(w_maxt[:, 1:2].bitcast(I32), w_maxt[:, 0:1].bitcast(I32), 0x7F800000, None,
                                   ALU.bitwise_and))
            then(eng.tensor_scalar(w_diag[:], const["ones"][0:NM, :], w_maxt[:, 1:2], W_LEAST, ALU.mult,
                                   ALU.max))
            eng.wait_ge(setup_pe, 3)
            then(eng.tensor_scalar(w_back[:], streams[1].banks[1][:, 0:NM], 1.0 / (W_TOP * X_SCALE), None,
                                   ALU.mult))
            then(eng.reciprocal(inv_back[:], w_back[:]))
            then(eng.tensor_scalar(w_scale[:], inv_back[:], 1.0 / X_SCALE, None, ALU.mult))
            def by_part(tl, k):
                return tl[:, 0:4 * NE].rearrange("p (e h k) -> p e h k", h=2, k=2)[:, :, :, k]
            def bias(k):
                return const["b13"][:].rearrange("p e (h k) -> p e h k", k=2)[:, :, :, k]
            eng.tensor_tensor(sc31[:], by_part(w_back, 0), by_part(w_back, 1), ALU.mult)
            eng.tensor_tensor(b3s[:], bias(0), by_part(w_back, 1), ALU.mult)
            eng.tensor_tensor(b1s[:], bias(1), by_part(inv_back, 1), ALU.mult)
            eng.tensor_scalar(stage["gate"], stage["gate"], w_scale[:, NM - 1:NM], None, ALU.mult)
            then(eng.tensor_tensor(w13, w13, w_scale[:, 0:NM - 1].unsqueeze(2).broadcast_to([P, NM - 1, F]),
                                   ALU.mult))
            eng.tensor_copy(g_hi[:], stage["gate"])
            then(eng.tensor_copy(w_hi[:], w13))
            eng.tensor_tensor(g_lo[:], stage["gate"], g_hi[:], ALU.subtract)
            then(eng.tensor_tensor(w_lo[:], w13, w_hi[:], ALU.subtract))
            assert n == SETUP_STEPS
            run("vector", eng)

        @block.scalar
        def _(eng):
            eng.wait_ge(load_sem, 16 * n_loads)
            eng.wait_ge(setup_dve, SETUP_STEPS)
            run("scalar", eng)
            for s in streams:
                eng.wait_ge(s.store_sem, 16 * rounds + 1)

        @block.gpsimd
        def _(eng):
            eng.wait_ge(load_sem, 16 * n_loads)
            eng.wait_ge(setup_dve, SETUP_STEPS)
            run("gpsimd", eng)


def record(nc, s, c, w, x_v, out_v):
    ident, ident_b = c["ident"], c["ident_b"]
    prev = s.last("tensor", "vector", "scalar")
    bank = [Buf(b, prev) for b in s.banks]
    H0, H1, Y, M = bank

    def bc(ap, shape):
        return ap.broadcast_to(shape)

    loaded = s.sp(lambda e, r: e.dma_start(s.x_load[:], x_v[r * 2 + s.index]), *s.last("vector", "gpsimd"))
    loaded.fenced = True
    s.step()

    def flat(t):
        return t[:].rearrange("p t d -> p (t d)")

    def norm(x, x_ready, a, b, xt_free, split=False):
        for t in range(T):
            op = s.dve(lambda e, r, t=t: e.bn_stats(s.stats[:, t, :], x[:, t, :]), x_ready, *s.last("vector"))
        st = op
        for t in range(T):
            op = s.dve(lambda e, r, t=t: e.bn_aggr(s.mv[:, t, :], s.stats[:, t, :]), st)
            op.fenced = True
        ve = s.dve(lambda e, r: e.tensor_scalar(s.ve[:], s.mv[:, :, 1], a, b, ALU.mult, ALU.add), op)
        rs = s.pool(lambda e, r: e.tensor_tensor(s.rstd[:], s.ve[:], w["half_neg"][:], ALU.pow), ve)
        s.step()
        done = []
        for t in range(T):
            xn = s.dve(lambda e, r, t=t: e.tensor_scalar(s.xn[:, t, :], x[:, t, :], s.mv[:, t, 0:1],
                                                         s.rstd[:, t:t + 1], ALU.subtract, ALU.mult),
                       rs, *s.xn_free)
            done.append(xn)
        for t in range(T):
            tr = s.pe(lambda e, r, t=t: e.transpose(M.ap[:, t * P:(t + 1) * P], s.xn[:, t, :], ident[:]),
                      done[t], *M.free)
        s.xn_free = [tr]
        if split:
            hi = s.act(lambda e, r: e.activation(s.xh[:], M.ap[:], ACT.Copy, scale=X_SCALE), tr, *xt_free)
            cp = s.dve(lambda e, r: e.scalar_tensor_tensor(s.xl[:], M.ap[:], X_SCALE, s.xh[:], ALU.mult,
                                                           ALU.subtract), hi, *xt_free)
        else:
            cp = s.act(lambda e, r: e.copy(s.xt[:], M.ap[:]), tr, *xt_free)
        M.free = [cp]
        s.step()
        return cp, tr

    s.xn_free = s.last("tensor")
    s.xt_free = s.last("tensor")
    s.xh_free = s.last("tensor")

    def logits(weight, xt_ready):
        for t in range(T):
            op = s.pe(lambda e, r, t=t: e.matmul(M.ap[:, t * E:(t + 1) * E], s.xt[:, t * P:(t + 1) * P],
                                                 weight[:], start=True, stop=True), xt_ready, *M.free)
        return op

    def first_best(src, src_ready, mx, rank, best, onehot):
        w8 = c["w8"][:].unsqueeze(1).broadcast_to([P, T, E])
        k = s.small
        o = s.dve(lambda e, r: e.tensor_reduce(s.red[mx][:], src, AX.X, ALU.max), src_ready)
        o = s.dve(lambda e, r: e.tensor_tensor(k["ge"][:], src, bc(s.red[mx][:].unsqueeze(2), [P, T, E]),
                                               ALU.is_ge), o)
        o = s.dve(lambda e, r: e.tensor_tensor(k["ge"][:], k["ge"][:], w8, ALU.mult), o)
        o = s.dve(lambda e, r: e.tensor_reduce(s.red[rank][:], k["ge"][:], AX.X, ALU.max), o)
        o = s.dve(lambda e, r: e.tensor_tensor(onehot, w8, bc(s.red[rank][:].unsqueeze(2), [P, T, E]),
                                               ALU.is_equal), o)
        return o

    def bf16_parts(src, src_ready, parts, free):
        k = s.small
        o = s.dve(lambda e, r: e.tensor_copy(parts[:, :, 0, :], src), src_ready, *free)
        o = s.dve(lambda e, r: e.tensor_tensor(k["r1_"][:], src, parts[:, :, 0, :], ALU.subtract), o)
        o = s.dve(lambda e, r: e.tensor_copy(parts[:, :, 1, :], k["r1_"][:]), o)
        o = s.dve(lambda e, r: e.tensor_tensor(k["r2_"][:], k["r1_"][:], parts[:, :, 1, :], ALU.subtract), o)
        return s.dve(lambda e, r: e.tensor_copy(parts[:, :, 2, :], k["r2_"][:]), o)

    def ffn0(x, x_ready, x_out, x_out_free):
        xt_ready, _ = norm(x, x_ready, 1.0, EPS, s.xh_free, split=True)
        k, red = s.small, s.red
        for t in range(T):
            sl = slice(t * P, (t + 1) * P)
            for n, (xp, gp) in enumerate(((s.xh, w["g_hi"]), (s.xl, w["g_hi"]), (s.xh, w["g_lo"]))):
                lg = s.pe(lambda e, r, t=t, sl=sl, n=n, xp=xp, gp=gp: e.matmul(
                    M.ap[:, t * E:(t + 1) * E], xp[:, sl], gp[:], start=(n == 0), stop=(n == 2)),
                    xt_ready, *M.free)
        mv = M.ap[:, 0:T * E].rearrange("p (t e) -> p t e", e=E)
        o = s.dve(lambda e, r: e.tensor_reduce(red["mx"][:], mv, AX.X, ALU.max), lg)
        o = s.dve(lambda e, r: e.tensor_tensor(k["lg"][:], mv, bc(red["mx"][:].unsqueeze(2), [P, T, E]),
                                               ALU.subtract), o)
        M.free = [o]
        o = s.act(lambda e, r: e.activation(k["ex"][:], k["lg"][:], ACT.Exp,
                                            scale=w["w_back"][:, NM - 1:NM]), o)
        s.step()
        o = s.dve(lambda e, r: e.tensor_reduce(red["sm"][:], k["ex"][:], AX.X, ALU.add), o)
        o = s.dve(lambda e, r: e.reciprocal(red["rc"][:], red["sm"][:]), o)
        sc = s.dve(lambda e, r: e.tensor_tensor(k["sc"][:], k["ex"][:],
                                                bc(red["rc"][:].unsqueeze(2), [P, T, E]), ALU.mult), o)
        o = s.dve(lambda e, r: e.tensor_tensor(k["bi"][:], k["sc"][:],
                                               c["gate_b"][:].unsqueeze(1).broadcast_to([P, T, E]),
                                               ALU.add), sc)
        o = first_best(k["bi"][:], o, "m1", "i1", None, k["oh1"][:])
        o = s.dve(lambda e, r: e.scalar_tensor_tensor(k["b2_"][:], k["oh1"][:], -3.0e38, k["bi"][:],
                                                      ALU.mult, ALU.add), o)
        o = first_best(k["b2_"][:], o, "m2", "i2", None, k["oh2"][:])
        o = s.dve(lambda e, r: e.tensor_tensor(k["oh"][:], k["oh1"][:], k["oh2"][:], ALU.add), o)
        cw = s.dve(lambda e, r: e.tensor_tensor(s.cw9[:, :, 0:E], k["sc"][:], k["oh"][:], ALU.mult), o,
                   *s.cw_free)
        parts = bf16_parts(s.cw9[:, :, 0:E], cw, s.cw3, s.cw_free)
        s.step()
        for t in range(T):
            o = s.pe(lambda e, r, t=t: e.transpose(M.ap[0:NE, t * P:(t + 1) * P], s.cw9[:, t, :], ident[:]),
                     cw, *M.free)
        cwt = s.act(lambda e, r: e.copy(s.cwt[:], M.ap[0:NE, :]), o, *s.cwt_free)
        M.free = [cwt]
        mb = M.ap[:].bitcast(BF16)
        for t in range(T):
            o = s.pe(lambda e, r, t=t: e.transpose(mb[0:3 * E, t * P:(t + 1) * P],
                                                   s.cw3[:, t, :, :].rearrange("p k e -> p (k e)"),
                                                   ident_b[:]), parts, *M.free)
        s.cw_free = [o]
        cwt3 = s.act(lambda e, r: e.copy(s.cwt3[:], mb[0:3 * E, 0:N]), o, *s.cwt_free)
        M.free = [cwt3]
        s.step()
        yfirst = [True]

        ring = [H0, H1, M]
        turn = [0]

        def take():
            turn[0] += 1
            return ring[turn[0] % 3]

        def project(B, e_, part):
            m = 4 * e_ + part
            wh, wl = w["w_hi"][:, m, :], w["w_lo"][:, m, :]
            for n, (wp, xp) in enumerate(((wh, s.xh), (wh, s.xl), (wl, s.xh))):
                o = s.pe(lambda e, r, n=n, wp=wp, xp=xp: e.matmul(B.ap[:], wp, xp[:], start=(n == 0),
                                                                  stop=(n == 2)), xt_ready, *B.free)
            return o

        def half(e_, part, t_buf, h_buf, tfree, hfree):
            B3, B1 = take(), take()
            m3 = project(B3, e_, 2 * part)
            m1 = project(B1, e_, 2 * part + 1)
            t = s.act(lambda e, r: e.activation(t_buf[:], B3.ap[:], ACT.Identity,
                                                scale=w["sc31"][:, e_, part:part + 1],
                                                bias=w["b3s"][:, e_, part:part + 1]), m3, *tfree)
            B3.free = [t]
            h = s.dve(lambda e, r: e.scalar_tensor_tensor(h_buf[:], B1.ap[:], w["b1s"][:, e_, part:part + 1],
                                                          t_buf[:], ALU.add, ALU.mult), m1, t, *hfree)
            B1.free = [h]
            return m1, h

        def down(e_, a_buf, ready):
            for t in range(T):
                first = yfirst[0]
                yfirst[0] = False
                o = s.pe(lambda e, r, t=t, first=first: e.matmul(
                    Y.ap[:, t * D:(t + 1) * D], a_buf[:, t * P:(t + 1) * P], c["w2"][:, e_, :],
                    start=first, stop=False, skip_group_check=True), ready, *Y.free)
            return o

        s.marks.append(("experts" + str(len(s.marks)), cwt3))
        live = {}

        def gate_half(e_):
            i = e_ % 2
            hg, gs = s.ffn["hg"][i], s.ffn["gs"][i]
            live[e_] = u = {}
            u["m"], h = half(e_, 0, s.ffn["tg"][i], hg, s.use["tg", i], s.use["hg", i])
            s.use["tg", i] = [h]
            return u, h, hg, gs, i

        def hold(u, h, hg, gs, i):
            u["g"] = s.dve(lambda e, r: e.tensor_scalar(hg[:], hg[:], LIMIT, None, ALU.min), h)

        def gate_act(u, h, hg, gs, i):
            g = u["g"]
            u["ga"] = s.act(lambda e, r: e.activation(gs[:], hg[:], ACT.Gelu_apprx_sigmoid), g,
                            *s.use["gs", i])
            s.use["hg", i] = [u["ga"]]

        def linear_half(e_):
            i = e_ % 2
            u = live[e_]
            u["m"], u["h"] = half(e_, 1, s.ffn["tl"][i], s.ffn["hl"][i], s.use["tl", i], s.use["hl", i])
            s.use["tl", i] = [u["h"]]

        def clip(e_):
            u, hl = live[e_], s.ffn["hl"][e_ % 2]
            u["l"] = s.dve(lambda e, r: e.tensor_scalar(hl[:], hl[:], LIMIT, -LIMIT, ALU.min, ALU.max),
                           u["h"])

        def combine(e_):
            i = e_ % 2
            u, hl, gs, am = live[e_], s.ffn["hl"][i], s.ffn["gs"][i], s.ffn["am"][i]
            u["a"] = s.dve(lambda e, r: e.scalar_tensor_tensor(am[:], hl[:], 1.0, gs[:], ALU.add, ALU.mult),
                           u["l"], u["ga"], *s.use["am", i])
            s.use["hl", i] = [u["a"]]
            s.use["gs", i] = [u["a"]]

        def spread(e_):
            i, C = e_ % 2, take()
            cb = s.pe(lambda e, r: e.matmul(C.ap[:], c["sel"][:, e_, :], s.cwt3[:], start=True,
                                            stop=True), cwt3, *C.free)
            live[e_]["cb"] = s.act(lambda e, r: e.copy(s.cwb[i][:], C.ap[:]), cb, *s.use["cwb", i])
            C.free = [live[e_]["cb"]]

        def weigh(e_):
            i = e_ % 2
            u, am = live[e_], s.ffn["am"][i]
            u["a"] = s.dve(lambda e, r: e.tensor_tensor(am[:], am[:], s.cwb[i][:], ALU.mult), u["a"], u["cb"])
            s.use["cwb", i] = [u["a"]]

        for e_ in range(NE + 2):
            one, two = e_ - 1, e_ - 2
            if e_ < NE:
                g = gate_half(e_)
            if 0 <= one < NE:
                clip(one)
            if e_ < NE:
                hold(*g)
            if 0 <= one < NE:
                combine(one)
            if e_ < E:
                spread(e_)
            if 0 <= two:
                o = down(two, s.ffn["am"][two % 2], live[two]["a"])
                s.use["am", two % 2] = [o]
            s.step()
            if e_ < NE:
                linear_half(e_)
                gate_act(*g)
            if 0 <= one < E:
                weigh(one)
            s.step()
        s.xh_free = [live[NE - 1]["m"]]
        for t in range(T):
            o = s.pe(lambda e, r, t=t: e.matmul(Y.ap[:, t * D:(t + 1) * D], s.cwt[:, t * P:(t + 1) * P],
                                                c["b2s"][:], start=False, stop=(t == T - 1),
                                                skip_group_check=True), cwt)
        s.cwt_free = [o]
        res = s.dve(lambda e, r: e.scalar_tensor_tensor(flat(x_out), Y.ap[:], 0.5, flat(x),
                                                        ALU.mult, ALU.add), o, *x_out_free)
        Y.free = [res]
        s.step()
        s.marks.append(("end" + str(len(s.marks)), res))
        return res

    s.use = {(n, i): s.last("vector", "scalar", "tensor") for n in ("tg", "tl", "hg", "hl", "gs", "am", "cwb")
             for i in range(2)}
    s.cw_free = s.last("tensor")
    s.cwt_free = s.last("tensor")

    def attn0(x, x_ready):
        xt_ready, tr = norm(x, x_ready, 1.0, EPS, s.xt_free)
        xb = s.pool(lambda e, r: e.tensor_tensor(s.x_bias[:], x[:], c["a0_ob"][:].unsqueeze(1)
                                                 .broadcast_to([P, T, D]), ALU.add), x_ready, tr)
        q = s.pe(lambda e, r: e.matmul(M.ap[:], c["a0_wq"][:], s.xt[:], start=True, stop=True), xt_ready,
                 *M.free)
        qs = s.act(lambda e, r: e.activation(s.qt[:], M.ap[:], ACT.Identity, bias=c["a0_bq"][:]), q,
                   *s.last("tensor"))
        M.free = [qs]
        kvs = []
        for b, B in enumerate((H0, H1)):
            for j in range(BATCH_TILES):
                t = b * BATCH_TILES + j
                o = s.pe(lambda e, r, t=t, j=j, B=B: e.matmul(B.ap[:, j * 2 * D:(j + 1) * 2 * D],
                                                              s.xt[:, t * P:(t + 1) * P], c["a0_wkv"][:],
                                                              start=True, stop=True), *B.free)
            bias = c["a0_bkv"][:].unsqueeze(1).broadcast_to([P, BATCH_TILES, 2 * D])
            kv = s.dve(lambda e, r, b=b, B=B, bias=bias: e.tensor_tensor(
                s.kv[:, b * BATCH_TILES:(b + 1) * BATCH_TILES, :],
                B.ap[:].rearrange("p (j n) -> p j n", j=BATCH_TILES), bias, ALU.add), o, *s.last("tensor"))
            B.free = [kv]
            kvs.append(kv)
        s.xt_free = [o]
        s.step()
        for b in range(NB):
            for j in range(BATCH_TILES):
                t = b * BATCH_TILES + j
                o = s.pe(lambda e, r, t=t, b=b, j=j: e.matmul(
                    Y.ap[:, b * D:(b + 1) * D], s.kv[:, t, 0:D], s.kv[:, t, D:2 * D], start=(j == 0),
                    stop=(j == BATCH_TILES - 1)), kvs[b], *Y.free)
        km = s.dve(lambda e, r: e.tensor_tensor(s.kvm[:], Y.ap[:, 0:NB * D].rearrange("p (b d) -> p b d", b=NB),
                                                c["blk4"][:].unsqueeze(1).broadcast_to([P, NB, D]),
                                                ALU.mult), o)
        Y.free = [km]
        for b in range(NB):
            o = s.pe(lambda e, r, b=b: e.matmul(M.ap[:, b * 256:(b + 1) * 256], s.kvm[:, b, :],
                                                s.qt[:, b * 256:(b + 1) * 256], start=True, stop=True),
                     km, qs, *M.free)
        ctx_ready = o
        s.step()
        g = s.gn
        for b in range(NB):
            o = s.dve(lambda e, r, b=b: e.bn_stats(s.gst[:, b, :], M.ap[:, b * 256:(b + 1) * 256]), ctx_ready)
        st = o
        for b in range(NB):
            o = s.dve(lambda e, r, b=b: e.bn_aggr(s.gmv[:, b, :], s.gst[:, b, :]), st)
            o.fenced = True
        gm = s.pe(lambda e, r: e.matmul(Y.ap[:, 0:NB], c["avg4"][:], s.gmv[:, :, 0], start=True, stop=True),
                  o, *Y.free)
        mean = s.dve(lambda e, r: e.tensor_copy(g["mean"][:], Y.ap[:, 0:NB]), gm)
        Y.free = [mean]
        o = s.dve(lambda e, r: e.tensor_tensor(g["dev"][:], s.gmv[:, :, 0], g["mean"][:], ALU.subtract), mean)
        o = s.dve(lambda e, r: e.tensor_tensor(g["dev"][:], g["dev"][:], g["dev"][:], ALU.mult), o)
        o = s.dve(lambda e, r: e.tensor_tensor(g["vv"][:], g["dev"][:], s.gmv[:, :, 1], ALU.add), o)
        gv = s.pe(lambda e, r: e.matmul(Y.ap[:, 0:NB], c["avg4"][:], g["vv"][:], start=True, stop=True),
                  o, *Y.free)
        o = s.dve(lambda e, r: e.tensor_scalar(g["ve"][:], Y.ap[:, 0:NB], EPS, None, ALU.add), gv)
        Y.free = [o]
        o = s.pool(lambda e, r: e.tensor_tensor(g["r"][:], g["ve"][:], w["half_neg"][:, 0:NB], ALU.pow), o)
        s.step()
        sc = s.dve(lambda e, r: e.tensor_scalar(g["sc"][:], g["r"][:], c["a0_gnw"][:], None, ALU.mult), o)
        o = s.dve(lambda e, r: e.tensor_tensor(g["t"][:], g["mean"][:], g["sc"][:], ALU.mult), sc)
        o = s.dve(lambda e, r: e.tensor_scalar(g["bi"][:], g["t"][:], -1.0, c["a0_gnb"][:], ALU.mult,
                                               ALU.add), o)
        for b in range(NB):
            cn = s.act(lambda e, r, b=b: e.activation(s.ctxn[:, b * 256:(b + 1) * 256],
                                                      M.ap[:, b * 256:(b + 1) * 256], ACT.Identity,
                                                      bias=g["bi"][:, b:b + 1], scale=g["sc"][:, b:b + 1]),
                       o, *s.last("tensor"))
        M.free = [cn]
        for t in range(T):
            o = s.pe(lambda e, r, t=t: e.matmul(H0.ap[:, t * D:(t + 1) * D], s.ctxn[:, t * P:(t + 1) * P],
                                                c["a0_wo"][:], start=True, stop=True), cn, *H0.free)
        res = s.dve(lambda e, r: e.tensor_tensor(flat(x), H0.ap[:], flat(s.x_bias), ALU.add), o, xb)
        H0.free = [res]
        s.step()
        s.marks.append(("end" + str(len(s.marks)), res))
        return res

    def ffn1(x, x_ready, x_out, x_out_free):
        xt_ready, _ = norm(x, x_ready, 1.0 + EPS, EPS * EPS, s.xt_free)
        lg = logits(c["f1_gate"], xt_ready)
        k = s.small
        cp = s.dve(lambda e, r: e.tensor_copy(k["lg"][:], M.ap[:, 0:T * E].rearrange("p (t e) -> p t e", e=E)),
                   lg)
        M.free = [cp]
        mk = first_best(k["lg"][:], cp, "m1", "i1", None, s.mask[:])
        mb = M.ap[:].bitcast(BF16)
        hs = []
        for j, B in enumerate((H0, H1)):
            m = s.pe(lambda e, r, j=j, B=B: e.matmul(B.ap[:], w["f1_w1s"][:, j * P:(j + 1) * P], s.xt[:],
                                                     start=True, stop=True), xt_ready, *B.free)
            ga = s.act(lambda e, r, j=j, B=B: e.activation(s.ffn["gs"][j][:], B.ap[:], ACT.Gelu,
                                                           bias=w["f1_b1s"][:, j:j + 1]), m,
                       *s.use["gs", j])
            B.free = [ga]
            hs.append(ga)
        s.xt_free = [m]
        s.step()
        for t in range(T):
            o = s.pe(lambda e, r, t=t: e.transpose(mb[0:E, t * P:(t + 1) * P], s.mask[:, t, :], ident_b[:]),
                     mk, *M.free)
        mt = s.act(lambda e, r: e.copy(s.maskt[:], mb[0:E, 0:N]), o, *s.maskt_free)
        M.free = [mt]
        s.step()
        gm = []
        for j in range(2):
            o = s.pe(lambda e, r, j=j: e.matmul(M.ap[:], c["sel1"][:, j, :], s.maskt[:], start=True,
                                                stop=True), mt, *M.free)
            o = s.dve(lambda e, r, j=j: e.tensor_tensor(s.ffn["am"][j][:], s.ffn["gs"][j][:], M.ap[:], ALU.mult), o, hs[j],
                      *s.use["am", j])
            M.free = [o]
            s.use["gs", j] = [o]
            gm.append(o)
        s.step()
        first = True
        for t in range(T):
            for j in range(2):
                o = s.pe(lambda e, r, t=t, j=j, first=first: e.matmul(
                    Y.ap[:, t * D:(t + 1) * D], s.ffn["am"][j][:, t * P:(t + 1) * P], c["f1_w2"][:, j, :],
                    start=first, stop=False, skip_group_check=True), gm[j], *Y.free)
                first = False
            for j in range(3):
                o = s.pe(lambda e, r, t=t, j=j: e.matmul(
                    Y.ap[:, t * D:(t + 1) * D], s.maskt[:, t * P:(t + 1) * P], w["f1_b2p"][:, j, :],
                    start=False, stop=(t == T - 1 and j == 2), skip_group_check=True), mt)
        s.use["am", 0] = [o]
        s.use["am", 1] = [o]
        s.maskt_free = [o]
        res = s.dve(lambda e, r: e.scalar_tensor_tensor(flat(x_out), Y.ap[:], 0.5, flat(x), ALU.mult,
                                                        ALU.add), o, *x_out_free)
        Y.free = [res]
        s.step()
        s.marks.append(("end" + str(len(s.marks)), res))
        return res

    s.maskt_free = s.last("tensor")

    def attn1(x, x_ready):
        xt_ready, tr = norm(x, x_ready, 1.0 + RMS_EPS, EPS * RMS_EPS, s.xt_free)
        G = 3 * NH1
        ring = [H0, H1, M]
        turn = [0]

        def take():
            turn[0] += 1
            return ring[turn[0] % 3]

        xb = s.pool(lambda e, r: e.tensor_tensor(s.x_bias[:], x[:], c["a1_ob"][:].unsqueeze(1)
                                                 .broadcast_to([P, T, D]), ALU.add), x_ready, tr)
        B = take()
        for t in range(T):
            o = s.pe(lambda e, r, t=t, B=B: e.matmul(B.ap[:, t * G:(t + 1) * G], s.xt[:, t * P:(t + 1) * P],
                                                     w["a1_wg"][:], start=True, stop=True), xt_ready, *B.free)
        z = s.dve(lambda e, r, B=B: e.tensor_tensor(
            s.z[:], B.ap[:, 0:T * G].rearrange("p (t g) -> p t g", t=T),
            c["a1_bg"][:].unsqueeze(1).broadcast_to([P, T, G]), ALU.add), o)
        B.free = [z]
        o = s.dve(lambda e, r: e.tensor_scalar(s.zc[:], s.z[:], Z_LEAST, None, ALU.max), z)
        o = s.act(lambda e, r: e.activation(s.ez[:], s.zc[:], ACT.Exp, scale=-1.0), o)
        e1 = s.dve(lambda e, r: e.tensor_scalar(s.e1[:], s.ez[:], 1.0, None, ALU.add), o)
        lnf = s.act(lambda e, r: e.activation(s.lnf[:], s.e1[:, :, 0:NH1], ACT.Ln), e1)
        gio = s.dve(lambda e, r: e.reciprocal(s.gio[:], s.e1[:, :, NH1:G]), e1)
        s.step()
        for t in range(T):
            B = take()
            o = s.pe(lambda e, r, t=t, B=B: e.matmul(B.ap[:, 0:3 * D], s.xt[:, t * P:(t + 1) * P],
                                                     w["a1_wqkv"][:], start=True, stop=True), xt_ready, *B.free)
            qk = s.act(lambda e, r, t=t, B=B: e.copy(s.qk[:, t, :], B.ap[:, 0:2 * D]), o, *s.last("vector"))
            v = s.act(lambda e, r, t=t, B=B: e.copy(s.v[:, t, :], B.ap[:, 2 * D:3 * D]), *s.last("tensor"))
            B.free = [v]
        s.xt_free = [o]
        s.step()
        NHH = 2 * NH1
        hd = DH1 // 2

        def heads(tl):
            return tl[:].rearrange("p t (h d) -> p t h d", h=NHH)

        cosb = c["cos"][:].unsqueeze(2).broadcast_to([P, T, NHH, DH1])
        o1 = s.dve(lambda e, r: e.tensor_tensor(heads(s.rc), heads(s.qk), cosb, ALU.mult), qk)
        for hh in range(2):
            sinb = c["sin"][:, :, hh * hd:(hh + 1) * hd].unsqueeze(2).broadcast_to([P, T, NHH, hd])
            o2 = s.dve(lambda e, r, hh=hh, sinb=sinb: e.tensor_tensor(
                heads(s.rs)[:, :, :, hh * hd:(hh + 1) * hd],
                heads(s.qk)[:, :, :, (1 - hh) * hd:(2 - hh) * hd], sinb, ALU.mult), qk)
        ks = s.dve(lambda e, r: e.tensor_tensor(s.rc[:, :, D:2 * D], s.rc[:, :, D:2 * D],
                                                s.rs[:, :, D:2 * D], ALU.add), o2)
        qps = []
        for par in range(2):
            def view(tl, par=par):
                return tl[:, :, 0:D].rearrange("p t (g h d) -> p t g h d", h=2, d=DH1)[:, :, :, par, :]
            qps.append(s.dve(lambda e, r, par=par, view=view: e.tensor_tensor(
                view(s.qpar[par]), view(s.rc), view(s.rs), ALU.add), o2, *s.last("tensor")))
        s.step()
        B = take()
        NL = T * NH1
        o = s.pe(lambda e, r, B=B: e.matmul(B.ap[:, 0:NL], c["tri"][:], s.lnf[:].rearrange("p t h -> p (t h)"),
                                            start=True, stop=True), lnf, *B.free)
        o = s.pe(lambda e, r, B=B: e.matmul(B.ap[:, NL:2 * NL], c["ones"][:],
                                            s.lnf[:].rearrange("p t h -> p (t h)"), start=True, stop=True))
        lc = s.dve(lambda e, r, B=B: e.tensor_copy(s.lc[:].rearrange("p t h -> p (t h)"), B.ap[:, 0:NL]), o)
        lr = s.dve(lambda e, r, B=B: e.tensor_tensor(s.lrest[:].rearrange("p t h -> p (t h)"),
                                                     B.ap[:, NL:2 * NL],
                                                     s.lc[:].rearrange("p t h -> p (t h)"),
                                                     ALU.subtract), lc)
        B.free = [lr]
        ec = s.act(lambda e, r: e.activation(s.ec[:], s.lc[:], ACT.Exp, scale=-1.0), lc)
        es = s.act(lambda e, r: e.activation(s.es[:], s.lrest[:], ACT.Exp, scale=-1.0), lr)
        parts = bf16_parts(s.lc[:], lc, s.lc3, s.last("tensor"))
        def hv(ap):
            return ap.rearrange("p t (h d) -> p t h d", h=NH1)
        kg = s.dve(lambda e, r: e.tensor_tensor(hv(s.kg[:]), hv(s.rc[:, :, D:2 * D]),
                                                s.gio[:, :, 0:NH1].unsqueeze(3)
                                                .broadcast_to([P, T, NH1, DH1]), ALU.mult),
                   ks, gio, *s.last("tensor"))
        kgs = s.dve(lambda e, r: e.tensor_tensor(
            hv(s.kgs[:]), hv(s.kg[:, 0:T:2, :]), s.es[:, 0:T:2, :].unsqueeze(3)
            .broadcast_to([P, NB, NH1, DH1]), ALU.mult), kg, es, *s.last("tensor"))
        for par in range(2):
            def view(tl, par=par):
                return tl.rearrange("p t (g h d) -> p t g h d", h=2, d=DH1)[:, :, :, par, :]
            ecv = s.ec[:, 1:T:2, :].rearrange("p t (g h) -> p t g h", h=2)[:, :, :, par]
            qd = s.dve(lambda e, r, par=par, view=view, ecv=ecv: e.tensor_tensor(
                view(s.qd[:]), view(s.qpar[par][:, 1:T:2, :]),
                ecv.unsqueeze(3).broadcast_to([P, NB, NH1 // 2, DH1]), ALU.mult), qps[1], ec,
                *s.last("tensor"))
        s.step()
        tgt = [(s.kg, s.kt, kg, T), (s.qpar[0], s.qpt[0], qps[0], T), (s.qpar[1], s.qpt[1], qps[1], T)]
        got = []
        for src, dst, ready, n in tgt:
            B = take()
            for t in range(n):
                o = s.pe(lambda e, r, t=t, src=src, B=B: e.transpose(B.ap[:, t * P:(t + 1) * P], src[:, t, :],
                                                                     ident[:]), ready, *B.free)
            cp = s.act(lambda e, r, dst=dst, B=B: e.copy(dst[:], B.ap[:]), o, *s.last("tensor"))
            B.free = [cp]
            got.append(cp)
        B = take()
        for j in range(NB):
            o = s.pe(lambda e, r, j=j, B=B: e.transpose(B.ap[:, j * P:(j + 1) * P], s.qd[:, j, :], ident[:]),
                     qd, *B.free)
        qdt = s.act(lambda e, r, B=B: e.copy(s.qdt[:].rearrange("p b n -> p (b n)"), B.ap[:, 0:NB * P]), o,
                    *s.last("tensor"))
        B.free = [qdt]
        B = take()
        bb = B.ap[:].bitcast(BF16)
        for t in range(T):
            o = s.pe(lambda e, r, t=t, bb=bb: e.transpose(bb[0:3 * NH1, t * P:(t + 1) * P],
                                                          s.lc3[:, t, :, :].rearrange("p k e -> p (k e)"),
                                                          ident_b[:]), parts, *B.free)
        lct = s.act(lambda e, r, bb=bb: e.copy(s.lct3[:], bb[0:3 * NH1, 0:N]), o, *s.last("tensor"))
        B.free = [lct]
        s.step()
        B = take()
        for b in range(NB):
            o = s.pe(lambda e, r, b=b, B=B: e.matmul(B.ap[:, b * D:(b + 1) * D], s.kgs[:, b, :],
                                                     s.v[:, b * BATCH_TILES, :], start=True, stop=True),
                     kgs, v, *B.free)
        st = s.dve(lambda e, r, B=B: e.tensor_tensor(s.st[:], B.ap[:, 0:NB * D]
                                                     .rearrange("p (b d) -> p b d", b=NB),
                                                     c["blk16"][:].unsqueeze(1).broadcast_to([P, NB, D]),
                                                     ALU.mult), o, *s.last("tensor"))
        B.free = [st]
        for b in range(NB):
            t = b * BATCH_TILES + 1
            o = s.pe(lambda e, r, b=b, t=t: e.matmul(Y.ap[:, t * D:(t + 1) * D], s.qdt[:, b, :], s.st[:, b, :],
                                                     start=(b == 0), stop=False, skip_group_check=True),
                     st, qdt, *Y.free)
        s.step()
        dec_free = [s.last("tensor", "vector"), s.last("tensor", "vector")]
        att_free = [s.last("tensor"), s.last("tensor")]

        def pv(h, ready):
            for t in range(T):
                o = s.pe(lambda e, r, t=t, h=h: e.matmul(
                    Y.ap[:, t * D + h * DH1:t * D + (h + 1) * DH1], s.att[h % 2][:, t * P:(t + 1) * P],
                    s.v[:, t, h * DH1:(h + 1) * DH1], start=False,
                    stop=(h == NH1 - 1 and t == T - 1), skip_group_check=True), ready)
            att_free[h % 2] = [o]
            return o

        s.marks.append(("heads" + str(len(s.marks)), st))
        pend = None
        for h in range(NH1):
            strip, par = 32 * (h // 2), h % 2
            B = take()
            s.pe(lambda e, r, h=h, B=B: e.matmul(B.ap[:], c["sel"][:, h, :], s.lct3[:], start=True, stop=False,
                                                 skip_group_check=True), lct, *B.free)
            for t in range(T):
                s.pe(lambda e, r, h=h, t=t, B=B: e.matmul(B.ap[:, t * P:(t + 1) * P],
                                                          s.lct3[:, t * P:(t + 1) * P], c["nsel"][:, h, :],
                                                          start=False, stop=False, skip_group_check=True))
            o = s.pe(lambda e, r, B=B: e.matmul(B.ap[:], ident_b[:], c["later"][:].unsqueeze(1)
                                                .broadcast_to([P, T, P]), start=False, stop=True,
                                                skip_group_check=True))
            de = s.act(lambda e, r, h=h, B=B: e.activation(s.dec[h % 2][:], B.ap[:], ACT.Exp, scale=-1.0), o,
                       *dec_free[h % 2])
            B.free = [de]
            B = take()
            for t in range(T):
                sl = slice(t * P, (t + 1) * P)
                o = s.pe(lambda e, r, sl=sl, strip=strip, par=par, B=B: e.matmul(
                    B.ap[:, sl], s.kt[strip:strip + 32, sl], s.qpt[par][strip:strip + 32, sl], start=True,
                    stop=True), *got, *B.free)
            at = s.dve(lambda e, r, h=h, B=B: e.tensor_tensor(s.att[h % 2][:], s.dec[h % 2][:], B.ap[:],
                                                              ALU.mult), o, de, *att_free[h % 2])
            B.free = [at]
            dec_free[h % 2] = [at]
            if pend:
                pv(*pend)
            pend = (h, at)
            s.step()
        o = pv(*pend)
        yo = s.dve(lambda e, r: e.tensor_tensor(hv(s.yo[:]), Y.ap[:].rearrange("p (t h d) -> p t h d", t=T, h=NH1),
                                               s.gio[:, :, NH1:2 * NH1].unsqueeze(3)
                                               .broadcast_to([P, T, NH1, DH1]), ALU.mult), o,
                  *s.last("tensor"))
        Y.free = [yo]
        B = take()
        for t in range(T):
            o = s.pe(lambda e, r, t=t, B=B: e.transpose(B.ap[:, t * P:(t + 1) * P], s.yo[:, t, :], ident[:]),
                     yo, *B.free)
        yt = s.act(lambda e, r, B=B: e.activation(s.yot[:], B.ap[:], ACT.Copy, scale=float(DH1) ** -0.5), o,
                   *s.last("tensor"))
        B.free = [yt]
        s.step()
        B = take()
        for t in range(T):
            o = s.pe(lambda e, r, t=t, B=B: e.matmul(B.ap[:, t * D:(t + 1) * D], s.yot[:, t * P:(t + 1) * P],
                                                     c["a1_wo"][:], start=True, stop=True), yt, *B.free)
        res = s.dve(lambda e, r, B=B: e.tensor_tensor(flat(x), B.ap[:], flat(s.x_bias), ALU.add), o, xb)
        B.free = [res]
        s.step()
        s.marks.append(("end" + str(len(s.marks)), res))
        return res

    s.marks = []
    r_ = ffn0(s.x_load, loaded, s.x, s.last("vector", "gpsimd"))
    r_ = attn0(s.x, r_)
    r_ = ffn0(s.x, r_, s.x, [])
    r_ = ffn1(s.x, r_, s.x, [])
    r_ = attn1(s.x, r_)

    s.dve(lambda e, r: e.wait_ge(s.store_sem, r * 16 + 1)).own_semaphore = True
    r_ = ffn1(s.x, r_, s.x_store, [])
    s.act(lambda e, r: e.dma_start(out_v[r * 2 + s.index], s.x_store[:]).then_inc(s.store_sem, 16),
          r_).own_semaphore = True


def constants():
    k = {}
    k["ident"] = np.eye(P, dtype=np.float32)
    k["w8"] = np.tile(np.arange(E, 0, -1, dtype=np.float32), (P, 1))
    sel = np.zeros((3 * E, E, P), np.float32)
    for e in range(E):
        sel[[e, E + e, 2 * E + e], e, :] = 1
    k["sel"] = sel
    sel1 = np.zeros((E, 2, P), np.float32)
    for e in range(E):
        sel1[e, e // 4, (e % 4) * 32:(e % 4) * 32 + 32] = 1
    k["sel1"] = sel1
    i = np.arange(P)
    k["blk4"] = (i[:, None] // 4 == i[None] // 4).astype(np.float32)
    k["avg4"] = k["blk4"] * np.float32(0.25)
    k["blk16"] = (i[:, None] // 16 == i[None] // 16).astype(np.float32)
    k["tri"] = (i[:, None] <= i[None]).astype(np.float32)
    k["ones"] = np.ones((P, P), np.float32)
    k["later"] = (i[:, None] > i[None]).astype(np.float32) * np.float32(30000.0)
    half = DH1 // 2
    inv = (np.float32(1.0) / np.float32(10000.0) ** (np.arange(half, dtype=np.float32) / np.float32(half)))
    pos = (np.arange(T) % BATCH_TILES)[None] * P + i[:, None]
    ang = pos[:, :, None].astype(np.float32) * inv.astype(np.float32)
    cos, sin = np.cos(ang).astype(np.float32), np.sin(ang).astype(np.float32)
    k["cos"] = np.concatenate([cos, cos], -1)
    k["sin"] = np.concatenate([-sin, sin], -1)
    return k


def kernel(**inputs):
    import concourse.bacc as _bacc
    from concourse.bass_utils import run_bass_kernel_spmd as _run

    a = {k: np.asarray(v) for k, v in inputs.items()}
    f0, f1, a0, a1 = "L0_ffn_", "L1_ffn_", "L0_attn_", "L1_attn_"
    x = a[a0 + "x"]

    def rows(v):
        return np.tile(v[None], (P, 1))

    def w13(w, sw):
        v = np.concatenate([w, sw[None]], 0).reshape(NE, F, 2, D)
        return v.transpose(3, 0, 2, 1)

    def b13(b, sb_):
        return np.concatenate([b, sb_[None]], 0).reshape(NE, F, 2).transpose(1, 0, 2)

    lay = {}
    w1v, w3v = w13(a[f0 + "w1"], a[f0 + "sw1"]), w13(a[f0 + "w3"], a[f0 + "sw3"])
    lay["w13"] = np.stack([w3v[:, :, 0], w1v[:, :, 0], w3v[:, :, 1], w1v[:, :, 1]], 2)
    b1v, b3v = b13(a[f0 + "b1"], a[f0 + "sb1"]), b13(a[f0 + "b3"], a[f0 + "sb3"])
    lay["b13"] = np.stack([b3v[:, :, 0], b1v[:, :, 0], b3v[:, :, 1], b1v[:, :, 1]], 2)
    lay["w2"] = np.concatenate([a[f0 + "w2"], a[f0 + "sw2"][None]], 0).transpose(2, 0, 1)
    lay["b2s"] = np.concatenate([a[f0 + "b2"], a[f0 + "sb2"][None]], 0)
    lay["gate"] = a[f0 + "gate_w"].T
    lay["gate_b"] = rows(a[f0 + "gate_b"])
    wqkv, bqkv = a[a0 + "Wqkv_w"], a[a0 + "Wqkv_b"]
    lay["a0_wq"] = wqkv[0:D].T
    lay["a0_wkv"] = wqkv[D:].T
    lay["a0_bq"] = bqkv[0:D, None]
    lay["a0_bkv"] = rows(bqkv[D:])
    lay["a0_gnw"] = a[a0 + "gn_w"][:, None]
    lay["a0_gnb"] = a[a0 + "gn_b"][:, None]
    lay["a0_wo"] = a[a0 + "out_w"].T
    lay["a0_ob"] = rows(a[a0 + "out_b"])
    lay["f1_gate"] = a[f1 + "Wg"].T
    lay["f1_lns"] = a[f1 + "ln_scale"].T
    lay["f1_lnb"] = a[f1 + "ln_bias"].T
    lay["f1_w1"] = a[f1 + "W1"].transpose(1, 0, 2).reshape(D, E * 32)
    lay["f1_b1"] = a[f1 + "b1"].reshape(2, P).T
    lay["f1_w2"] = a[f1 + "W2"].reshape(2, P, D).transpose(1, 0, 2)
    lay["f1_b2"] = a[f1 + "b2"]
    lay["a1_nw"] = a[a1 + "norm_w"][:, None]
    lay["a1_wqkv"] = np.concatenate([a[a1 + "Wq"], a[a1 + "Wk"], a[a1 + "Wv"]], 0).T
    lay["a1_wg"] = np.concatenate([a[a1 + "Wbeta"], a[a1 + "Wig"], a[a1 + "Wog"]], 0).T
    lay["a1_bg"] = rows(np.concatenate([a[a1 + "bbeta"], a[a1 + "big"], a[a1 + "bog"]], 0))
    lay["a1_wo"] = a[a1 + "Wout"].T
    lay["a1_ob"] = rows(a[a1 + "bout"])
    lay.update(constants())
    lay = {k: np.ascontiguousarray(v) for k, v in lay.items()}

    nc = _bacc.Bacc("TRN2", target_bir_lowering=False, num_devices=1)
    arrays = {"in_" + k: v for k, v in lay.items()}
    dram = {k: nc.dram_tensor("in_" + k, v.shape, mybir.dt.from_np(v.dtype), kind="ExternalInput").ap()
            for k, v in lay.items()}
    arrays["x_dram"] = np.ascontiguousarray(x.reshape(-1, D))
    x_in = nc.dram_tensor("x_dram", arrays["x_dram"].shape, F32, kind="ExternalInput").ap()
    out = nc.dram_tensor("out_dram", arrays["x_dram"].shape, F32, kind="ExternalOutput").ap()
    build(nc, dram, x_in, out)
    r = _run(nc, [arrays], core_ids=[0])
    return r.results[0]["out_dram"].reshape(x.shape)
```

```python
from contextlib import ExitStack

import numpy as np

import concourse.bass as bass
from concourse import mybir

F32 = mybir.dt.float32
BF16 = mybir.dt.bfloat16
F16 = mybir.dt.float16
I32 = mybir.dt.int32
ALU = mybir.AluOpType
ACT = mybir.ActivationFunctionType
AX = mybir.AxisListType

P = 128
D = 128
T = 4
N = T * P
BATCH_TILES = 2
NB = T // BATCH_TILES
ROUND = 120.0
OFFSETS = dict(head=0.56, middle=1.38, tail=1.94)
GAIN = 0.0024
BIAS = dict(head=-17.8, middle=-2.5, tail=-13.4)
E = 8
NE = E + 1
F = 128
LIMIT, ALPHA = 7.0, 1.702
NH1, DH1 = 8, 16
EPS = 1e-5
RMS_EPS = 1e-6
NM = 4 * NE + 1
X_SCALE = 1024.0
W_TOP = 2.0 ** 14
W_LEAST = 2.0 ** -40
Z_LEAST = -43.0


SETUP_STEPS = 20


class Op:

    def __init__(self, lane, engine, emit, waits):
        self.lane, self.engine, self.emit, self.waits = lane, engine, emit, waits
        self.needed, self.ordinal = False, None
        self.took = None
        self.behind = None
        self.on = None
        self.fenced = False
        self.own_semaphore = False


class LastRound:

    def __init__(self, lane, engine):
        self.lane, self.engine = lane, engine


class Earlier:

    def __init__(self, op):
        op.needed = True
        self.op, self.lane, self.engine = op, op.lane, op.engine


ENGINES = ("sync", "tensor", "vector", "scalar", "gpsimd")


DRIP = ("tensor", "vector", "scalar")


class Lane:

    def __init__(self, name):
        self.name, self.offset, self.steps = name, OFFSETS[name], [[]]
        self.between = []

    def step(self):
        self.steps.append([])

    def put(self, engine, emit, *waits):
        op = Op(self.name, engine, emit, [w for w in waits if w is not None])
        for w in op.waits:
            if isinstance(w, Op):
                w.needed = True
        self.steps[-1].append(op)
        if self.between and engine in DRIP:
            self.steps[-1].append(self.between.pop(0))
        return op

    def pe(self, emit, *waits):
        return self.put("tensor", emit, *waits)

    def dve(self, emit, *waits):
        return self.put("vector", emit, *waits)

    def act(self, emit, *waits):
        return self.put("scalar", emit, *waits)

    def pool(self, emit, *waits):
        return self.put("gpsimd", emit, *waits)

    def sp(self, emit, *waits):
        return self.put("sync", emit, *waits)

    def last(self, *engines):
        return [LastRound(self.name, e) for e in engines]


class Estimate:

    @staticmethod
    def columns(ap):
        n = 1
        for k in ap.shape[1:]:
            n *= k
        return n

    def matmul(self, out, lhsT, rhs, **_):
        passes = 4 if rhs.dtype == F32 else 1
        if lhsT.shape[1] == 32:
            return 0.07
        return max(passes * self.columns(out) / 2400, 0.03 * passes)

    def transpose(self, out, in_, identity):
        return (2 if in_.dtype == F32 else 1) * P / 2400

    def two_inputs(self, out, *_, **__):
        return 0.09 + self.columns(out) / 960

    tensor_tensor = scalar_tensor_tensor = two_inputs

    def tensor_copy(self, out, in_):
        return 0.07 + self.columns(out) / 1920

    def tensor_scalar(self, out, in_, scalar, *_):
        return 0.07 + self.columns(out) / (1920 if isinstance(scalar, float) else 700)

    def reduction(self, out, in_, *_):
        return 0.07 + self.columns(in_) / 960

    tensor_reduce = bn_stats = bn_aggr = reciprocal = reduction

    def activation(self, out, in_, func, **kw):
        self.table = TABLES.get(func)
        scaled = 0.0 if isinstance(kw.get("scale", 1.0), float) else 0.1
        return 0.1 + scaled + self.columns(out) / 1200

    def copy(self, out, in_):
        return 0.06 + self.columns(out) / 1200

    def dma_start(self, *_):
        return 2.0


TABLES = {ACT.Gelu_apprx_sigmoid: 1, ACT.Exp: 2, ACT.Ln: 2, ACT.Gelu: 3}
TABLE_LOAD = 1.3
HOPS = {"tensor": 0.2, "vector": 0.13, "scalar": 0.2, "gpsimd": 0.2, "sync": 0.0}


def hop(w, op):
    return HOPS[w.engine] + (0.1 if op.engine == "tensor" else 0.0)


def estimate(op):
    e = Estimate()
    e.table = None
    if op.own_semaphore:
        return 0.0, None
    t = op.emit(e, 0)
    return (t + 0.7 if op.engine == "gpsimd" else t), e.table


def cut(lanes):
    for lane in lanes:
        ops = lane.all = [op for step in lane.steps for op in step]
        for op in ops:
            op.on, op.behind = None, 0
        _, starts, _ = play([ops], 5)
        index = {op: i for i, op in enumerate(ops)}
        inside = set()
        for use in lane.uses:
            first = min(index[op] for op in ops if use in op.waits)
            inside.update(range(first + 1, max(index[op] for op in use.free) + 1))
            for op in use.free:
                op.needed = True
        left = (int(lane.offset) + 1 - lane.offset) * ROUND
        at = next((i for i, op in enumerate(ops) if i not in inside and starts[op] >= left), len(ops))
        for i, op in enumerate(ops):
            op.behind = int(lane.offset) + (i >= at)
        lane.ops = ops[at:] + ops[:at]
    finals = {(lane.name, e): [op for op in lane.all if op.engine == e and not op.own_semaphore][-1:]
              for lane in lanes for e in ENGINES}
    for lane in lanes:
        for op in lane.ops:
            op.on = []
            for w in op.waits:
                if isinstance(w, Op):
                    op.on.append((w, 0))
                elif isinstance(w, Earlier):
                    op.on.append((w.op, 1))
                elif isinstance(w, LastRound):
                    op.on.extend((f, 1) for f in finals[w.lane, w.engine])
            assert all(w.behind <= op.behind + back for w, back in op.on)


def play(lanes, banks):
    queues = [{e: [op for op in lane if op.engine == e] for e in ENGINES} for lane in lanes]
    inside = {op for lane in lanes for op in lane}
    needs, rest, at = {}, {}, [dict.fromkeys(ENGINES, 0) for _ in lanes]
    wants = {}
    for op in inside:
        if op.took is None:
            op.took = estimate(op)
        if op.on is None:
            needs[op] = [w for w in op.waits if isinstance(w, Op) and w in inside]
        else:
            needs[op] = [w for w, back in op.on if w in inside and w.behind == op.behind + back]
        wants[op] = [w for w in op.waits if isinstance(w, BankUse)]
    chained = {}
    for lane in lanes:
        after = {}
        for op in reversed(lane):
            rest[op] = op.took[0] + max(chained.get(op, 0.0), after.get(op.engine, 0.0))
            after[op.engine] = rest[op]
            for w in needs[op]:
                chained[w] = max(chained.get(w, 0.0), rest[op] + hop(w, op))
    free = dict.fromkeys(ENGINES, 0.0)
    end, order, starts, ready_at, placed = {}, [], {}, {}, {}
    uses = [[] for _ in range(banks)]
    table = None
    while len(order) < len(inside):
        able = []
        bank_free, bank = min(((max([0.0] + [end[w] + HOPS[w.engine] for use in u[-1:] for w in use.free]), k)
                               for k, u in enumerate(uses)
                               if all(w in end for use in u[-1:] for w in use.free)), default=(0.0, None))
        for n, q in enumerate(queues):
            for e in ENGINES:
                if at[n][e] == len(q[e]):
                    continue
                op = q[e][at[n][e]]
                if op not in ready_at:
                    if any(w not in end for w in needs[op]):
                        continue
                    ready_at[op] = max([0.0] + [end[w] + hop(w, op) for w in needs[op]])
                start = max(ready_at[op], free[e])
                if any(use not in placed for use in wants[op]):
                    if bank is None:
                        continue
                    start = max(start, bank_free)
                if op.took[1] and op.took[1] != table:
                    start += TABLE_LOAD
                able.append((start, n, op))
        start, n, op = min(able, key=lambda a: a[0] - GAIN * (rest[a[2]] + BIAS[a[2].lane]))
        for use in wants[op]:
            if use not in placed:
                placed[use] = bank
                uses[bank].append(use)
        at[n][op.engine] += 1
        starts[op] = start
        end[op] = free[op.engine] = start + op.took[0]
        table = op.took[1] or table
        order.append(op)
    return order, starts, uses


def place(uses, banks=None):
    for k, of_bank in enumerate(uses):
        for i, use in enumerate(of_bank):
            n = len(of_bank)
            use.earlier = [(of_bank[(i - j) % n].free, int(i - j < 0)) for j in range(1, n + 1)]
            if banks:
                use.ap = banks[k]


class BankUse:

    def __init__(self, ap):
        self.ap, self.free, self.earlier = ap, [self], ()


class Buf:

    def __init__(self, ap, free):
        self.ap, self.free = ap, list(free)


def build(nc, dram, packed, x_in, out):
    chunks = x_in.shape[0] // N
    nc.disable_value_cache = True
    x_v = x_in.rearrange("(c t p) d -> c p t d", t=T, p=P)
    out_v = out.rearrange("(c t p) d -> c p t d", t=T, p=P)

    with ExitStack() as ctx:
        def sb(name, shape, dt=F32):
            return ctx.enter_context(nc.sbuf_tensor(name, shape, dt))

        const = {}
        staged = ("sel", "sel1", "later_gate", "w13")
        for name, ap in dram.items():
            if name not in staged:
                const[name] = sb("w_" + name, list(ap.shape), ap.dtype)
        at = 0
        for name, shape in packed:
            n = int(np.prod(shape[1:]))
            view = const["packed"][:, at:at + n]
            const[name] = view.rearrange("p (a b) -> p a b", b=shape[2]) if len(shape) == 3 else view
            at += n
        for name in ("sel", "nsel", "sel1", "later", "ident_b"):
            shape = {"ident_b": [P, P], "later": [P, P], "nsel": dram["sel"].shape}.get(name)
            const[name] = sb("w_" + name, list(shape or dram[name].shape), BF16)
        f1_w1s = sb("f1_w1s", [P, E * 32])
        f1_b1s = sb("f1_b1s", [P, 2])
        f1_b2p = sb("f1_b2p", [E, 3, D], BF16)
        f1_b2r = sb("f1_b2r", [E, 2, D])
        w_hi = sb("w_hi", [P, 4 * NE, F], F16)
        w_lo = sb("w_lo", [P, 4 * NE, F], F16)
        g_hi = sb("g_hi", [P, E], F16)
        g_lo = sb("g_lo", [P, E], F16)
        w_max = sb("w_max", [P, NM])
        w_maxt = sb("w_maxt", [NM, 4])
        w_diag = sb("w_diag", [NM, P])
        w_scale = sb("w_scale", [P, NM])
        w_back = sb("w_back", [P, NM])
        sc31 = sb("sc31", [P, NE, 2])
        b3s = sb("b3s", [P, NE, 2])
        b1s = sb("b1s", [P, NE, 2])
        inv_back = sb("inv_back", [P, NM])
        a1_wqkv = sb("a1_wqkv", [P, 3 * D])
        a1_wg = sb("a1_wg", [P, 3 * NH1])
        half_neg = sb("half_neg", [P, T])

        fence = ctx.enter_context(nc.semaphore("fence"))
        load_sem = ctx.enter_context(nc.semaphore("weights_loaded"))
        setup_dve = ctx.enter_context(nc.semaphore("setup_vector"))
        setup_pe = ctx.enter_context(nc.semaphore("setup_tensor"))
        n_loads = len(dram)

        lanes = [Lane(name) for name in ("head", "middle", "tail")]
        banks = [ctx.enter_context(nc.psum_tensor(f"bank{k}", [P, N], F32)) for k in range(8 - len(lanes))]
        for s in lanes:
            s.sems = {e: ctx.enter_context(nc.semaphore(f"{e}_{s.name}")) for e in ENGINES}
            s.sums = ctx.enter_context(nc.psum_tensor(f"sums_{s.name}", [P, N], F32))

            def tile(name, shape, dt=F32, s=s):
                return sb(f"{name}_{s.name}", shape, dt)
            s.x_in = tile("x_in", [P, T, D])
            s.x_out = tile("x_out", [P, T, D])
            s.xn = tile("xn", [P, T, D])
            s.stats = tile("stats", [P, T, 6])
            s.mv = tile("mv", [P, T, 2])
            s.ve = tile("ve", [P, T])
            s.rstd = tile("rstd", [P, T])
            s.small = {k: tile(k, [P, T, E]) for k in
                       ("lg", "ex", "sc", "bi", "ge", "oh1", "b2_", "oh2", "oh", "cw", "r1_", "r2_")}
            s.red = {k: tile(k, [P, T]) for k in ("mx", "sm", "rc", "m1", "i1", "m2", "i2")}
            arena = s.arena = tile("arena", [P, 12, N])

            def piece(i, n=1, t=None, arena=arena):
                ap = arena[:, i:i + n, :].rearrange("p a n -> p (a n)")
                return ap.rearrange("p (t d) -> p t d", t=t) if t else ap
            s.ffn = {k: [piece(i), piece(i + 1)] for k, i in
                     (("tg", 0), ("tl", 2), ("hg", 4), ("hl", 6), ("gs", 8), ("am", 10))}
            if s.name != "tail":
                s.xh = tile("xh", [P, N], F16)
                s.xl = tile("xl", [P, N], F16)
                s.cwb = [tile(f"cwb{i}", [P, N]) for i in range(2)]
                s.cw9 = tile("cw9", [P, T, NE])
                s.cw3 = tile("cw3", [P, T, 3, E], BF16)
                s.cwt = tile("cwt", [NE, N])
                s.cwt3 = tile("cwt3", [3 * E, N], BF16)
            s.xt = tile("xt", [P, N])
            s.x = tile("x", [P, T, D])
            if s.name != "middle":
                s.x_bias = tile("x_bias", [P, T, D])
            if s.name == "head":
                s.kv = piece(0, 2, T)
                s.qt = piece(2)
                s.kvm = tile("kvm", [P, NB, D])
                s.ctxn = piece(3)
                s.gn = {k: tile("gn_" + k, [P, NB]) for k in ("mean", "dev", "vv", "ve", "r", "sc", "t", "bi")}
                s.gst = tile("gst", [P, NB, 6])
                s.gmv = tile("gmv", [P, NB, 2])
            if s.name != "head":
                s.mask = tile("mask", [P, T, E], BF16)
                s.maskt = tile("maskt", [E, N], BF16)
            if s.name == "tail":
                for k in ("z", "zc", "ez", "e1"):
                    s.small[k] = tile(k, [P, T, 3 * NH1])
                s.z, s.zc, s.ez, s.e1 = (s.small[k] for k in ("z", "zc", "ez", "e1"))
                s.gio = tile("gio", [P, T, 2 * NH1])
                s.lnf = tile("lnf", [P, T, NH1])
                s.lc = tile("lc", [P, T, NH1])
                s.lrest = tile("lrest", [P, T, NH1])
                s.ec = tile("ec", [P, T, NH1])
                s.es = tile("es", [P, T, NH1])
                s.lc3 = tile("lc3", [P, T, 3, NH1], BF16)
                s.lct3 = tile("lct3", [3 * NH1, N], BF16)
                s.qk = piece(0, 2, T)
                s.v = piece(6, 1, T)
                s.rc = piece(2, 2, T)
                s.rs = piece(4, 2, T)
                s.qpar = [tile(f"qpar{i}", [P, T, D]) for i in range(2)]
                s.vpar = [tile(f"vpar{i}", [P, T, D]) for i in range(2)]
                s.kg = piece(7, 1, T)
                s.kgs = tile("kgs", [P, NB, D])
                s.qd = tile("qd", [P, NB, D])
                s.kt = piece(0)
                s.qpt = [piece(1), piece(4)]
                s.qdt = tile("qdt", [P, NB, P])
                s.st = tile("st", [P, NB, D])
                s.dec = [piece(8), piece(9)]
                s.att = [piece(10), piece(11)]
                s.yot = piece(5)
        head, middle, tail = lanes
        store_sem = ctx.enter_context(nc.semaphore("stored"))
        folded = dict(f1_w1s=f1_w1s, f1_b1s=f1_b1s, f1_b2p=f1_b2p, a1_wqkv=a1_wqkv, a1_wg=a1_wg,
                      half_neg=half_neg, w_hi=w_hi, w_lo=w_lo, g_hi=g_hi, g_lo=g_lo, w_back=w_back,
                      sc31=sc31, b3s=b3s, b1s=b1s)
        tail.previous_out, middle.previous_out = middle.x_out, head.x_out
        copied_t, tail_end = record(nc, tail, const, folded, x_v, out_v, store_sem, None)
        copied_m, middle_end = record(nc, middle, const, folded, x_v, out_v, store_sem, copied_t)
        _, head_end = record(nc, head, const, folded, x_v, out_v, store_sem, copied_m)
        for op, end in ((copied_t, middle_end), (copied_m, head_end)):
            op.waits.append(end)
            end.needed = True

        cut(lanes)
        depth = max(op.behind for s in lanes for op in s.ops) + 1
        order, _, uses = play([s.ops for s in lanes], len(banks))
        place(uses, banks)
        queues = {e: [op for op in order if op.engine == e] for e in ENGINES}
        totals = {}
        for s in lanes:
            for e in ENGINES:
                mine = [op for step in s.steps for op in step if op.engine == e]
                counted = [op for op in mine if not op.own_semaphore]
                if counted:
                    counted[-1].needed = True
                n = 0
                for op in mine:
                    if op.needed:
                        n += 1
                        op.ordinal = n
                totals[s.name, e] = n
        sems = {(s.name, e): s.sems[e] for s in lanes for e in ENGINES}

        def run(engine_name, eng):
            step = 16 if engine_name == "sync" else 1
            for s in lanes:
                eng.sem_inc(s.sems[engine_name], 1)
            if engine_name == "scalar":
                eng.sem_inc(store_sem, 1)

            def once(r, chosen):
                seen = {}
                base = {}

                def before(key, back):
                    if (key, back) not in base:
                        per_chunk = totals[key] * (16 if key[1] == "sync" else 1)
                        v = (r - back) * per_chunk + 1
                        base[key, back] = v if isinstance(v, int) else eng.snap(v)
                    return base[key, back]

                for op in queues[engine_name]:
                    if op.behind not in chosen:
                        continue
                    for w in op.waits:
                        if isinstance(w, BankUse):
                            ends = next([(o, o.behind + back) for o in free] for free, back in w.earlier
                                        if not isinstance(r, int) or free[0] is w.free[0]
                                        or 0 <= r - free[0].behind - back < chunks)
                        elif isinstance(w, Earlier):
                            ends = [(w.op, op.behind + 1)]
                        else:
                            ends = [(w, op.behind)]
                        for o, back in ends:
                            key = (o.lane, o.engine)
                            if isinstance(r, int) and r < back:
                                continue
                            k = 0 if isinstance(o, LastRound) else o.ordinal
                            if seen.get(key, (-9, 0)) >= (-back, k):
                                continue
                            seen[key] = (-back, k)
                            unit = 16 if o.engine == "sync" else 1
                            eng.wait_ge(sems[key], before(key, back) + k * unit)
                            if op.fenced:
                                eng.sem_inc(fence, 1)
                    ins = op.emit(eng, r - op.behind if op.behind else r)
                    if op.needed:
                        ins.then_inc(sems[op.lane, op.engine], step)

            for i in range(depth):
                once(i, range(i + 1))
            with eng.Fori(depth, chunks) as r:
                once(r, range(depth))
            for i in range(depth - 1):
                once(chunks + i, range(i + 1, depth))

        arena = head.arena
        stage = {
            "sel": arena[0:3 * E, 0:2, :].rearrange("p a (e n) -> p (a e) n", n=P),
            "sel1": arena[0:E, 2, 0:2 * P].rearrange("p (j n) -> p j n", j=2),
            "later": arena[:, 3, 0:P],
            "gate": arena[:, 3, P:P + E],
            "later_gate": arena[:, 3, 0:P + E],
            "w13": middle.arena[:, 0:9, :].rearrange("p a n -> p (a n)").rearrange("p (m n) -> p m n",
                                                                                    n=F),
        }

        def load(eng, names):
            for name in names:
                eng.dma_start(stage[name] if name in stage else const[name][:],
                              dram[name]).then_inc(load_sem, 16)

        block = ctx.enter_context(nc.Block())

        @block.sync
        def _(eng):
            load(eng, ("w13", "sel", "b2s"))
            run("sync", eng)

        @block.tensor
        def _(eng):
            eng.wait_ge(load_sem, 16 * n_loads)
            for j in range(2):
                for e in range(4):
                    col = (4 * j + e) * 32
                    ins = eng.matmul(banks[0][32 * e:32 * e + 32, j:j + 1],
                                     const["f1_w1"][:, col:col + 32],
                                     const["f1_lnb"][:, 4 * j + e:4 * j + e + 1], start=True, stop=True)
            ins.then_inc(setup_pe, 1)
            eng.wait_ge(setup_dve, 11)
            eng.transpose(banks[1][0:NM, 0:P], w_max[:], const["ident"][:]).then_inc(setup_pe, 1)
            eng.wait_ge(setup_dve, 14)
            eng.matmul(banks[2][:, 0:NM], w_diag[:], const["ident"][0:NM, 0:NM], start=True,
                       stop=True).then_inc(setup_pe, 1)
            eng.wait_ge(setup_dve, SETUP_STEPS)
            run("tensor", eng)

        @block.vector
        def _(eng):
            eng.memset(half_neg[:], -0.5).then_inc(setup_dve, 1)
            n = 1
            for s in (head, middle):
                eng.memset(s.cw9[:, :, E:NE], 1.0)
            for q in tail.qpar + tail.vpar:
                eng.memset(q[:], 0.0)
            eng.wait_ge(load_sem, 16 * n_loads)
            eng.tensor_tensor(f1_w1s[:].rearrange("p (e h) -> p e h", e=E),
                              const["f1_w1"][:].rearrange("p (e h) -> p e h", e=E),
                              const["f1_lns"][:].unsqueeze(2).broadcast_to([P, E, 32]),
                              ALU.mult).then_inc(setup_dve, 1)
            eng.tensor_scalar(a1_wqkv[:], const["a1_wqkv"][:], const["a1_nw"][:], None,
                              ALU.mult).then_inc(setup_dve, 1)
            eng.tensor_scalar(a1_wg[:], const["a1_wg"][:], const["a1_nw"][:], None,
                              ALU.mult).then_inc(setup_dve, 1)
            for name in ("sel", "sel1", "later"):
                eng.tensor_copy(const[name][:], stage[name])
            eng.tensor_copy(const["ident_b"][:], const["ident"][:])
            eng.tensor_scalar(const["nsel"][:], stage["sel"], -1.0, None, ALU.mult)
            n = 4
            eng.tensor_copy(f1_b2p[:, 0, :], const["f1_b2"][:]).then_inc(setup_dve, 1)
            for k in range(2):
                n += 1
                eng.wait_ge(setup_dve, n)
                src = const["f1_b2"][:] if k == 0 else f1_b2r[:, 0, :]
                eng.tensor_tensor(f1_b2r[:, k, :], src, f1_b2p[:, k, :], ALU.subtract).then_inc(setup_dve, 1)
                n += 1
                eng.wait_ge(setup_dve, n)
                eng.tensor_copy(f1_b2p[:, k + 1, :], f1_b2r[:, k, :]).then_inc(setup_dve, 1)
            n += 1
            assert n == 9
            eng.wait_ge(setup_pe, 1)
            eng.tensor_tensor(f1_b1s[:], banks[0][:, 0:2], const["f1_b1"][:],
                              ALU.add).then_inc(setup_dve, 1)
            n = 10

            def then(ins):
                nonlocal n
                ins.then_inc(setup_dve, 1)
                n += 1
                eng.wait_ge(setup_dve, n)

            w13 = stage["w13"]
            eng.tensor_reduce(w_max[:, 0:NM - 1], w13, AX.X, ALU.max, apply_absolute_value=True)
            then(eng.tensor_reduce(w_max[:, NM - 1:NM], stage["gate"], AX.X, ALU.max,
                                   apply_absolute_value=True))
            eng.wait_ge(setup_pe, 2)
            then(eng.tensor_reduce(w_maxt[:, 0:1], banks[1][0:NM, 0:P], AX.X, ALU.max))
            then(eng.tensor_scalar(w_maxt[:, 1:2].bitcast(I32), w_maxt[:, 0:1].bitcast(I32), 0x7F800000, None,
                                   ALU.bitwise_and))
            then(eng.tensor_scalar(w_diag[:], const["ones"][0:NM, :], w_maxt[:, 1:2], W_LEAST, ALU.mult,
                                   ALU.max))
            eng.wait_ge(setup_pe, 3)
            then(eng.tensor_scalar(w_back[:], banks[2][:, 0:NM], 1.0 / (W_TOP * X_SCALE), None,
                                   ALU.mult))
            then(eng.reciprocal(inv_back[:], w_back[:]))
            then(eng.tensor_scalar(w_scale[:], inv_back[:], 1.0 / X_SCALE, None, ALU.mult))
            def by_part(tl, k):
                return tl[:, 0:4 * NE].rearrange("p (e h k) -> p e h k", h=2, k=2)[:, :, :, k]
            def bias(k):
                return const["b13"][:].rearrange("p e (h k) -> p e h k", k=2)[:, :, :, k]
            eng.tensor_tensor(sc31[:], by_part(w_back, 0), by_part(w_back, 1), ALU.mult)
            eng.tensor_tensor(b3s[:], bias(0), by_part(w_back, 1), ALU.mult)
            eng.tensor_tensor(b1s[:], bias(1), by_part(inv_back, 1), ALU.mult)
            eng.tensor_scalar(stage["gate"], stage["gate"], w_scale[:, NM - 1:NM], None, ALU.mult)
            then(eng.tensor_tensor(w13, w13, w_scale[:, 0:NM - 1].unsqueeze(2).broadcast_to([P, NM - 1, F]),
                                   ALU.mult))
            eng.tensor_copy(g_hi[:], stage["gate"])
            then(eng.tensor_copy(w_hi[:], w13))
            eng.tensor_tensor(g_lo[:], stage["gate"], g_hi[:], ALU.subtract)
            then(eng.tensor_tensor(w_lo[:], w13, w_hi[:], ALU.subtract))
            assert n == SETUP_STEPS
            run("vector", eng)

        @block.scalar
        def _(eng):
            load(eng, ("later_gate", "packed", "sel1", "f1_b2"))
            eng.wait_ge(load_sem, 16 * n_loads)
            eng.wait_ge(setup_dve, SETUP_STEPS)
            run("scalar", eng)
            eng.wait_ge(store_sem, 16 * chunks + 1)

        @block.gpsimd
        def _(eng):
            eng.wait_ge(load_sem, 16 * n_loads)
            eng.wait_ge(setup_dve, SETUP_STEPS)
            run("gpsimd", eng)


def record(nc, s, c, w, x_v, out_v, store_sem, next_copied):
    ident, ident_b = c["ident"], c["ident_b"]
    prev = s.last("tensor", "vector", "scalar")
    Y = Buf(s.sums, prev)
    s.uses = []

    def take():
        use = BankUse(s.sums)
        s.uses.append(use)
        return use

    def bc(ap, shape):
        return ap.broadcast_to(shape)

    def flat(t):
        return t[:].rearrange("p t d -> p (t d)")

    def norm(x, x_ready, a, b, xt_free, split=False):
        for t in range(T):
            op = s.dve(lambda e, r, t=t: e.bn_stats(s.stats[:, t, :], x[:, t, :]), x_ready, *s.last("vector"))
        st = op
        for t in range(T):
            op = s.dve(lambda e, r, t=t: e.bn_aggr(s.mv[:, t, :], s.stats[:, t, :]), st)
            op.fenced = True
        ve = s.dve(lambda e, r: e.tensor_scalar(s.ve[:], s.mv[:, :, 1], a, b, ALU.mult, ALU.add), op)
        rs = s.pool(lambda e, r: e.tensor_tensor(s.rstd[:], s.ve[:], w["half_neg"][:], ALU.pow), ve)
        s.step()
        done = []
        for t in range(T):
            xn = s.dve(lambda e, r, t=t: e.tensor_scalar(s.xn[:, t, :], x[:, t, :], s.mv[:, t, 0:1],
                                                         s.rstd[:, t:t + 1], ALU.subtract, ALU.mult),
                       rs, *s.xn_free)
            done.append(xn)
        M = take()
        for t in range(T):
            tr = s.pe(lambda e, r, t=t: e.transpose(M.ap[:, t * P:(t + 1) * P], s.xn[:, t, :], ident[:]),
                      done[t], *M.free)
        s.xn_free = [tr]
        if split:
            hi = s.act(lambda e, r: e.activation(s.xh[:], M.ap[:], ACT.Copy, scale=X_SCALE), tr, *xt_free)
            cp = s.dve(lambda e, r: e.scalar_tensor_tensor(s.xl[:], M.ap[:], X_SCALE, s.xh[:], ALU.mult,
                                                           ALU.subtract), hi, *xt_free)
        else:
            cp = s.act(lambda e, r: e.copy(s.xt[:], M.ap[:]), tr, *xt_free)
        M.free = [cp]
        s.step()
        return cp, tr

    s.xn_free = s.last("tensor")
    s.xt_free = s.last("tensor")
    s.xh_free = s.last("tensor")

    def logits(M, weight, xt_ready):
        for t in range(T):
            op = s.pe(lambda e, r, t=t: e.matmul(M.ap[:, t * E:(t + 1) * E], s.xt[:, t * P:(t + 1) * P],
                                                 weight[:], start=True, stop=True), xt_ready, *M.free)
        return op

    def first_best(src, src_ready, mx, rank, best, onehot):
        w8 = c["w8"][:].unsqueeze(1).broadcast_to([P, T, E])
        k = s.small
        o = s.dve(lambda e, r: e.tensor_reduce(s.red[mx][:], src, AX.X, ALU.max), src_ready)
        o = s.dve(lambda e, r: e.tensor_tensor(k["ge"][:], src, bc(s.red[mx][:].unsqueeze(2), [P, T, E]),
                                               ALU.is_ge), o)
        o = s.dve(lambda e, r: e.tensor_tensor(k["ge"][:], k["ge"][:], w8, ALU.mult), o)
        o = s.dve(lambda e, r: e.tensor_reduce(s.red[rank][:], k["ge"][:], AX.X, ALU.max), o)
        o = s.dve(lambda e, r: e.tensor_tensor(onehot, w8, bc(s.red[rank][:].unsqueeze(2), [P, T, E]),
                                               ALU.is_equal), o)
        return o

    def bf16_parts(src, src_ready, parts, free):
        k = s.small
        o = s.dve(lambda e, r: e.tensor_copy(parts[:, :, 0, :], src), src_ready, *free)
        o = s.dve(lambda e, r: e.tensor_tensor(k["r1_"][:], src, parts[:, :, 0, :], ALU.subtract), o)
        o = s.dve(lambda e, r: e.tensor_copy(parts[:, :, 1, :], k["r1_"][:]), o)
        o = s.dve(lambda e, r: e.tensor_tensor(k["r2_"][:], k["r1_"][:], parts[:, :, 1, :], ALU.subtract), o)
        return s.dve(lambda e, r: e.tensor_copy(parts[:, :, 2, :], k["r2_"][:]), o)

    def ffn0(x, x_ready, x_out, x_out_free):
        xt_ready, _ = norm(x, x_ready, 1.0, EPS, s.xh_free, split=True)
        k, red = s.small, s.red
        ML = take()
        for t in range(T):
            sl = slice(t * P, (t + 1) * P)
            for n, (xp, gp) in enumerate(((s.xh, w["g_hi"]), (s.xl, w["g_hi"]), (s.xh, w["g_lo"]))):
                lg = s.pe(lambda e, r, t=t, sl=sl, n=n, xp=xp, gp=gp: e.matmul(
                    ML.ap[:, t * E:(t + 1) * E], xp[:, sl], gp[:], start=(n == 0), stop=(n == 2)),
                    xt_ready, *ML.free)
        def mv():
            return ML.ap[:, 0:T * E].rearrange("p (t e) -> p t e", e=E)
        o = s.dve(lambda e, r: e.tensor_reduce(red["mx"][:], mv(), AX.X, ALU.max), lg)
        o = s.dve(lambda e, r: e.tensor_tensor(k["lg"][:], mv(), bc(red["mx"][:].unsqueeze(2), [P, T, E]),
                                               ALU.subtract), o)
        ML.free = [o]
        o = s.act(lambda e, r: e.activation(k["ex"][:], k["lg"][:], ACT.Exp,
                                            scale=w["w_back"][:, NM - 1:NM]), o)
        s.step()
        so_far, s.steps = s.steps, [[]]
        o = s.dve(lambda e, r: e.tensor_reduce(red["sm"][:], k["ex"][:], AX.X, ALU.add), o)
        o = s.dve(lambda e, r: e.reciprocal(red["rc"][:], red["sm"][:]), o)
        sc = s.dve(lambda e, r: e.tensor_tensor(k["sc"][:], k["ex"][:],
                                                bc(red["rc"][:].unsqueeze(2), [P, T, E]), ALU.mult), o)
        o = s.dve(lambda e, r: e.tensor_tensor(k["bi"][:], k["sc"][:],
                                               c["gate_b"][:].unsqueeze(1).broadcast_to([P, T, E]),
                                               ALU.add), sc)
        o = first_best(k["bi"][:], o, "m1", "i1", None, k["oh1"][:])
        o = s.dve(lambda e, r: e.scalar_tensor_tensor(k["b2_"][:], k["oh1"][:], -3.0e38, k["bi"][:],
                                                      ALU.mult, ALU.add), o)
        o = first_best(k["b2_"][:], o, "m2", "i2", None, k["oh2"][:])
        o = s.dve(lambda e, r: e.tensor_tensor(k["oh"][:], k["oh1"][:], k["oh2"][:], ALU.add), o)
        cw = s.dve(lambda e, r: e.tensor_tensor(s.cw9[:, :, 0:E], k["sc"][:], k["oh"][:], ALU.mult), o,
                   *s.cw_free)
        parts = bf16_parts(s.cw9[:, :, 0:E], cw, s.cw3, s.cw_free)
        s.step()
        MC = take()
        for t in range(T):
            o = s.pe(lambda e, r, t=t: e.transpose(MC.ap[0:NE, t * P:(t + 1) * P], s.cw9[:, t, :], ident[:]),
                     cw, *MC.free)
        cwt = s.act(lambda e, r: e.copy(s.cwt[:], MC.ap[0:NE, :]), o, *s.cwt_free)
        MC.free = [cwt]
        M2 = take()
        for t in range(T):
            o = s.pe(lambda e, r, t=t: e.transpose(M2.ap[:].bitcast(BF16)[0:3 * E, t * P:(t + 1) * P],
                                                   s.cw3[:, t, :, :].rearrange("p k e -> p (k e)"),
                                                   ident_b[:]), parts, *M2.free)
        s.cw_free = [o]
        cwt3 = s.act(lambda e, r: e.copy(s.cwt3[:], M2.ap[:].bitcast(BF16)[0:3 * E, 0:N]), o, *s.cwt_free)
        M2.free = [cwt3]
        s.between = [op for step in s.steps for op in step]
        s.steps = so_far
        yfirst = [True]
        experts = [E] + list(range(E))

        def project(B, e_, part):
            m = 4 * experts[e_] + part
            wh, wl = w["w_hi"][:, m, :], w["w_lo"][:, m, :]
            for n, (wp, xp) in enumerate(((wh, s.xh), (wh, s.xl), (wl, s.xh))):
                o = s.pe(lambda e, r, n=n, wp=wp, xp=xp: e.matmul(B.ap[:], wp, xp[:], start=(n == 0),
                                                                  stop=(n == 2)), xt_ready, *B.free)
            return o

        def half(e_, part, t_buf, h_buf, tfree, hfree):
            B3, B1 = take(), take()
            m3 = project(B3, e_, 2 * part)
            m1 = project(B1, e_, 2 * part + 1)
            t = s.act(lambda e, r: e.activation(t_buf[:], B3.ap[:], ACT.Identity,
                                                scale=w["sc31"][:, experts[e_], part:part + 1],
                                                bias=w["b3s"][:, experts[e_], part:part + 1]), m3, *tfree)
            B3.free = [t]
            h = s.dve(lambda e, r: e.scalar_tensor_tensor(h_buf[:], B1.ap[:], w["b1s"][:, experts[e_], part:part + 1],
                                                          t_buf[:], ALU.add, ALU.mult), m1, t, *hfree)
            B1.free = [h]
            return m1, h

        def down(e_, a_buf, ready):
            for t in range(T):
                first = yfirst[0]
                yfirst[0] = False
                o = s.pe(lambda e, r, t=t, first=first: e.matmul(
                    Y.ap[:, t * D:(t + 1) * D], a_buf[:, t * P:(t + 1) * P], c["w2"][:, experts[e_], :],
                    start=first, stop=False, skip_group_check=True), ready, *Y.free)
            return o

        live = {}

        def gate_half(e_):
            i = e_ % 2
            hg, gs = s.ffn["hg"][i], s.ffn["gs"][i]
            live[e_] = u = {}
            u["m"], h = half(e_, 0, s.ffn["tg"][i], hg, s.use["tg", i], s.use["hg", i])
            s.use["tg", i] = [h]
            return u, h, hg, gs, i

        def hold(u, h, hg, gs, i):
            u["g"] = s.dve(lambda e, r: e.tensor_scalar(hg[:], hg[:], LIMIT, None, ALU.min), h)

        def gate_act(u, h, hg, gs, i):
            g = u["g"]
            u["ga"] = s.act(lambda e, r: e.activation(gs[:], hg[:], ACT.Gelu_apprx_sigmoid), g,
                            *s.use["gs", i])
            s.use["hg", i] = [u["ga"]]

        def linear_half(e_):
            i = e_ % 2
            u = live[e_]
            u["m"], u["h"] = half(e_, 1, s.ffn["tl"][i], s.ffn["hl"][i], s.use["tl", i], s.use["hl", i])
            s.use["tl", i] = [u["h"]]

        def clip(e_):
            u, hl = live[e_], s.ffn["hl"][e_ % 2]
            u["l"] = s.dve(lambda e, r: e.tensor_scalar(hl[:], hl[:], LIMIT, -LIMIT, ALU.min, ALU.max),
                           u["h"])

        def combine(e_):
            i = e_ % 2
            u, hl, gs, am = live[e_], s.ffn["hl"][i], s.ffn["gs"][i], s.ffn["am"][i]
            u["a"] = s.dve(lambda e, r: e.scalar_tensor_tensor(am[:], hl[:], 1.0, gs[:], ALU.add, ALU.mult),
                           u["l"], u["ga"], *s.use["am", i])
            s.use["hl", i] = [u["a"]]
            s.use["gs", i] = [u["a"]]

        def spread(e_):
            i, C = e_ % 2, take()
            cb = s.pe(lambda e, r: e.matmul(C.ap[:], c["sel"][:, experts[e_], :], s.cwt3[:], start=True,
                                            stop=True), cwt3, *C.free)
            live[e_]["cb"] = s.act(lambda e, r: e.copy(s.cwb[i][:], C.ap[:]), cb, *s.use["cwb", i])
            C.free = [live[e_]["cb"]]

        def weigh(e_):
            i = e_ % 2
            u, am = live[e_], s.ffn["am"][i]
            u["a"] = s.dve(lambda e, r: e.tensor_tensor(am[:], am[:], s.cwb[i][:], ALU.mult), u["a"], u["cb"])
            s.use["cwb", i] = [u["a"]]

        for e_ in range(NE + 2):
            one, two = e_ - 1, e_ - 2
            if e_ < NE:
                g = gate_half(e_)
            if 0 <= one < NE:
                clip(one)
            if e_ < NE:
                hold(*g)
            if 0 <= one < NE:
                combine(one)
            if 1 <= one < NE:
                assert not s.between
                spread(one)
            if 0 <= two:
                o = down(two, s.ffn["am"][two % 2], live[two]["a"])
                s.use["am", two % 2] = [o]
            s.step()
            if e_ < NE:
                linear_half(e_)
                gate_act(*g)
            if 1 <= one < NE:
                weigh(one)
            s.step()
        s.xh_free = [live[NE - 1]["m"]]
        for t in range(T):
            o = s.pe(lambda e, r, t=t: e.matmul(Y.ap[:, t * D:(t + 1) * D], s.cwt[:, t * P:(t + 1) * P],
                                                c["b2s"][:], start=False, stop=(t == T - 1),
                                                skip_group_check=True), cwt)
        s.cwt_free = [o]
        res = s.dve(lambda e, r: e.scalar_tensor_tensor(flat(x_out), Y.ap[:], 0.5, flat(x),
                                                        ALU.mult, ALU.add), o, *x_out_free)
        Y.free = [res]
        s.step()
        return res

    s.use = {(n, i): s.last("vector", "scalar", "tensor") for n in ("tg", "tl", "hg", "hl", "gs", "am", "cwb")
             for i in range(2)}
    s.cw_free = s.last("tensor")
    s.cwt_free = s.last("tensor")

    def attn0(x, x_ready, x_out, x_out_free):
        xt_ready, tr = norm(x, x_ready, 1.0, EPS, s.xt_free)
        xb = s.pool(lambda e, r: e.tensor_tensor(s.x_bias[:], x[:], c["a0_ob"][:].unsqueeze(1)
                                                 .broadcast_to([P, T, D]), ALU.add), x_ready, tr)
        MQ = take()
        q = s.pe(lambda e, r: e.matmul(MQ.ap[:], c["a0_wq"][:], s.xt[:], start=True, stop=True), xt_ready,
                 *MQ.free)
        qs = s.act(lambda e, r: e.activation(s.qt[:], MQ.ap[:], ACT.Identity, bias=c["a0_bq"][:]), q,
                   *s.last("tensor"))
        MQ.free = [qs]
        kvs = []
        for b in range(NB):
            B = take()
            for j in range(BATCH_TILES):
                t = b * BATCH_TILES + j
                o = s.pe(lambda e, r, t=t, j=j, B=B: e.matmul(B.ap[:, j * 2 * D:(j + 1) * 2 * D],
                                                              s.xt[:, t * P:(t + 1) * P], c["a0_wkv"][:],
                                                              start=True, stop=True), *B.free)
            bias = c["a0_bkv"][:].unsqueeze(1).broadcast_to([P, BATCH_TILES, 2 * D])
            kv = s.dve(lambda e, r, b=b, B=B, bias=bias: e.tensor_tensor(
                s.kv[:, b * BATCH_TILES:(b + 1) * BATCH_TILES, :],
                B.ap[:].rearrange("p (j n) -> p j n", j=BATCH_TILES), bias, ALU.add), o, *s.last("tensor"))
            B.free = [kv]
            kvs.append(kv)
        s.xt_free = [o]
        s.step()
        for b in range(NB):
            for j in range(BATCH_TILES):
                t = b * BATCH_TILES + j
                o = s.pe(lambda e, r, t=t, b=b, j=j: e.matmul(
                    Y.ap[:, b * D:(b + 1) * D], s.kv[:, t, 0:D], s.kv[:, t, D:2 * D], start=(j == 0),
                    stop=(j == BATCH_TILES - 1)), kvs[b], *Y.free)
        km = s.dve(lambda e, r: e.tensor_tensor(s.kvm[:], Y.ap[:, 0:NB * D].rearrange("p (b d) -> p b d", b=NB),
                                                c["blk4"][:].unsqueeze(1).broadcast_to([P, NB, D]),
                                                ALU.mult), o)
        Y.free = [km]
        MX = take()
        for b in range(NB):
            o = s.pe(lambda e, r, b=b: e.matmul(MX.ap[:, b * 256:(b + 1) * 256], s.kvm[:, b, :],
                                                s.qt[:, b * 256:(b + 1) * 256], start=True, stop=True),
                     km, qs, *MX.free)
        ctx_ready = o
        s.step()
        g = s.gn
        for b in range(NB):
            o = s.dve(lambda e, r, b=b: e.bn_stats(s.gst[:, b, :], MX.ap[:, b * 256:(b + 1) * 256]), ctx_ready)
        st = o
        for b in range(NB):
            o = s.dve(lambda e, r, b=b: e.bn_aggr(s.gmv[:, b, :], s.gst[:, b, :]), st)
            o.fenced = True
        gm = s.pe(lambda e, r: e.matmul(Y.ap[:, 0:NB], c["avg4"][:], s.gmv[:, :, 0], start=True, stop=True),
                  o, *Y.free)
        mean = s.dve(lambda e, r: e.tensor_copy(g["mean"][:], Y.ap[:, 0:NB]), gm)
        Y.free = [mean]
        o = s.dve(lambda e, r: e.tensor_tensor(g["dev"][:], s.gmv[:, :, 0], g["mean"][:], ALU.subtract), mean)
        o = s.dve(lambda e, r: e.tensor_tensor(g["dev"][:], g["dev"][:], g["dev"][:], ALU.mult), o)
        o = s.dve(lambda e, r: e.tensor_tensor(g["vv"][:], g["dev"][:], s.gmv[:, :, 1], ALU.add), o)
        gv = s.pe(lambda e, r: e.matmul(Y.ap[:, 0:NB], c["avg4"][:], g["vv"][:], start=True, stop=True),
                  o, *Y.free)
        o = s.dve(lambda e, r: e.tensor_scalar(g["ve"][:], Y.ap[:, 0:NB], EPS, None, ALU.add), gv)
        Y.free = [o]
        o = s.pool(lambda e, r: e.tensor_tensor(g["r"][:], g["ve"][:], w["half_neg"][:, 0:NB], ALU.pow), o)
        s.step()
        sc = s.dve(lambda e, r: e.tensor_scalar(g["sc"][:], g["r"][:], c["a0_gnw"][:], None, ALU.mult), o)
        o = s.dve(lambda e, r: e.tensor_tensor(g["t"][:], g["mean"][:], g["sc"][:], ALU.mult), sc)
        o = s.dve(lambda e, r: e.tensor_scalar(g["bi"][:], g["t"][:], -1.0, c["a0_gnb"][:], ALU.mult,
                                               ALU.add), o)
        for b in range(NB):
            cn = s.act(lambda e, r, b=b: e.activation(s.ctxn[:, b * 256:(b + 1) * 256],
                                                      MX.ap[:, b * 256:(b + 1) * 256], ACT.Identity,
                                                      bias=g["bi"][:, b:b + 1], scale=g["sc"][:, b:b + 1]),
                       o, *s.last("tensor"))
        MX.free = [cn]
        H0 = take()
        for t in range(T):
            o = s.pe(lambda e, r, t=t: e.matmul(H0.ap[:, t * D:(t + 1) * D], s.ctxn[:, t * P:(t + 1) * P],
                                                c["a0_wo"][:], start=True, stop=True), cn, *H0.free)
        res = s.dve(lambda e, r: e.tensor_tensor(flat(x_out), H0.ap[:], flat(s.x_bias), ALU.add), o, xb,
                    *x_out_free)
        H0.free = [res]
        s.step()
        return res

    def ffn1(x, x_ready, x_out, x_out_free):
        xt_ready, _ = norm(x, x_ready, 1.0 + EPS, EPS * EPS, s.xt_free)
        ML = take()
        lg = logits(ML, c["f1_gate"], xt_ready)
        k = s.small
        cp = s.dve(lambda e, r: e.tensor_copy(k["lg"][:], ML.ap[:, 0:T * E].rearrange("p (t e) -> p t e", e=E)),
                   lg)
        ML.free = [cp]
        mk = first_best(k["lg"][:], cp, "m1", "i1", None, s.mask[:])
        hs = []
        for j in range(2):
            B = take()
            m = s.pe(lambda e, r, j=j, B=B: e.matmul(B.ap[:], w["f1_w1s"][:, j * P:(j + 1) * P], s.xt[:],
                                                     start=True, stop=True), xt_ready, *B.free)
            ga = s.act(lambda e, r, j=j, B=B: e.activation(s.ffn["gs"][j][:], B.ap[:], ACT.Gelu,
                                                           bias=w["f1_b1s"][:, j:j + 1]), m,
                       *s.use["gs", j])
            B.free = [ga]
            hs.append(ga)
        s.xt_free = [m]
        s.step()
        MT = take()
        for t in range(T):
            o = s.pe(lambda e, r, t=t: e.transpose(MT.ap[:].bitcast(BF16)[0:E, t * P:(t + 1) * P], s.mask[:, t, :], ident_b[:]),
                     mk, *MT.free)
        mt = s.act(lambda e, r: e.copy(s.maskt[:], MT.ap[:].bitcast(BF16)[0:E, 0:N]), o, *s.maskt_free)
        MT.free = [mt]
        s.step()
        gm = []
        for j in range(2):
            M = take()
            o = s.pe(lambda e, r, j=j, M=M: e.matmul(M.ap[:], c["sel1"][:, j, :], s.maskt[:], start=True,
                                                     stop=True), mt, *M.free)
            o = s.dve(lambda e, r, j=j, M=M: e.tensor_tensor(s.ffn["am"][j][:], s.ffn["gs"][j][:], M.ap[:],
                                                             ALU.mult), o, hs[j], *s.use["am", j])
            M.free = [o]
            s.use["gs", j] = [o]
            gm.append(o)
        s.step()
        first = True
        for t in range(T):
            for j in range(2):
                o = s.pe(lambda e, r, t=t, j=j, first=first: e.matmul(
                    Y.ap[:, t * D:(t + 1) * D], s.ffn["am"][j][:, t * P:(t + 1) * P], c["f1_w2"][:, j, :],
                    start=first, stop=False, skip_group_check=True), gm[j], *Y.free)
                first = False
            for j in range(3):
                o = s.pe(lambda e, r, t=t, j=j: e.matmul(
                    Y.ap[:, t * D:(t + 1) * D], s.maskt[:, t * P:(t + 1) * P], w["f1_b2p"][:, j, :],
                    start=False, stop=(t == T - 1 and j == 2), skip_group_check=True), mt)
        s.use["am", 0] = [o]
        s.use["am", 1] = [o]
        s.maskt_free = [o]
        res = s.dve(lambda e, r: e.scalar_tensor_tensor(flat(x_out), Y.ap[:], 0.5, flat(x), ALU.mult,
                                                        ALU.add), o, *x_out_free)
        Y.free = [res]
        s.step()
        return res

    s.maskt_free = s.last("tensor")

    def attn1(x, x_ready):
        xt_ready, tr = norm(x, x_ready, 1.0 + RMS_EPS, EPS * RMS_EPS, s.xt_free)
        G = 3 * NH1
        xb = s.pool(lambda e, r: e.tensor_tensor(s.x_bias[:], x[:], c["a1_ob"][:].unsqueeze(1)
                                                 .broadcast_to([P, T, D]), ALU.add), x_ready, tr)
        B = take()
        for t in range(T):
            o = s.pe(lambda e, r, t=t, B=B: e.matmul(B.ap[:, t * G:(t + 1) * G], s.xt[:, t * P:(t + 1) * P],
                                                     w["a1_wg"][:], start=True, stop=True), xt_ready, *B.free)
        z = s.dve(lambda e, r, B=B: e.tensor_tensor(
            s.z[:], B.ap[:, 0:T * G].rearrange("p (t g) -> p t g", t=T),
            c["a1_bg"][:].unsqueeze(1).broadcast_to([P, T, G]), ALU.add), o)
        B.free = [z]
        o = s.dve(lambda e, r: e.tensor_scalar(s.zc[:], s.z[:], Z_LEAST, None, ALU.max), z)
        o = s.act(lambda e, r: e.activation(s.ez[:], s.zc[:], ACT.Exp, scale=-1.0), o)
        e1 = s.dve(lambda e, r: e.tensor_scalar(s.e1[:], s.ez[:], 1.0, None, ALU.add), o)
        lnf = s.act(lambda e, r: e.activation(s.lnf[:], s.e1[:, :, 0:NH1], ACT.Ln), e1)
        gio = s.dve(lambda e, r: e.reciprocal(s.gio[:], s.e1[:, :, NH1:G]), e1)
        s.step()
        for t in range(T):
            B = take()
            o = s.pe(lambda e, r, t=t, B=B: e.matmul(B.ap[:, 0:3 * D], s.xt[:, t * P:(t + 1) * P],
                                                     w["a1_wqkv"][:], start=True, stop=True), xt_ready, *B.free)
            qk = s.act(lambda e, r, t=t, B=B: e.copy(s.qk[:, t, :], B.ap[:, 0:2 * D]), o, *s.last("vector"))
            v = s.act(lambda e, r, t=t, B=B: e.copy(s.v[:, t, :], B.ap[:, 2 * D:3 * D]), *s.last("tensor"))
            B.free = [v]
        s.xt_free = [o]
        for par in range(2):
            def view(tl, par=par):
                return tl[:].rearrange("p t (g h d) -> p t g h d", h=2, d=DH1)[:, :, :, par, :]
            vps = s.act(lambda e, r, par=par, view=view: e.copy(view(s.vpar[par]), view(s.v)), v,
                        *s.last("tensor"))
        s.step()
        NHH = 2 * NH1
        hd = DH1 // 2

        def heads(tl):
            return tl[:].rearrange("p t (h d) -> p t h d", h=NHH)

        cosb = c["cos"][:].unsqueeze(2).broadcast_to([P, T, NHH, DH1])
        o1 = s.dve(lambda e, r: e.tensor_tensor(heads(s.rc), heads(s.qk), cosb, ALU.mult), qk)
        for hh in range(2):
            sinb = c["sin"][:, :, hh * hd:(hh + 1) * hd].unsqueeze(2).broadcast_to([P, T, NHH, hd])
            o2 = s.dve(lambda e, r, hh=hh, sinb=sinb: e.tensor_tensor(
                heads(s.rs)[:, :, :, hh * hd:(hh + 1) * hd],
                heads(s.qk)[:, :, :, (1 - hh) * hd:(2 - hh) * hd], sinb, ALU.mult), qk)
        ks = s.dve(lambda e, r: e.tensor_tensor(s.rc[:], s.rc[:], s.rs[:], ALU.add), o2)
        qps = []
        for par in range(2):
            def view(tl, par=par):
                return tl[:, :, 0:D].rearrange("p t (g h d) -> p t g h d", h=2, d=DH1)[:, :, :, par, :]
            og = s.gio[:, :, NH1:2 * NH1].rearrange("p t (g h) -> p t g h", h=2)[:, :, :, par]
            qps.append(s.dve(lambda e, r, par=par, view=view, og=og: e.tensor_tensor(
                view(s.qpar[par]), view(s.rc), og.unsqueeze(3).broadcast_to([P, T, NH1 // 2, DH1]),
                ALU.mult), ks, gio, *s.last("tensor")))
        s.step()
        B = take()
        NL = T * NH1
        o = s.pe(lambda e, r, B=B: e.matmul(B.ap[:, 0:NL], c["tri"][:], s.lnf[:].rearrange("p t h -> p (t h)"),
                                            start=True, stop=True), lnf, *B.free)
        o = s.pe(lambda e, r, B=B: e.matmul(B.ap[:, NL:2 * NL], c["ones"][:],
                                            s.lnf[:].rearrange("p t h -> p (t h)"), start=True, stop=True))
        lc = s.dve(lambda e, r, B=B: e.tensor_copy(s.lc[:].rearrange("p t h -> p (t h)"), B.ap[:, 0:NL]), o)
        lr = s.dve(lambda e, r, B=B: e.tensor_tensor(s.lrest[:].rearrange("p t h -> p (t h)"),
                                                     B.ap[:, NL:2 * NL],
                                                     s.lc[:].rearrange("p t h -> p (t h)"),
                                                     ALU.subtract), lc)
        B.free = [lr]
        ec = s.act(lambda e, r: e.activation(s.ec[:], s.lc[:], ACT.Exp, scale=-1.0), lc)
        es = s.act(lambda e, r: e.activation(s.es[:], s.lrest[:], ACT.Exp, scale=-1.0), lr)
        parts = bf16_parts(s.lc[:], lc, s.lc3, s.last("tensor"))
        def hv(ap):
            return ap.rearrange("p t (h d) -> p t h d", h=NH1)
        kg = s.dve(lambda e, r: e.tensor_tensor(hv(s.kg[:]), hv(s.rc[:, :, D:2 * D]),
                                                s.gio[:, :, 0:NH1].unsqueeze(3)
                                                .broadcast_to([P, T, NH1, DH1]), ALU.mult),
                   ks, gio, *s.last("tensor"))
        kgs = s.dve(lambda e, r: e.tensor_tensor(
            hv(s.kgs[:]), hv(s.kg[:, 0:T:2, :]), s.es[:, 0:T:2, :].unsqueeze(3)
            .broadcast_to([P, NB, NH1, DH1]), ALU.mult), kg, es, *s.last("tensor"))
        for par in range(2):
            def view(tl, par=par):
                return tl.rearrange("p t (g h d) -> p t g h d", h=2, d=DH1)[:, :, :, par, :]
            ecv = s.ec[:, 1:T:2, :].rearrange("p t (g h) -> p t g h", h=2)[:, :, :, par]
            qd = s.dve(lambda e, r, par=par, view=view, ecv=ecv: e.tensor_tensor(
                view(s.qd[:]), view(s.qpar[par][:, 1:T:2, :]),
                ecv.unsqueeze(3).broadcast_to([P, NB, NH1 // 2, DH1]), ALU.mult), qps[1], ec,
                *s.last("tensor"))
        s.step()
        tgt = [(s.kg, s.kt, kg, T), (s.qpar[0], s.qpt[0], qps[0], T), (s.qpar[1], s.qpt[1], qps[1], T)]
        got = []
        for src, dst, ready, n in tgt:
            B = take()
            for t in range(n):
                o = s.pe(lambda e, r, t=t, src=src, B=B: e.transpose(B.ap[:, t * P:(t + 1) * P], src[:, t, :],
                                                                     ident[:]), ready, *B.free)
            cp = s.act(lambda e, r, dst=dst, B=B: e.copy(dst[:], B.ap[:]), o, *s.last("tensor"))
            B.free = [cp]
            got.append(cp)
        B = take()
        for j in range(NB):
            o = s.pe(lambda e, r, j=j, B=B: e.transpose(B.ap[:, j * P:(j + 1) * P], s.qd[:, j, :], ident[:]),
                     qd, *B.free)
        qdt = s.act(lambda e, r, B=B: e.copy(s.qdt[:].rearrange("p b n -> p (b n)"), B.ap[:, 0:NB * P]), o,
                    *s.last("tensor"))
        B.free = [qdt]
        B = take()
        for t in range(T):
            o = s.pe(lambda e, r, t=t, B=B: e.transpose(B.ap[:].bitcast(BF16)[0:3 * NH1, t * P:(t + 1) * P],
                                                          s.lc3[:, t, :, :].rearrange("p k e -> p (k e)"),
                                                          ident_b[:]), parts, *B.free)
        lct = s.act(lambda e, r, B=B: e.copy(s.lct3[:], B.ap[:].bitcast(BF16)[0:3 * NH1, 0:N]), o, *s.last("tensor"))
        B.free = [lct]
        s.step()
        B = take()
        for b in range(NB):
            o = s.pe(lambda e, r, b=b, B=B: e.matmul(B.ap[:, b * D:(b + 1) * D], s.kgs[:, b, :],
                                                     s.v[:, b * BATCH_TILES, :], start=True, stop=True),
                     kgs, v, *B.free)
        st = s.dve(lambda e, r, B=B: e.tensor_tensor(s.st[:], B.ap[:, 0:NB * D]
                                                     .rearrange("p (b d) -> p b d", b=NB),
                                                     c["blk16"][:].unsqueeze(1).broadcast_to([P, NB, D]),
                                                     ALU.mult), o, *s.last("tensor"))
        B.free = [st]
        for b in range(NB):
            t = b * BATCH_TILES + 1
            o = s.pe(lambda e, r, b=b, t=t: e.matmul(Y.ap[:, t * P:(t + 1) * P], s.st[:, b, :], s.qdt[:, b, :],
                                                     start=(b == 0), stop=False, skip_group_check=True),
                     st, qdt, *Y.free)
        s.step()
        dec_free = [s.last("tensor", "vector"), s.last("tensor", "vector")]
        att_free = [s.last("tensor"), s.last("tensor")]

        def pv(h, ready):
            for t in range(T):
                sl = slice(t * P, (t + 1) * P)
                strip = slice(32 * (h // 2), 32 * (h // 2) + 32)
                o = s.pe(lambda e, r, t=t, h=h, sl=sl, strip=strip: e.matmul(
                    Y.ap[strip, sl], s.vpar[h % 2][:, t, strip], s.att[h % 2][:, sl], start=False,
                    stop=(h == NH1 - 1 and t == T - 1), skip_group_check=True), ready, vps)
            att_free[h % 2] = [o]
            return o

        pend = None
        for h in range(NH1):
            strip, par = 32 * (h // 2), h % 2
            B = take()
            s.pe(lambda e, r, h=h, B=B: e.matmul(B.ap[:], c["sel"][:, h, :], s.lct3[:], start=True, stop=False,
                                                 skip_group_check=True), lct, *B.free)
            for t in range(T):
                s.pe(lambda e, r, h=h, t=t, B=B: e.matmul(B.ap[:, t * P:(t + 1) * P],
                                                          s.lct3[:, t * P:(t + 1) * P], c["nsel"][:, h, :],
                                                          start=False, stop=False, skip_group_check=True))
            o = s.pe(lambda e, r, B=B: e.matmul(B.ap[:], ident_b[:], c["later"][:].unsqueeze(1)
                                                .broadcast_to([P, T, P]), start=False, stop=True,
                                                skip_group_check=True))
            de = s.act(lambda e, r, h=h, B=B: e.activation(s.dec[h % 2][:], B.ap[:], ACT.Exp, scale=-1.0), o,
                       *dec_free[h % 2])
            B.free = [de]
            B = take()
            for t in range(T):
                sl = slice(t * P, (t + 1) * P)
                o = s.pe(lambda e, r, sl=sl, strip=strip, par=par, B=B: e.matmul(
                    B.ap[:, sl], s.kt[strip:strip + 32, sl], s.qpt[par][strip:strip + 32, sl], start=True,
                    stop=True), *got, *B.free)
            at = s.dve(lambda e, r, h=h, B=B: e.tensor_tensor(s.att[h % 2][:], s.dec[h % 2][:], B.ap[:],
                                                              ALU.mult), o, de, *att_free[h % 2])
            B.free = [at]
            dec_free[h % 2] = [at]
            if pend:
                pv(*pend)
            pend = (h, at)
            s.step()
        o = pv(*pend)
        yt = s.act(lambda e, r: e.activation(s.yot[:], Y.ap[:], ACT.Copy, scale=float(DH1) ** -0.5), o,
                   *s.last("tensor"))
        Y.free = [yt]
        s.step()
        B = take()
        for t in range(T):
            o = s.pe(lambda e, r, t=t, B=B: e.matmul(B.ap[:, t * D:(t + 1) * D], s.yot[:, t * P:(t + 1) * P],
                                                     c["a1_wo"][:], start=True, stop=True), yt, *B.free)
        res = s.dve(lambda e, r, B=B: e.tensor_tensor(flat(s.x), B.ap[:], flat(s.x_bias), ALU.add), o, xb,
                    *s.last("vector", "gpsimd"))
        B.free = [res]
        s.step()
        return res

    if s.name == "head":
        copied = s.sp(lambda e, r: e.dma_start(s.x_in[:], x_v[r]))
        copied.fenced = True
    else:
        src = s.previous_out
        copied = s.act(lambda e, r: e.copy(flat(s.x_in), flat(src)), *s.last("vector", "gpsimd"))
    handed = [Earlier(next_copied)] if next_copied else []
    if s.name == "head":
        r_ = ffn0(s.x_in, copied, s.x, s.last("vector", "gpsimd"))
        copied.waits.append(Earlier(r_))
        end = attn0(s.x, r_, s.x_out, handed)
    elif s.name == "middle":
        r_ = ffn0(s.x_in, copied, s.x, s.last("vector", "gpsimd"))
        end = ffn1(s.x, r_, s.x_out, handed)
    else:
        r_ = attn1(s.x_in, copied)
        s.dve(lambda e, r: e.wait_ge(store_sem, r * 16 + 1)).own_semaphore = True
        end = ffn1(s.x, r_, s.x_out, [])
        s.act(lambda e, r: e.dma_start(out_v[r], s.x_out[:]).then_inc(store_sem, 16),
              end).own_semaphore = True
    return copied, end


def constants():
    k = {}
    k["ident"] = np.eye(P, dtype=np.float32)
    k["w8"] = np.tile(np.arange(E, 0, -1, dtype=np.float32), (P, 1))
    sel = np.zeros((3 * E, E, P), np.float32)
    for e in range(E):
        sel[[e, E + e, 2 * E + e], e, :] = 1
    k["sel"] = sel
    sel1 = np.zeros((E, 2, P), np.float32)
    for e in range(E):
        sel1[e, e // 4, (e % 4) * 32:(e % 4) * 32 + 32] = 1
    k["sel1"] = sel1
    i = np.arange(P)
    k["blk4"] = (i[:, None] // 4 == i[None] // 4).astype(np.float32)
    k["avg4"] = k["blk4"] * np.float32(0.25)
    k["blk16"] = (i[:, None] // 16 == i[None] // 16).astype(np.float32)
    k["tri"] = (i[:, None] <= i[None]).astype(np.float32)
    k["ones"] = np.ones((P, P), np.float32)
    k["later"] = (i[:, None] > i[None]).astype(np.float32) * np.float32(30000.0)
    half = DH1 // 2
    inv = (np.float32(1.0) / np.float32(10000.0) ** (np.arange(half, dtype=np.float32) / np.float32(half)))
    pos = (np.arange(T) % BATCH_TILES)[None] * P + i[:, None]
    ang = pos[:, :, None].astype(np.float32) * inv.astype(np.float32)
    cos, sin = np.cos(ang).astype(np.float32), np.sin(ang).astype(np.float32)
    k["cos"] = np.concatenate([cos, cos], -1)
    k["sin"] = np.concatenate([-sin, sin], -1)
    return k


def kernel(**inputs):
    import concourse.bacc as _bacc
    from concourse.bass_utils import run_bass_kernel_spmd as _run

    a = {k: np.asarray(v) for k, v in inputs.items()}
    f0, f1, a0, a1 = "L0_ffn_", "L1_ffn_", "L0_attn_", "L1_attn_"
    x = a[a0 + "x"]

    def rows(v):
        return np.tile(v[None], (P, 1))

    def w13(w, sw):
        v = np.concatenate([w, sw[None]], 0).reshape(NE, F, 2, D)
        return v.transpose(3, 0, 2, 1)

    def b13(b, sb_):
        return np.concatenate([b, sb_[None]], 0).reshape(NE, F, 2).transpose(1, 0, 2)

    lay = {}
    w1v, w3v = w13(a[f0 + "w1"], a[f0 + "sw1"]), w13(a[f0 + "w3"], a[f0 + "sw3"])
    lay["w13"] = np.stack([w3v[:, :, 0], w1v[:, :, 0], w3v[:, :, 1], w1v[:, :, 1]], 2)
    b1v, b3v = b13(a[f0 + "b1"], a[f0 + "sb1"]), b13(a[f0 + "b3"], a[f0 + "sb3"])
    lay["b13"] = np.stack([b3v[:, :, 0], b1v[:, :, 0], b3v[:, :, 1], b1v[:, :, 1]], 2)
    lay["w2"] = np.concatenate([a[f0 + "w2"], a[f0 + "sw2"][None]], 0).transpose(2, 0, 1)
    lay["b2s"] = np.concatenate([a[f0 + "b2"], a[f0 + "sb2"][None]], 0)
    lay["gate"] = a[f0 + "gate_w"].T
    lay["gate_b"] = rows(a[f0 + "gate_b"])
    wqkv, bqkv = a[a0 + "Wqkv_w"], a[a0 + "Wqkv_b"]
    lay["a0_wq"] = wqkv[0:D].T
    lay["a0_wkv"] = wqkv[D:].T
    lay["a0_bq"] = bqkv[0:D, None]
    lay["a0_bkv"] = rows(bqkv[D:])
    lay["a0_gnw"] = a[a0 + "gn_w"][:, None]
    lay["a0_gnb"] = a[a0 + "gn_b"][:, None]
    lay["a0_wo"] = a[a0 + "out_w"].T
    lay["a0_ob"] = rows(a[a0 + "out_b"])
    lay["f1_gate"] = a[f1 + "Wg"].T
    lay["f1_lns"] = a[f1 + "ln_scale"].T
    lay["f1_lnb"] = a[f1 + "ln_bias"].T
    lay["f1_w1"] = a[f1 + "W1"].transpose(1, 0, 2).reshape(D, E * 32)
    lay["f1_b1"] = a[f1 + "b1"].reshape(2, P).T
    lay["f1_w2"] = a[f1 + "W2"].reshape(2, P, D).transpose(1, 0, 2)
    lay["f1_b2"] = a[f1 + "b2"]
    lay["a1_nw"] = a[a1 + "norm_w"][:, None]
    lay["a1_wqkv"] = np.concatenate([a[a1 + "Wq"], a[a1 + "Wk"], a[a1 + "Wv"]], 0).T
    lay["a1_wg"] = np.concatenate([a[a1 + "Wbeta"], a[a1 + "Wig"], a[a1 + "Wog"]], 0).T
    lay["a1_bg"] = rows(np.concatenate([a[a1 + "bbeta"], a[a1 + "big"], a[a1 + "bog"]], 0))
    lay["a1_wo"] = a[a1 + "Wout"].T
    lay["a1_ob"] = rows(a[a1 + "bout"])
    lay.update(constants())
    lay["later_gate"] = np.concatenate([lay.pop("later"), lay.pop("gate")], 1)
    alone = ("w13", "sel", "sel1", "later_gate", "b2s", "f1_b2")
    packed = [(k, v.shape) for k, v in lay.items() if k not in alone]
    lay["packed"] = np.concatenate([lay.pop(k).reshape(P, -1) for k, _ in packed], 1)
    lay = {k: np.ascontiguousarray(v) for k, v in lay.items()}

    nc = _bacc.Bacc("TRN2", target_bir_lowering=False, num_devices=1)
    arrays = {"in_" + k: v for k, v in lay.items()}
    dram = {k: nc.dram_tensor("in_" + k, v.shape, mybir.dt.from_np(v.dtype), kind="ExternalInput").ap()
            for k, v in lay.items()}
    arrays["x_dram"] = np.ascontiguousarray(x.reshape(-1, D))
    x_in = nc.dram_tensor("x_dram", arrays["x_dram"].shape, F32, kind="ExternalInput").ap()
    out = nc.dram_tensor("out_dram", arrays["x_dram"].shape, F32, kind="ExternalOutput").ap()
    build(nc, dram, packed, x_in, out)
    r = _run(nc, [arrays], core_ids=[0])
    return r.results[0]["out_dram"].reshape(x.shape)
```
